# Optimizing a Trainium2 kernel written in Bass

```python
import numpy as np
import jax
import jax.numpy as jnp

def _softmax(x, axis=-1):
    return jax.nn.softmax(x, axis=axis)

def _gelu(x):
    return jax.nn.gelu(x, approximate=True)

def _silu(x):
    return jax.nn.silu(x)

def _sigmoid(x):
    return jax.nn.sigmoid(x)

def _layernorm(x, axis=-1, eps=1e-05):
    m = jnp.mean(x, axis=axis, keepdims=True)
    v = jnp.var(x, axis=axis, keepdims=True)
    return (x - m) / jnp.sqrt(v + eps)

def _scatter_add(tgt, idx, src, axis=0):
    return tgt.at[idx].add(src)

def _segment_sum(src, seg, n):
    return jax.ops.segment_sum(src, seg, n)
kernel_name = 'mk_sandwich_d2_jaxref_r8_deec10'

def setup_inputs(seed: int=0):
    np.random.seed(seed)
    _w = jnp.asarray

    def _L0_attn_setup():
        import jax, jax.numpy as jnp
        import numpy as np
        D_MODEL, D_STATE, HEAD_DIM, EXPAND, K, N_GROUPS = (128, 128, 64, 2, 4, 1)
        D_INNER = EXPAND * D_MODEL
        N_HEADS = D_INNER // HEAD_DIM
        D_PROJ = 2 * D_INNER + 2 * N_GROUPS * D_STATE + N_HEADS
        EPS = 1e-06

        def _silu(v):
            return v * jax.nn.sigmoid(v)
        key = jax.random.key(seed)
        ks = jax.random.split(key, 8)
        B, L = (2, 256)
        x = jax.random.normal(ks[0], (B, L, D_MODEL), dtype=jnp.float32)
        norm_w = jnp.ones((D_MODEL,), jnp.float32)
        in_proj_w = jax.random.normal(ks[1], (D_PROJ, D_MODEL), jnp.float32) * D_MODEL ** (-0.5)
        conv_w = jax.random.normal(ks[2], (D_INNER, 1, K), jnp.float32) * K ** (-0.5)
        conv_b = jnp.zeros((D_INNER,), jnp.float32)
        A_log = jnp.log(jax.random.uniform(ks[3], (N_HEADS,)) * 15.0 + 1.0)
        D = jnp.ones((N_HEADS,), jnp.float32)
        dt_bias = jnp.log(jax.random.uniform(ks[4], (N_HEADS,)) * 0.099 + 0.001)
        out_proj_w = jax.random.normal(ks[5], (D_MODEL, D_INNER), jnp.float32) * D_INNER ** (-0.5)
        return {'x': x, 'norm_w': norm_w, 'in_proj_w': in_proj_w, 'conv_w': conv_w, 'conv_b': conv_b, 'A_log': A_log, 'D': D, 'dt_bias': dt_bias, 'out_proj_w': out_proj_w}
    _L0_attn_in = _L0_attn_setup()

    def _L0_ffn_setup():
        import jax, jax.numpy as jnp
        import numpy as np
        TOP_K = 2
        EPS = 1e-09
        key = jax.random.key(seed)
        ks = jax.random.split(key, 6)
        B, T, D, H, E = (4, 256, 128, 256, 8)
        x = jax.random.normal(ks[0], (B, T, D), dtype=jnp.float32)
        Wg = jax.random.normal(ks[1], (E, D), dtype=jnp.float32) * 0.02
        W1 = jax.random.normal(ks[2], (E, 2 * H, D), dtype=jnp.float32) * 0.02
        b1 = jax.random.normal(ks[3], (E, 2 * H), dtype=jnp.float32) * 0.02
        Wo = jax.random.normal(ks[4], (D, H), dtype=jnp.float32) * 0.02
        bo = jax.random.normal(ks[5], (D,), dtype=jnp.float32) * 0.02
        return {'x': x, 'Wg': Wg, 'W1': W1, 'b1': b1, 'Wo': Wo, 'bo': bo}
    _L0_ffn_in = _L0_ffn_setup()

    def _L1_attn_setup():
        import jax, jax.numpy as jnp
        import numpy as np
        DIM = 128
        G = 32
        QK = 128
        HID = 256
        NUM_BUCKETS = 32
        MAX_DIST = 128
        BIAS_SCALE = QK ** 0.5
        LN_EPS = 1e-05

        def t5_rel_bias(rel_table):
            pos = jnp.arange(G)
            rel = pos[None, :] - pos[:, None]
            n = jnp.maximum(-rel, 0)
            max_exact = NUM_BUCKETS // 2
            is_small = n < max_exact
            ln_ratio = np.log(MAX_DIST / max_exact)
            val_large = max_exact + (jnp.log(jnp.maximum(n, 1).astype(jnp.float32) / max_exact) / ln_ratio * (NUM_BUCKETS - max_exact)).astype(jnp.int32)
            val_large = jnp.minimum(val_large, NUM_BUCKETS - 1)
            bucket = jnp.where(is_small, n, val_large)
            return rel_table[bucket] * BIAS_SCALE
        key = jax.random.key(seed)
        ks = jax.random.split(key, 10)
        s = 0.02
        return {'x': jax.random.normal(ks[0], (4, 512, DIM), dtype=jnp.float32), 'ln_w': jnp.ones((DIM,), jnp.float32), 'ln_b': jnp.zeros((DIM,), jnp.float32), 'Wh': jax.random.normal(ks[1], (DIM, 2 * HID), jnp.float32) * s, 'bh': jnp.zeros((2 * HID,), jnp.float32), 'Wqk': jax.random.normal(ks[2], (DIM, QK), jnp.float32) * s, 'bqk': jnp.zeros((QK,), jnp.float32), 'qk_w': jax.random.normal(ks[3], (4, QK), jnp.float32) * s + 1.0, 'qk_b': jnp.zeros((4, QK), jnp.float32), 'rel_table': jax.random.normal(ks[4], (NUM_BUCKETS,), jnp.float32) * s, 'Wout': jax.random.normal(ks[5], (HID, DIM), jnp.float32) * s, 'bout': jnp.zeros((DIM,), jnp.float32)}
    _L1_attn_in = _L1_attn_setup()

    def _L1_ffn_setup():
        import jax, jax.numpy as jnp
        import numpy as np
        DIM = 128
        HIDDEN = 384
        SCALE = 1.0 / 127.0

        def _dequant(w_int, dtype):
            return w_int.astype(dtype) * jnp.asarray(SCALE, dtype)
        key = jax.random.key(seed)
        k_x, k_g, k_u, k_d = jax.random.split(key, 4)
        x = jax.random.normal(k_x, (4, 256, DIM), dtype=jnp.float32)
        w_gate = jax.random.randint(k_g, (HIDDEN, DIM), -127, 128, dtype=jnp.int32)
        w_up = jax.random.randint(k_u, (HIDDEN, DIM), -127, 128, dtype=jnp.int32)
        w_down = jax.random.randint(k_d, (DIM, HIDDEN), -127, 128, dtype=jnp.int32)
        return {'x': x, 'w_gate': w_gate, 'w_up': w_up, 'w_down': w_down}
    _L1_ffn_in = _L1_ffn_setup()
    _d = {'L0_attn_x': _L0_attn_in['x'], 'L0_attn_norm_w': _L0_attn_in['norm_w'], 'L0_attn_in_proj_w': _L0_attn_in['in_proj_w'], 'L0_attn_conv_w': _L0_attn_in['conv_w'], 'L0_attn_conv_b': _L0_attn_in['conv_b'], 'L0_attn_A_log': _L0_attn_in['A_log'], 'L0_attn_D': _L0_attn_in['D'], 'L0_attn_dt_bias': _L0_attn_in['dt_bias'], 'L0_attn_out_proj_w': _L0_attn_in['out_proj_w'], 'L0_ffn_Wg': _L0_ffn_in['Wg'], 'L0_ffn_W1': _L0_ffn_in['W1'], 'L0_ffn_b1': _L0_ffn_in['b1'], 'L0_ffn_Wo': _L0_ffn_in['Wo'], 'L0_ffn_bo': _L0_ffn_in['bo'], 'L1_attn_ln_w': _L1_attn_in['ln_w'], 'L1_attn_ln_b': _L1_attn_in['ln_b'], 'L1_attn_Wh': _L1_attn_in['Wh'], 'L1_attn_bh': _L1_attn_in['bh'], 'L1_attn_Wqk': _L1_attn_in['Wqk'], 'L1_attn_bqk': _L1_attn_in['bqk'], 'L1_attn_qk_w': _L1_attn_in['qk_w'], 'L1_attn_qk_b': _L1_attn_in['qk_b'], 'L1_attn_rel_table': _L1_attn_in['rel_table'], 'L1_attn_Wout': _L1_attn_in['Wout'], 'L1_attn_bout': _L1_attn_in['bout'], 'L1_ffn_w_gate': _L1_ffn_in['w_gate'], 'L1_ffn_w_up': _L1_ffn_in['w_up'], 'L1_ffn_w_down': _L1_ffn_in['w_down']}
    _x0 = _d['L0_attn_x']
    _d['L0_attn_x'] = jax.random.normal(jax.random.fold_in(jax.random.key(seed), 1), (8, 512, 128), dtype=_x0.dtype)
    del _x0
    return _d

def reference(L0_attn_x, L0_attn_norm_w, L0_attn_in_proj_w, L0_attn_conv_w, L0_attn_conv_b, L0_attn_A_log, L0_attn_D, L0_attn_dt_bias, L0_attn_out_proj_w, L0_ffn_Wg, L0_ffn_W1, L0_ffn_b1, L0_ffn_Wo, L0_ffn_bo, L1_attn_ln_w, L1_attn_ln_b, L1_attn_Wh, L1_attn_bh, L1_attn_Wqk, L1_attn_bqk, L1_attn_qk_w, L1_attn_qk_b, L1_attn_rel_table, L1_attn_Wout, L1_attn_bout, L1_ffn_w_gate, L1_ffn_w_up, L1_ffn_w_down):

    def _L0_attn_ref(x, norm_w, in_proj_w, conv_w, conv_b, A_log, D, dt_bias, out_proj_w):
        import jax, jax.numpy as jnp
        import numpy as np
        D_MODEL, D_STATE, HEAD_DIM, EXPAND, K, N_GROUPS = (128, 128, 64, 2, 4, 1)
        D_INNER = EXPAND * D_MODEL
        N_HEADS = D_INNER // HEAD_DIM
        D_PROJ = 2 * D_INNER + 2 * N_GROUPS * D_STATE + N_HEADS
        EPS = 1e-06

        def _silu(v):
            return v * jax.nn.sigmoid(v)
        Bsz, L, _ = x.shape
        residual = x
        xn = x * jax.lax.rsqrt(jnp.mean(x * x, axis=-1, keepdims=True) + EPS) * norm_w
        proj = xn @ in_proj_w.T
        i = 0
        z = proj[..., i:i + D_INNER]
        i += D_INNER
        x_ssm = proj[..., i:i + D_INNER]
        i += D_INNER
        bc = N_GROUPS * D_STATE
        Bm = proj[..., i:i + bc].reshape(Bsz, L, N_GROUPS, D_STATE)
        i += bc
        Cm = proj[..., i:i + bc].reshape(Bsz, L, N_GROUPS, D_STATE)
        i += bc
        dt_raw = proj[..., i:i + N_HEADS]
        xc = jnp.transpose(x_ssm, (0, 2, 1))
        xc = jax.lax.conv_general_dilated(xc, conv_w, window_strides=(1,), padding=[(K - 1, 0)], dimension_numbers=('NCH', 'OIH', 'NCH'), feature_group_count=D_INNER)
        xc = xc + conv_b[None, :, None]
        x_conv = _silu(jnp.transpose(xc, (0, 2, 1)))
        dt = jax.nn.softplus(dt_raw + dt_bias)
        dA = jnp.exp(-jnp.exp(A_log)[None, None, :] * dt)
        x_heads = x_conv.reshape(Bsz, L, N_HEADS, HEAD_DIM)
        dt_x = dt[..., None] * x_heads
        group_idx = jnp.arange(N_HEADS) // (N_HEADS // N_GROUPS)
        Bg = Bm[:, :, group_idx, :]
        Cg = Cm[:, :, group_idx, :]

        def step(h, inp):
            dA_t, dtx_t, B_t, C_t = inp
            h = h * dA_t[..., None, None] + dtx_t[..., None] * B_t[:, :, None, :]
            y_t = jnp.einsum('bhpn,bhn->bhp', h, C_t)
            return (h, y_t)
        h0 = jnp.zeros((Bsz, N_HEADS, HEAD_DIM, D_STATE), jnp.float32)
        xs = (jnp.moveaxis(dA, 1, 0).astype(jnp.float32), jnp.moveaxis(dt_x, 1, 0).astype(jnp.float32), jnp.moveaxis(Bg, 1, 0).astype(jnp.float32), jnp.moveaxis(Cg, 1, 0).astype(jnp.float32))
        _, y = jax.lax.scan(step, h0, xs)
        y = jnp.moveaxis(y, 0, 1).astype(x.dtype)
        y = y + D[None, None, :, None] * x_heads
        y = y.reshape(Bsz, L, D_INNER) * _silu(z)
        return residual + y @ out_proj_w.T

    def _L0_ffn_ref(x, Wg, W1, b1, Wo, bo):
        import jax, jax.numpy as jnp
        import numpy as np
        TOP_K = 2
        EPS = 1e-09
        E = Wg.shape[0]
        gate_logits = jnp.einsum('btd,ed->bte', x, Wg)
        gate_scores = jax.nn.softmax(gate_logits, axis=-1)
        topk_val, topk_idx = jax.lax.top_k(gate_scores, TOP_K)
        topk_val = topk_val / (topk_val.sum(axis=-1, keepdims=True) + EPS)
        comb = (jax.nn.one_hot(topk_idx, E, dtype=x.dtype) * topk_val[..., None]).sum(axis=-2)
        out = jnp.zeros_like(x)
        for e in range(E):
            h = jnp.einsum('btd,hd->bth', x, W1[e]) + b1[e]
            a, b = jnp.split(h, 2, axis=-1)
            g = a * jax.nn.sigmoid(b)
            eo = jnp.einsum('bth,dh->btd', g, Wo) + bo
            out = out + eo * comb[..., e:e + 1]
        return out

    def _L1_attn_ref(x, ln_w, ln_b, Wh, bh, Wqk, bqk, qk_w, qk_b, rel_table, Wout, bout):
        import jax, jax.numpy as jnp
        import numpy as np
        DIM = 128
        G = 32
        QK = 128
        HID = 256
        NUM_BUCKETS = 32
        MAX_DIST = 128
        BIAS_SCALE = QK ** 0.5
        LN_EPS = 1e-05

        def t5_rel_bias(rel_table):
            pos = jnp.arange(G)
            rel = pos[None, :] - pos[:, None]
            n = jnp.maximum(-rel, 0)
            max_exact = NUM_BUCKETS // 2
            is_small = n < max_exact
            ln_ratio = np.log(MAX_DIST / max_exact)
            val_large = max_exact + (jnp.log(jnp.maximum(n, 1).astype(jnp.float32) / max_exact) / ln_ratio * (NUM_BUCKETS - max_exact)).astype(jnp.int32)
            val_large = jnp.minimum(val_large, NUM_BUCKETS - 1)
            bucket = jnp.where(is_small, n, val_large)
            return rel_table[bucket] * BIAS_SCALE
        b, n, _ = x.shape
        g = G
        ng = n // g
        mu = jnp.mean(x, -1, keepdims=True)
        var = jnp.var(x, -1, keepdims=True)
        normed = (x - mu) * jax.lax.rsqrt(var + LN_EPS) * ln_w + ln_b
        hv = jax.nn.silu(normed @ Wh + bh)
        v, gate = jnp.split(hv, 2, axis=-1)
        qk = jax.nn.silu(normed @ Wqk + bqk)
        qk4 = qk[..., None, :] * qk_w + qk_b
        quad_q, lin_q, quad_k, lin_k = [qk4[..., h, :] for h in range(4)]
        grp = lambda t: t.reshape(b, ng, g, t.shape[-1])
        quad_q, quad_k, lin_q, lin_k, vg = map(grp, (quad_q, quad_k, lin_q, lin_k, v))
        sim = jnp.einsum('bgid,bgjd->bgij', quad_q, quad_k) / g
        sim = sim + t5_rel_bias(rel_table)
        attn = jnp.square(jax.nn.relu(sim))
        causal_mask = jnp.triu(jnp.ones((g, g), bool), 1)
        attn = jnp.where(causal_mask, 0.0, attn)
        quad_out = jnp.einsum('bgij,bgje->bgie', attn, vg)
        lin_kv = jnp.einsum('bgnd,bgne->bgde', lin_k, vg) / g
        lin_kv = jnp.cumsum(lin_kv, axis=1)
        lin_kv = jnp.pad(lin_kv, ((0, 0), (1, 0), (0, 0), (0, 0)))[:, :-1]
        lin_out = jnp.einsum('bgde,bgnd->bgne', lin_kv, lin_q)
        out = gate * (quad_out + lin_out).reshape(b, n, HID)
        return out @ Wout + bout + x

    def _L1_ffn_ref(x, w_gate, w_up, w_down):
        import jax, jax.numpy as jnp
        import numpy as np
        DIM = 128
        HIDDEN = 384
        SCALE = 1.0 / 127.0

        def _dequant(w_int, dtype):
            return w_int.astype(dtype) * jnp.asarray(SCALE, dtype)
        wg = _dequant(w_gate, x.dtype)
        wu = _dequant(w_up, x.dtype)
        wd = _dequant(w_down, x.dtype)
        gate = jnp.einsum('bsd,hd->bsh', x, wg)
        up = jnp.einsum('bsd,hd->bsh', x, wu)
        h = jax.nn.silu(gate) * up
        return jnp.einsum('bsh,dh->bsd', h, wd)
    x = L0_attn_x
    x = x + _layernorm(_L0_attn_ref(_layernorm(x, axis=-1), L0_attn_norm_w, L0_attn_in_proj_w, L0_attn_conv_w, L0_attn_conv_b, L0_attn_A_log, L0_attn_D, L0_attn_dt_bias, L0_attn_out_proj_w), axis=-1)
    x = x + _layernorm(_L0_ffn_ref(_layernorm(x, axis=-1), L0_ffn_Wg, L0_ffn_W1, L0_ffn_b1, L0_ffn_Wo, L0_ffn_bo), axis=-1)
    x = x + _layernorm(_L1_attn_ref(_layernorm(x, axis=-1), L1_attn_ln_w, L1_attn_ln_b, L1_attn_Wh, L1_attn_bh, L1_attn_Wqk, L1_attn_bqk, L1_attn_qk_w, L1_attn_qk_b, L1_attn_rel_table, L1_attn_Wout, L1_attn_bout), axis=-1)
    x = x + _layernorm(_L1_ffn_ref(_layernorm(x, axis=-1), L1_ffn_w_gate, L1_ffn_w_up, L1_ffn_w_down), axis=-1)
    return x

_drawn_inputs = setup_inputs


def setup_inputs(seed=0):
    import zlib

    import numpy as np

    out = dict(_drawn_inputs(seed))
    spreads = {'L0_attn_norm_w': (1.0, 0.2),
     'L0_attn_conv_b': (0.0, 0.1),
     'L0_attn_D': (1.0, 0.2),
     'L1_attn_ln_w': (1.0, 0.6),
     'L1_attn_ln_b': (0.0, 0.8),
     'L1_attn_bh': (0.0, 0.8),
     'L1_attn_bqk': (0.0, 2.0),
     'L1_attn_qk_b': (0.0, 2.0),
     'L1_attn_bout': (0.0, 0.8)}
    factors = {'L1_attn_Wh': 8.0,
     'L1_attn_Wqk': 8.0,
     'L1_attn_qk_w': 64.0,
     'L1_attn_rel_table': 64.0,
     'L1_attn_Wout': 8.0}
    for name, (base, spread) in spreads.items():
        noise = np.random.default_rng([zlib.crc32(name.encode()), seed]).standard_normal(out[name].shape)
        drawn = base * np.exp(spread * noise) if base else spread * noise
        out[name] = jnp.asarray(drawn.astype(out[name].dtype))
    for name, factor in factors.items():
        out[name] = (out[name] * factor).astype(out[name].dtype)
    return out
```

```python
import concourse.bass as bass
from concourse import mybir
from contextlib import ExitStack

ALU = mybir.AluOpType
ACT = mybir.ActivationFunctionType
AX = mybir.AxisListType
F32 = mybir.dt.float32
F32R = mybir.dt.float32r
BF16 = mybir.dt.bfloat16
I32 = mybir.dt.int32
U32 = mybir.dt.uint32

P = 128
SEQS, TOK = 8, 512
CH = TOK // P
NT = SEQS * CH
HEADS, HD = 4, 64
INNER = HEADS * HD
EXPERTS, HID = 8, 256
GROUP = 32
FFN = 384
LN_EPS, RMS_EPS, TOP_EPS = 1e-5, 1e-6, 1e-9
FAR = -1e30


GATE_STEPS = 25


def t5_buckets():
    import math
    return [n if n < 16 else min(31, 16 + int(math.log(n / 16) / math.log(8) * 16)) for n in range(GROUP)]


BUCKETS = t5_buckets()


def build(nc, x_in, norm_w, in_wT, conv_w, conv_b, A_log, D_skip, dt_bias, out_wT, WgT, W1T, b1, WoT, bo,
          ln_w, ln_b, Wh, bh, Wqk, bqk, qk_w, qk_b, rel, Wout, bout, wgT, wuT, wdT, out):
    ctx = ExitStack()
    with ctx:
        def sb(name, shape, dt=F32):
            return ctx.enter_context(nc.sbuf_tensor(name, shape, dt))

        def sem(name):
            return ctx.enter_context(nc.semaphore(name))

        X = sb("X", [P, SEQS, CH, P])
        RES = sb("RES", [P, SEQS, CH, P])
        res_mean = sb("res_mean", [P, SEQS, CH])
        res_rstd = sb("res_rstd", [P, SEQS, CH])
        ps = ctx.enter_context(nc.psum_tensor("ps", [P, 8, 512], F32))

        def bank(b):
            return ps[:, b, :]

        ident = sb("ident", [P, P])
        identb = sb("identb", [P, P], BF16)
        negavg = sb("negavg", [P, P])
        avgrow = sb("avgrow", [1, P])
        cumneg = sb("cumneg", [P, P])
        allneg = sb("allneg", [P, P])
        far4 = sb("far4", [P, HEADS, P], BF16)
        mhalf = sb("mhalf", [P, CH])
        iota8 = sb("iota8", [P, EXPERTS])
        iota8i = sb("iota8i", [P, EXPERTS], I32)
        near = sb("near", [P, P])
        before = sb("before", [P, P])

        w_in = sb("w_in", [P, 772])
        w_in_hi = sb("w_in_hi", [P, 772], F32R)
        w_in_lo = sb("w_in_lo", [P, 772], F32R)
        normw = sb("normw", [P, 1])
        convw = sb("convw", [P, 2, 4])
        convb = sb("convb", [P, 2])
        dskip = sb("dskip", [P, 2])
        alog = sb("alog", [P, HEADS])
        dtb = sb("dtb", [P, HEADS])
        w_out = sb("w_out", [P, 2, P])
        w1 = sb("w1", [P, 512])
        w1_hi = sb("w1_hi", [P, EXPERTS, 512], F32R)
        w1_lo = sb("w1_lo", [P, EXPERTS, 512], F32R)
        b1r = sb("b1r", [1, 512])
        wg = sb("wg", [P, EXPERTS])
        wg_hi = sb("wg_hi", [P, EXPERTS], F32R)
        wg_lo = sb("wg_lo", [P, EXPERTS], F32R)
        w_o = sb("w_o", [P, 2, P])
        bo_rows = sb("bo_rows", [P, P])
        w4 = sb("w4", [P, 640])
        w4s = sb("w4s", [P, 640])
        w4_hi = sb("w4_hi", [P, 640], F32R)
        w4_lo = sb("w4_lo", [P, 640], F32R)
        b4r = sb("b4r", [1, 640])
        lnw = sb("lnw", [P, 1])
        lnb = sb("lnb", [P, 1])
        lnb_avg = sb("lnb_avg", [P, P])
        qkw = sb("qkw", [P, 4])
        qkb = sb("qkb", [P, 4])
        w_att = sb("w_att", [P, 2, P])
        bout_rows = sb("bout_rows", [P, P])
        table = sb("table", [GROUP, 32])
        shifted = sb("shifted", [GROUP, 65])
        wff = sb("wff", [P, 2 * FFN])
        wff_i = wff[:].bitcast(I32)
        wff_hi = sb("wff_hi", [P, 2 * FFN], F32R)
        wff_lo = sb("wff_lo", [P, 2 * FFN], F32R)
        wdn = sb("wdn", [P, 3, P])
        wdn_i = wdn[:].bitcast(I32)

        ZT_hi = [sb(f"ZT_hi{k}", [P, TOK], F32R) for k in range(2)]
        ZT_lo = [sb(f"ZT_lo{k}", [P, TOK], F32R) for k in range(2)]
        Z = sb("Z", [P, CH, P])
        add = sb("add", [P, CH, P])
        stats_t = sb("stats_t", [P, CH, 6])
        mv = sb("mv", [P, CH, 2])
        rstd = sb("rstd", [P, CH])
        rtmp = sb("rtmp", [P, 4, CH])
        rsc = sb("rsc", [P, CH])
        shift = sb("shift", [P, CH])
        z1 = sb("z1", [P, CH, P])
        rstats_t = sb("rstats_t", [P, CH, 6])
        rmv = sb("rmv", [P, CH, 2])
        rvar = sb("rvar", [P, CH])

        scratch = nc.dram_tensor("rel_scratch", [GROUP * 65], F32, kind="Internal").ap()

        early = ExitStack()

        def sb(name, shape, dt=F32):
            return early.enter_context(nc.sbuf_tensor(name, shape, dt))

        x_mean = sb("x_mean", [P, SEQS, CH])
        x_rstd = sb("x_rstd", [P, SEQS, CH])
        XT_hi = sb("XT_hi", [P, SEQS, TOK], F32R)
        XT_lo = sb("XT_lo", [P, SEQS, TOK], F32R)
        NC = NT * HEADS
        cpartsT = sb("cpartsT", [P, 3, P], BF16)
        dt_t, ecum_t, etail_t, dec_t = (sb(n, [P, SEQS, CH, HEADS]) for n in ("dt_t", "ecum_t", "etail_t", "dec_t"))
        expA = sb("expA", [P, HEADS])
        parts = sb("parts", [P, NT, P], BF16)
        headrows = sb("headrows", [P, HEADS, P], BF16)
        headrows_neg = sb("headrows_neg", [P, HEADS, P], BF16)
        u = sb("u", [P, 2, TOK])
        th = sb("th", [P, 2, TOK])
        xc = sb("xc", [P, 2, TOK])
        Bf = sb("Bf", [P, TOK])
        Cf = sb("Cf", [P, TOK])
        gz = sb("gz", [P, 2, TOK])
        St = sb("St", [P, INNER])
        Sd = sb("Sd", [P, INNER])
        ytok = sb("ytok", [P, CH, INNER])
        sm = ytok[:].rearrange("p c (k n) -> p (c k) n", n=NC)
        credit = sb("credit", [1, 2])
        yf = sb("yf", [P, 2, TOK])

        dtx = sb("dtx", [P, 2, INNER])
        wdtx = sb("wdtx", [P, INNER])
        cparts = wdtx[:, 0:3 * NC // 2].bitcast(BF16).rearrange("p (q n) -> p q n", q=3)
        Btok = sb("Btok", [P, P])
        Edec = sb("Edec", [P, 2, HEADS, P])
        Mdec = Edec

        early.close()

        def sb(name, shape, dt=F32):
            return ctx.enter_context(nc.sbuf_tensor(name, shape, dt))

        lg = sb("lg", [P, CH, EXPERTS])
        top = sb("top", [P, CH, 8])
        topi = sb("topi", [P, CH, 8], U32)
        topf = sb("topf", [P, CH, 2])
        ge = sb("ge", [P, 4, CH, EXPERTS + 1])
        gs = sb("gs", [P, 6, CH])
        pick = sb("pick", [P, 2, CH, EXPERTS])
        comb = [sb(f"comb{k}", [P, CH, EXPERTS]) for k in range(2)]
        csum = [sb(f"csum{k}", [P, CH]) for k in range(2)]
        sig = sb("sig", [P, 4, HID])
        gb = sb("gb", [P, 2, EXPERTS, HID])
        acc = [sb(f"acc{k}", [P, HID]) for k in range(2)]
        accT = sb("accT", [P, 2, P])

        qkf = sb("qkf", [P, TOK])
        qv = sb("qv", [P, 4, TOK])
        vt = sb("vt", [P, CH, HID])
        gt = sb("gt", [P, 2, TOK])
        lkt = sb("lkt", [P, CH, P])
        at = sb("at", [P, 2, TOK])
        kvs = sb("kvs", [P, 3, HID])
        og = sb("og", [P, 2, TOK])

        sg = sb("sg", [P, 3, TOK])
        hf = [sb(f"hf{k}", [P, 3, TOK]) for k in range(2)]

        x_loaded, w1_loaded, weights_loaded, rel_written, rel_loaded = (
            sem(n) for n in ("x_loaded", "w1_loaded", "weights_loaded", "rel_written", "rel_loaded"))
        consts, zeroed, fillers = sem("consts"), sem("zeroed"), sem("fillers")
        set_v, set_t, set_a, set_g = sem("set_v"), sem("set_t"), sem("set_a"), sem("set_g")
        rows_moved, zT_stashed, out_stored = sem("rows_moved"), sem("zT_stashed"), sem("out_stored")
        add_made, x_new, stats_made, mv_made, scale_made, z_made = (
            sem(n) for n in ("add_made", "x_new", "stats_made", "mv_made", "scale_made", "z_made"))
        zT_made, hi_made, lo_made = sem("zT_made"), sem("hi_made"), sem("lo_made")
        pool_step = sem("pool_step")
        res_made, rstats_made, rmv_made, rrstd_made = (
            sem(n) for n in ("res_made", "rstats_made", "rmv_made", "rrstd_made"))
        fold_made, folded, w1hi_made, w1lo_made, dt_made = (
            sem(n) for n in ("fold_made", "folded", "w1hi_made", "w1lo_made", "dt_made"))
        step_v, step_a = sem("step_v"), sem("step_a")
        expA_made, cum_in_psum, cum_copied, parts_made, partsT_in_psum, shifted_made, wlo_made, resD_made = (
            sem(n) for n in ("expA_made", "cum_in_psum", "cum_copied", "parts_made", "partsT_in_psum", "shifted_made",
                             "wlo_made", "resD_made"))
        b1_loaded, waited = sem("b1_loaded"), sem("waited")
        proj_made, tap_made, conv_made, bc_made, th_made, xc_made, tz_made, gz_made = (
            sem("A_" + n) for n in ("proj", "tap", "conv", "bc", "th", "xc", "tz", "gz"))
        G_made, T_made, D_made, E_made, M_made, dtx_made, btok_made, wdtx_made = (
            sem("A_" + n) for n in ("G", "T", "D", "E", "M", "dtx", "btok", "wdtx"))
        Y_made, y1_made, y_made, S_made, sd_made, st_made, YT_made, yf_made, yg_made, out_made, z1_made = (
            sem("A_" + n) for n in ("Y", "y1", "y", "S", "sd", "st", "YT", "yf", "yg", "out", "z1"))
        h_made, sig_made, g_made, half_made, acc_made, accT_in_psum, accT_made, moe_made = (
            sem("B_" + n) for n in ("h", "sig", "g", "half", "acc", "accTp", "accT", "moe"))
        logits_made, gate_v, gate_a = sem("B_logits"), sem("B_gate_v"), sem("B_gate_a")
        cproj_made, cact_made, var_made, s1_made, s2_made, lkT_made, lkt_made, att_made = (
            sem("C_" + n) for n in ("proj", "act", "var", "s1", "s2", "lkT", "lkt", "att"))
        kv_made, kvs_made, o_made, og_made, cout_made, cz_made, czb_made = (
            sem("C_" + n) for n in ("kv", "kvs", "o", "og", "out", "cz", "czb"))
        gu_made, sg_made, hf_made, dn_made = (
            sem("D_" + n) for n in ("gu", "sg", "hf", "dn"))

        block = ctx.enter_context(nc.Block())

        def cols(c):
            return slice(c * P, (c + 1) * P)

        NLOADS = 28
        BCREDIT = 4
        DCREDIT = 3

        def wait_apart(engine, semaphore, value):
            engine.wait_ge(semaphore, value).then_inc(waited, 1)

        @block.sync
        def _(sp):
            loads = [
                (normw[:], norm_w), (convw[:], conv_w), (convb[:], conv_b), (w_in[:], in_wT),
                (w_out[:], out_wT.rearrange("(k p) n -> p k n", p=P)), (wg[:], WgT),
                (w_o[:], WoT.rearrange("(k p) n -> p k n", p=P)),
                (bo_rows[:], bo.to_broadcast([P, P])), (bout_rows[:], bout.to_broadcast([P, P])),
                (alog[:], A_log.to_broadcast([P, HEADS])), (dtb[:], dt_bias.to_broadcast([P, HEADS])),
                (table[:], rel.to_broadcast([GROUP, 32])),
                (w4[:, 0:512], Wh), (w4[:, 512:640], Wqk), (b4r[:, 0:512], bh), (b4r[:, 512:640], bqk),
                (lnw[:], ln_w), (lnb[:], ln_b), (qkw[:], qk_w), (qkb[:], qk_b),
                (wff_i[:, 0:FFN], wgT), (wff_i[:, FFN:2 * FFN], wuT),
                (wdn_i, wdT.rearrange("(k p) n -> p k n", p=P)),
                (w_att[:], Wout.rearrange("(k p) n -> p k n", p=P)),
            ]
            for half in range(2):
                for q in range(2):
                    head = 2 * half + q
                    loads.append((dskip[HD * q:HD * q + HD, half:half + 1],
                                  D_skip[:, head:head + 1].to_broadcast([HD, 1])))
            assert len(loads) == NLOADS
            sp.dma_start(X[:, 0], x_in[0].rearrange("(c p) d -> p c d", p=P)).then_inc(x_loaded, 16)
            for dst, src in loads:
                sp.dma_start(dst, src).then_inc(weights_loaded, 16)
            sp.dma_start(w1[:], W1T[0]).then_inc(w1_loaded, 16)
            sp.dma_start(b1r[:], b1[:, 0]).then_inc(b1_loaded, 16)

            def stash(i):
                sp.wait_ge(hi_made, i + 1)
                sp.dma_start(XT_hi[:, i, :].bitcast(F32), ZT_hi[0][:].bitcast(F32)).then_inc(zT_stashed, 16)
                wait_apart(sp, lo_made, i + 1)
                sp.dma_start(XT_lo[:, i, :].bitcast(F32), ZT_lo[0][:].bitcast(F32)).then_inc(zT_stashed, 16)

            with sp.Fori(1, SEQS) as i:
                sp.wait_ge(x_loaded, i * 16)
                sp.dma_start(X[:, i], x_in[i].rearrange("(c p) d -> p c d", p=P)).then_inc(x_loaded, 16)
                sp.wait_ge(w1lo_made, i)
                sp.dma_start(w1[:], W1T[i]).then_inc(w1_loaded, 16)
                sp.wait_ge(fold_made, i)
                sp.dma_start(b1r[:], b1[:, i]).then_inc(b1_loaded, 16)
                stash(i - 1)
            stash(SEQS - 1)
            sp.wait_ge(shifted_made, 2 + len(set(BUCKETS[16:])))
            sp.dma_start(scratch.rearrange("(p n) -> p n", n=65), shifted[:]).then_inc(rel_written, 16)
            sp.wait_ge(rel_written, 16)
            sp.wait_ge(fillers, 1)
            for g in range(P // GROUP):
                sp.dma_start(near[GROUP * g:GROUP * (g + 1), GROUP * g:GROUP * (g + 1)],
                             scratch[0:GROUP * 64].rearrange("(p n) -> p n", n=64)[:, 0:GROUP])\
                  .then_inc(rel_loaded, 16)
            sp.wait_ge(fillers, 1)
            sp.wait_ge(parts_made, 6)
            for head in range(HEADS):
                for q in range(3):
                    sp.dma_start(parts[3 * head + q:3 * head + q + 1, :, :], cpartsT[head:P:HEADS, q, :])\
                      .then_inc(rows_moved, 16)
            with sp.Fori(0, SEQS) as i:
                sp.wait_ge(x_new, 3 * SEQS + i + 1)
                sp.dma_start(out[i].rearrange("(c p) d -> p c d", p=P), X[:, i]).then_inc(out_stored, 16)
            sp.wait_ge(out_stored, 16 * SEQS)

        NROWS = 16 * 3 * HEADS

        STEPS_TWICE, STEPS_ONCE, STEPS_RES = 10, 6, 2

        @block.gpsimd
        def _(pool):
            pool.memset(ident[:], 0.0).then_inc(set_g, 1)
            pool.memset(negavg[:], -1.0 / P).then_inc(set_g, 1)
            pool.memset(avgrow[:], 1.0 / P).then_inc(set_g, 1)
            pool.memset(mhalf[:], -0.5).then_inc(set_g, 1)
            pool.memset(allneg[:], -1.0).then_inc(set_g, 1)
            pool.wait_ge(set_g, 5)
            pool.affine_select(out=ident[:], in_=ident[:], compare_op=ALU.not_equal, fill=1.0, base=0,
                               pattern=[[-1, P]], channel_multiplier=1).then_inc(consts, 1)
            pool.affine_select(out=cumneg[:], in_=allneg[:], compare_op=ALU.is_ge, fill=0.0, base=0,
                               pattern=[[1, P]], channel_multiplier=-1).then_inc(consts, 1)
            pool.iota(iota8i[:], pattern=[[1, EXPERTS]], base=0, channel_multiplier=0).then_inc(consts, 1)
            pool.wait_ge(consts, 3)
            pool.tensor_copy(iota8[:], iota8i[:]).then_inc(consts, 1)
            pool.tensor_copy(identb[:], ident[:]).then_inc(consts, 1)

            def scales(stage, i, done):
                n = stage * SEQS + i
                steps = [done]

                def step(ins):
                    steps[0] = steps[0] + 1
                    ins.then_inc(pool_step, 1)
                    wait_apart(pool, pool_step, steps[0])

                wait_apart(pool, mv_made, (n + 1) * CH)
                m, v = mv[:, :, 0], mv[:, :, 1]
                t0, r, t2, t3 = (rtmp[:, k, :] for k in range(4))
                step(pool.tensor_scalar(t0, v, LN_EPS, None, ALU.add))
                step(pool.tensor_tensor(r, t0, mhalf[:], ALU.pow))
                step(pool.tensor_copy(x_rstd[:, i, :], r))
                step(pool.tensor_copy(x_mean[:, i, :], m))
                if stage in (0, 2):
                    step(pool.tensor_tensor(t2, v, r, ALU.mult))
                    step(pool.tensor_tensor(t2, t2, r, ALU.mult))
                    step(pool.tensor_scalar(t2, t2, RMS_EPS if stage == 0 else LN_EPS, None, ALU.add))
                    step(pool.tensor_tensor(t3, t2, mhalf[:], ALU.pow))
                    step(pool.tensor_tensor(rsc[:], r, t3, ALU.mult))
                else:
                    step(pool.tensor_copy(rsc[:], r))
                step(pool.tensor_tensor(t2, m, rsc[:], ALU.mult))
                pool.tensor_scalar(shift[:], t2, -1.0, 1.0, ALU.mult, ALU.add).then_inc(scale_made, 1)
                return steps[0]

            def res_scales(stage, i, done):
                n = (stage - 1) * SEQS + i
                wait_apart(pool, rmv_made, (n + 1) * CH)
                pool.tensor_scalar(rvar[:], rmv[:, :, 1], LN_EPS, None, ALU.add).then_inc(pool_step, 1)
                wait_apart(pool, pool_step, done + 1)
                pool.tensor_tensor(res_rstd[:, i, :], rvar[:], mhalf[:], ALU.pow).then_inc(pool_step, 1)
                wait_apart(pool, pool_step, done + 2)
                pool.tensor_copy(res_mean[:, i, :], rmv[:, :, 0]).then_inc(rrstd_made, 1)
                return done + STEPS_RES

            done = scales(0, 0, 0)
            assert done == STEPS_TWICE
            pool.wait_ge(set_a, 1)
            pool.tensor_tensor(w_in_lo[:], w_in[:], w_in_hi[:].bitcast(F32), ALU.subtract).then_inc(wlo_made, 1)

            def stage0(i, done, last=False):
                if not last:
                    done = scales(0, i + 1, done)
                pool.wait_ge(w1hi_made, i + 1)
                pool.tensor_tensor(w1_lo[:, i, :], w1[:], w1_hi[:, i, :].bitcast(F32), ALU.subtract)\
                    .then_inc(w1lo_made, 1)
                return done

            with pool.Fori(0, SEQS - 1) as i:
                stage0(i, done + i * STEPS_TWICE)
            done += (SEQS - 1) * STEPS_TWICE
            stage0(SEQS - 1, done, last=True)

            pool.memset(parts[:].bitcast(F32), 0.0).then_inc(set_g, 1)
            pool.memset(headrows[:], 1.0).then_inc(set_g, 1)
            pool.memset(far4[:], 0.0).then_inc(set_g, 1)
            pool.wait_ge(set_g, 8)
            pool.affine_select(out=headrows[:], in_=headrows[:], compare_op=ALU.is_ge, fill=0.0, base=0,
                               pattern=[[-3, HEADS], [0, P]], channel_multiplier=1).then_inc(set_g, 1)
            pool.affine_select(out=far4[:], in_=far4[:], compare_op=ALU.is_ge, fill=FAR, base=0,
                               pattern=[[0, HEADS], [1, P]], channel_multiplier=-1).then_inc(set_g, 1)
            pool.wait_ge(set_g, 10)
            pool.affine_select(out=headrows[:], in_=headrows[:], compare_op=ALU.is_ge, fill=0.0, base=2,
                               pattern=[[3, HEADS], [0, P]], channel_multiplier=-1).then_inc(set_g, 1)
            pool.wait_ge(set_g, 11)
            pool.tensor_scalar(headrows_neg[:], headrows[:], -1.0, None, ALU.mult).then_inc(set_g, 1)
            pool.wait_ge(set_g, 12)
            pool.memset(near[:], FAR).then_inc(fillers, 1)
            pool.memset(before[:], 1.0 / GROUP).then_inc(fillers, 1)
            pool.wait_ge(fillers, 2)
            for g in range(P // GROUP):
                pool.memset(before[GROUP * g:GROUP * (g + 1), 0:GROUP * (g + 1)], 0.0).then_inc(fillers, 1)
            pool.wait_ge(fillers, 2 + P // GROUP)
            for n, (lo, w, hi) in enumerate(((wg_lo, wg, wg_hi), (w4_lo, w4s, w4_hi), (wff_lo, wff, wff_hi))):
                pool.wait_ge(set_a, n + 2)
                pool.tensor_tensor(lo[:], w[:], hi[:].bitcast(F32), ALU.subtract).then_inc(wlo_made, 1)
            pool.wait_ge(rel_loaded, 16 * (P // GROUP))
            pool.affine_select(out=near[:], in_=near[:], compare_op=ALU.is_ge, fill=FAR, base=0,
                               pattern=[[1, P]], channel_multiplier=-1).then_inc(fillers, 1)

            def stageA(i, done):
                for c in range(CH - 1):
                    pool.wait_ge(dtx_made, i * CH + c + 1)
                    pool.wait_ge(S_made, i * 3 + c)
                    pool.tensor_tensor(wdtx[:].rearrange("p (h d) -> p h d", h=HEADS),
                                       dtx[:, c % 2].rearrange("p (h d) -> p h d", h=HEADS),
                                       etail_t[:, i, c, :].unsqueeze(2).to_broadcast([P, HEADS, HD]), ALU.mult)\
                        .then_inc(wdtx_made, 1)
                    if c > 0:
                        pool.wait_ge(st_made, i * 3 + c)
                        pool.tensor_tensor(Sd[:].rearrange("p (h d) -> p h d", h=HEADS),
                                           St[:].rearrange("p (h d) -> p h d", h=HEADS),
                                           dec_t[:, i, c, :].unsqueeze(2).to_broadcast([P, HEADS, HD]), ALU.mult)\
                            .then_inc(sd_made, 1)
                for half in range(2):
                    pool.wait_ge(yf_made, i * 2 + half + 1)
                    pool.tensor_tensor(yf[:, half], yf[:, half], gz[:, half], ALU.mult).then_inc(yg_made, 1)
                return res_scales(1, i, done)

            with pool.Fori(0, SEQS) as i:
                stageA(i, done + i * STEPS_RES)
            done += SEQS * STEPS_RES

            def stageB(i, par, done, first=False, last=False):
                if not last:
                    done = scales(1, i + 1, done)
                for c in range(CH):
                    t = i * CH + c
                    pool.wait_ge(g_made, t * EXPERTS + 4 + BCREDIT)
                    b = gb[:, c % 2]
                    pool.tensor_tensor(b[:, 0:2], b[:, 0:2], b[:, 2:4], ALU.add).then_inc(half_made, 1)
                    pool.wait_ge(g_made, t * EXPERTS + 8 + BCREDIT)
                    pool.tensor_tensor(b[:, 4:6], b[:, 4:6], b[:, 6:8], ALU.add).then_inc(half_made, 1)
                    pool.wait_ge(half_made, t * 3 + 2)
                    pool.tensor_tensor(b[:, 0:2], b[:, 0:2], b[:, 4:6], ALU.add).then_inc(half_made, 1)
                    if c == 2 and not first:
                        done = res_scales(2, i - 1, done)
                return done

            done = scales(1, 0, done)
            done = stageB(0, 0, done, first=True)
            both = STEPS_ONCE + STEPS_RES
            with pool.Fori(1, SEQS - 2, 2) as i:
                for par in (1, 0):
                    k = 1 - par
                    stageB(i + k, par, done + (i - 1 + k) * both)
            done += (SEQS - 2) * both
            done = stageB(SEQS - 1, 1, done, last=True)
            done = res_scales(2, SEQS - 1, done)

            def stageC(i, done, last=0):
                if last < 1:
                    done = scales(2, i + 2, done)
                pool.wait_ge(cz_made, (i + 1) * CH)
                pool.tensor_tensor(z1[:], z1[:], bout_rows[:].unsqueeze(1).to_broadcast([P, CH, P]), ALU.add)\
                    .then_inc(czb_made, 1)
                return res_scales(3, i, done)

            done = scales(2, 0, done)
            done = scales(2, 1, done)
            both = STEPS_TWICE + STEPS_RES
            with pool.Fori(0, SEQS - 2) as i:
                stageC(i, done + i * both)
            done += (SEQS - 2) * both
            done = stageC(SEQS - 2, done, 1)
            done = stageC(SEQS - 1, done, 2)

            def stageD(i, done, first=False, last=0):
                if last < 1:
                    done = scales(3, i + 2, done)
                if not first:
                    done = res_scales(4, i - 1, done)
                return done

            done = scales(3, 0, done)
            done = scales(3, 1, done)
            both = STEPS_ONCE + STEPS_RES
            done = stageD(0, done, first=True)
            with pool.Fori(1, SEQS - 2) as i:
                stageD(i, done + (i - 1) * both)
            done += (SEQS - 3) * both
            done = stageD(SEQS - 2, done, last=1)
            done = stageD(SEQS - 1, done, last=2)
            res_scales(4, SEQS - 1, done)

        @block.scalar
        def _(act):
            def hi(stage, i, par, free, value):
                act.wait_ge(zT_made, stage * SEQS + i + 1)
                if free is not None:
                    act.wait_ge(free, value)
                act.activation(ZT_hi[par][:], bank(5), ACT.Copy).then_inc(hi_made, 1)

            act.wait_ge(weights_loaded, 16 * NLOADS)
            act.activation(expA[:], alog[:], ACT.Exp).then_inc(expA_made, 1)
            act.wait_ge(set_v, 1)
            act.activation(w_in_hi[:], w_in[:], ACT.Copy).then_inc(set_a, 1)

            with act.Fori(0, SEQS) as i:
                act.wait_ge(zT_stashed, i * 32)
                hi(0, i, 0, dt_made, i)
                act.wait_ge(folded, i + 1)
                act.activation(w1_hi[:, i, :], w1[:], ACT.Copy).then_inc(w1hi_made, 1)
            act.wait_ge(step_v, 1)
            act.activation(sm[:, 1], sm[:, 0], ACT.Abs).then_inc(step_a, 1)
            act.wait_ge(step_a, 1)
            act.activation(sm[:, 2], sm[:, 1], ACT.Exp, scale=-1.0).then_inc(step_a, 1)

            def small(a):
                return a[:].rearrange("p s c h -> p (s c h)")

            act.wait_ge(cum_copied, 2)
            act.activation(small(ecum_t), sm[:, 3], ACT.Exp).then_inc(step_a, 1)
            act.activation(small(etail_t), sm[:, 4], ACT.Exp).then_inc(step_a, 1)
            act.activation(small(dec_t), bank(4)[:, 0:NC], ACT.Exp).then_inc(step_a, 1)

            for n, (h, w) in enumerate(((wg_hi, wg), (w4_hi, w4s), (wff_hi, wff))):
                act.wait_ge(set_v, (7, 9, 10)[n])
                act.activation(h[:], w[:], ACT.Copy).then_inc(set_a, 1)

            def frontA(i):
                for half in range(2):
                    act.wait_ge(proj_made, i * 6 + half + 1)
                    act.wait_ge(xc_made, i * 2)
                    act.activation(u[:, half], bank(half), ACT.Identity, bias=convb[:, half:half + 1],
                                   scale=convw[:, half, 3:4]).then_inc(tap_made, 1)
                for n, (dst, b) in enumerate(((Bf, 2), (Cf, 0))):
                    act.wait_ge(proj_made, i * 6 + 3 + n)
                    act.wait_ge(Y_made, i * CH)
                    act.activation(dst[:], bank(b), ACT.Copy).then_inc(bc_made, 1)
                for half in range(2):
                    act.wait_ge(conv_made, i * 6 + 3 * half + 3)
                    act.activation(th[:, half], u[:, half], ACT.Tanh).then_inc(th_made, 1)
                for half in range(2):
                    act.wait_ge(proj_made, i * 6 + 5 + half)
                    act.wait_ge(yg_made, i * 2)
                    act.activation(gz[:, half], bank(1 + half), ACT.Tanh, scale=0.5).then_inc(tz_made, 1)

            def midA(i):
                for c in range(CH):
                    act.wait_ge(D_made, i * CH + c + 1)
                    act.wait_ge(Y_made, i * CH + max(c - 1, 0))
                    act.activation(Edec[:, c % 2].rearrange("p h i -> p (h i)"), bank(4), ACT.Exp).then_inc(E_made, 1)
                    if c < CH - 1:
                        act.wait_ge(dtx_made, i * CH + c + 1)
                        act.wait_ge(S_made, i * 3 + c)
                        act.activation(Btok[:], bank(3)[:, INNER:INNER + P], ACT.Copy).then_inc(btok_made, 1)

            frontA(0)
            with act.Fori(0, SEQS - 1) as i:
                midA(i)
                frontA(i + 1)
            midA(SEQS - 1)

            def gateB(i):
                act.wait_ge(gate_v, i * GATE_STEPS + 7)
                act.activation(ge[:, 1], ge[:, 0], ACT.Sigmoid).then_inc(gate_a, 1)
                act.activation(ge[:, 2], ge[:, 0], ACT.Sigmoid, scale=-1.0).then_inc(gate_a, 1)

            def accT_copy(t):
                act.wait_ge(accT_in_psum, t + 1)
                act.wait_ge(moe_made, t)
                act.activation(accT[:], bank(6)[:, 0:HID].rearrange("p (k n) -> p k n", k=2), ACT.Copy)\
                    .then_inc(accT_made, 1)

            def stageB(i, par, first=False, last=False):
                for c in range(CH):
                    t = i * CH + c
                    for e in range(EXPERTS):
                        n = t * EXPERTS + e
                        act.wait_ge(h_made, n + 1)
                        act.wait_ge(g_made, n + 1)
                        act.activation(sig[:, e % 4], bank(e % 4)[:, HID:2 * HID], ACT.Sigmoid).then_inc(sig_made, 1)
                        if e == 0 and not (first and c < 2):
                            accT_copy(t - 2)
                        if e == 5 and c == 1 and not last:
                            hi(1, i + 1, 1 - par, h_made, i * 32)
                    if c == 2 and not last:
                        gateB(i + 1)

            hi(1, 0, 0, zT_stashed, 32 * SEQS)
            gateB(0)
            stageB(0, 0, first=True)
            with act.Fori(1, SEQS - 2, 2) as i:
                stageB(i, 1)
                stageB(i + 1, 0)
            stageB(SEQS - 1, 1, last=True)
            accT_copy(NT - 2)
            accT_copy(NT - 1)

            def frontC(i):
                act.wait_ge(cproj_made, i * 5 + 1)
                act.wait_ge(var_made, i * 4)
                act.activation(qkf[:], bank(2), ACT.Silu).then_inc(cact_made, 1)
                act.wait_ge(o_made, i * 2)
                for k in range(2):
                    act.wait_ge(cproj_made, i * 5 + 2 + k)
                    act.activation(vt[:, 2 * k:2 * k + 2, :], bank(3 + k).rearrange("p (c n) -> p c n", c=2), ACT.Silu)\
                        .then_inc(cact_made, 1)
                for half in range(2):
                    act.wait_ge(cproj_made, i * 5 + 4 + half)
                    act.wait_ge(og_made, i * 2)
                    act.activation(gt[:, half], bank(half), ACT.Silu).then_inc(cact_made, 1)

            def stageC(i, par, last=0):
                act.wait_ge(lkT_made, i + 1)
                act.wait_ge(kv_made, i * 3)
                act.activation(lkt[:].rearrange("p c d -> p (c d)"), bank(2), ACT.Copy).then_inc(lkt_made, 1)
                for c in range(3):
                    act.wait_ge(kv_made, i * 3 + c + 1)
                    act.wait_ge(o_made, i * 2)
                    act.activation(kvs[:, c], bank(3)[:, 0:HID], ACT.Copy, scale=1.0 / GROUP).then_inc(kvs_made, 1)
                if last < 1:
                    hi(2, i + 2, par, cproj_made, (i + 1) * 5)
                if last < 2:
                    frontC(i + 1)

            hi(2, 0, 0, None, 0)
            hi(2, 1, 1, None, 0)
            frontC(0)
            with act.Fori(0, SEQS - 3, 2) as i:
                stageC(i, 0)
                stageC(i + 1, 1)
            stageC(SEQS - 2, 0, 1)
            stageC(SEQS - 1, 1, 2)

            def stageD(i, par, first=False, last=False):
                if not last:
                    hi(3, i + 1, 1 - par, gu_made, i * 3)
                for m in range(3):
                    act.wait_ge(gu_made, i * 3 + m + 1)
                    act.wait_ge(hf_made, i * 3 + m + 1)
                    act.activation(sg[:, m], bank(m), ACT.Silu, scale=1.0 / 127).then_inc(sg_made, 1)
                if not first:
                    residD(i - 1)

            def residD(i):
                act.wait_ge(dn_made, i + 1)
                act.activation(RES[:, i].rearrange("p c d -> p (c d)"), bank(7), ACT.Copy).then_inc(resD_made, 1)

            hi(3, 0, 0, None, 0)
            stageD(0, 0, first=True)
            with act.Fori(1, SEQS - 2, 2) as i:
                stageD(i, 1)
                stageD(i + 1, 0)
            stageD(SEQS - 1, 1, last=True)
            residD(SEQS - 1)

        @block.vector
        def _(dve):
            def apart(semaphore, value):
                wait_apart(dve, semaphore, value)

            def stats(stage, i):
                n = stage * SEQS + i
                apart(mv_made, n * CH)
                for c in range(CH):
                    dve.bn_stats(stats_t[:, c], X[:, i, c]).then_inc(stats_made, 1)
                dve.wait_ge(stats_made, (n + 1) * CH)
                apart(scale_made, n)
                for c in range(CH):
                    dve.bn_aggr(mv[:, c], stats_t[:, c]).then_inc(mv_made, 1)

            def apply(stage, i):
                n = (stage - 1) * SEQS + i
                dve.wait_ge(rrstd_made, n + 1)
                for c in range(CH):
                    dve.tensor_scalar(add[:, c], RES[:, i, c], res_mean[:, i, c:c + 1], res_rstd[:, i, c:c + 1],
                                      ALU.subtract, ALU.mult).then_inc(add_made, 1)
                dve.wait_ge(add_made, (n + 1) * CH)
                dve.tensor_tensor(X[:, i], X[:, i], add[:], ALU.add).then_inc(x_new, 1)
                dve.wait_ge(x_new, n + 1)

            def z(stage, i):
                n = stage * SEQS + i
                dve.wait_ge(scale_made, n + 1)
                dve.wait_ge(zT_made, n)
                for c in range(CH):
                    if stage in (0, 3):
                        dve.tensor_scalar(Z[:, c], X[:, i, c], mv[:, c, 0:1], rsc[:, c:c + 1],
                                          ALU.subtract, ALU.mult).then_inc(z_made, 1)
                    else:
                        dve.tensor_scalar(Z[:, c], X[:, i, c], rsc[:, c:c + 1], shift[:, c:c + 1],
                                          ALU.mult, ALU.add).then_inc(z_made, 1)

            def lo(stage, i, par):
                dve.wait_ge(hi_made, stage * SEQS + i + 1)
                dve.tensor_tensor(ZT_lo[par][:], bank(5), ZT_hi[par][:].bitcast(F32), ALU.subtract).then_inc(lo_made, 1)

            def rstats(stage, i):
                n = (stage - 1) * SEQS + i
                apart(rmv_made, n * CH)
                for c in range(CH):
                    dve.bn_stats(rstats_t[:, c], RES[:, i, c]).then_inc(rstats_made, 1)
                dve.wait_ge(rstats_made, (n + 1) * CH)
                apart(rrstd_made, n)
                for c in range(CH):
                    dve.bn_aggr(rmv[:, c], rstats_t[:, c]).then_inc(rmv_made, 1)

            dve.memset(credit[:, 0:1], 0.0).then_inc(g_made, BCREDIT)
            dve.memset(credit[:, 1:2], 0.0).then_inc(hf_made, DCREDIT)

            dve.wait_ge(x_loaded, 16)
            stats(0, 0)
            dve.wait_ge(weights_loaded, 16 * NLOADS)
            dve.tensor_scalar(w_in[:], w_in[:], normw[:], None, ALU.mult).then_inc(set_v, 1)

            def stage0(i, last=False):
                if not last:
                    dve.wait_ge(x_loaded, (i + 2) * 16)
                z(0, i)
                if not last:
                    stats(0, i + 1)
                dve.wait_ge(fold_made, i + 1)
                dve.tensor_tensor(w1[:], w1[:], bank(1), ALU.add).then_inc(folded, 1)
                lo(0, i, 0)

            with dve.Fori(0, SEQS - 1) as i:
                stage0(i)
            stage0(SEQS - 1, last=True)

            cb = lambda a: a.unsqueeze(1).to_broadcast([P, NT, HEADS])
            th3 = lambda a: a.rearrange("p (t h) -> p t h", h=HEADS)
            flat = lambda a: a[:].rearrange("p s c h -> p (s c h)")
            steps = [0]

            def step(ins):
                steps[0] += 1
                ins.then_inc(step_v, 1)
                dve.wait_ge(step_v, steps[0])

            dve.wait_ge(dt_made, SEQS)
            step(dve.tensor_tensor(th3(sm[:, 0]), th3(bank(2)[:, 0:NC]), cb(dtb[:]), ALU.add))
            dve.wait_ge(step_a, 2)
            step(dve.tensor_scalar(sm[:, 5], sm[:, 2], 2.0, None, ALU.add))
            step(dve.reciprocal(sm[:, 6], sm[:, 5]))
            step(dve.tensor_tensor(sm[:, 7], sm[:, 2], sm[:, 6], ALU.mult))
            step(dve.tensor_tensor(sm[:, 5], sm[:, 7], sm[:, 7], ALU.mult))
            step(dve.tensor_scalar(sm[:, 6], sm[:, 5], 1.0 / 15, None, ALU.mult))
            for k in (13, 11, 9, 7, 5, 3):
                step(dve.scalar_tensor_tensor(sm[:, 6], sm[:, 6], 1.0 / k, sm[:, 5], ALU.add, ALU.mult))
            step(dve.scalar_tensor_tensor(sm[:, 6], sm[:, 6], 1.0, sm[:, 7], ALU.add, ALU.mult))
            step(dve.tensor_scalar(sm[:, 1], sm[:, 0], 0.0, None, ALU.max))
            step(dve.scalar_tensor_tensor(flat(dt_t), sm[:, 6], 2.0, sm[:, 1], ALU.mult, ALU.add))
            dve.wait_ge(expA_made, 1)
            step(dve.tensor_tensor(th3(sm[:, 7]), th3(flat(dt_t)), cb(expA[:]), ALU.mult))
            assert steps[0] == 16
            dve.wait_ge(cum_in_psum, 2)
            dve.tensor_copy(sm[:, 3], bank(3)[:, 0:NC]).then_inc(cum_copied, 1)
            dve.wait_ge(cum_copied, 1)
            dve.tensor_tensor(sm[:, 4], bank(4)[:, 0:NC], sm[:, 3], ALU.subtract).then_inc(cum_copied, 1)
            dve.tensor_copy(cparts[:, 0], sm[:, 3]).then_inc(parts_made, 1)
            dve.wait_ge(parts_made, 1)
            dve.tensor_tensor(sm[:, 5], sm[:, 3], cparts[:, 0], ALU.subtract).then_inc(parts_made, 1)
            dve.wait_ge(parts_made, 2)
            dve.tensor_copy(cparts[:, 1], sm[:, 5]).then_inc(parts_made, 1)
            dve.wait_ge(parts_made, 3)
            dve.tensor_tensor(sm[:, 6], sm[:, 5], cparts[:, 1], ALU.subtract).then_inc(parts_made, 1)
            dve.wait_ge(parts_made, 4)
            dve.tensor_copy(cparts[:, 2], sm[:, 6]).then_inc(parts_made, 1)
            dve.wait_ge(partsT_in_psum, 1)
            dve.tensor_copy(cpartsT[:], bank(6).bitcast(BF16)[:, 0:3 * P].rearrange("p (q n) -> p q n", q=3))\
               .then_inc(parts_made, 1)

            dve.tensor_scalar(convw[:], convw[:], 0.5, None, ALU.mult).then_inc(set_v, 1)
            dve.tensor_scalar(convb[:], convb[:], 0.5, None, ALU.mult).then_inc(set_v, 1)
            dve.tensor_scalar(w_out[:], w_out[:], 0.5, None, ALU.mult).then_inc(set_v, 1)
            dve.tensor_scalar(w4s[:], w4[:], lnw[:], None, ALU.mult).then_inc(set_v, 1)
            dve.tensor_scalar(lnb_avg[:], allneg[:], lnb[:], -1.0 / P, ALU.mult, ALU.mult).then_inc(set_v, 1)
            dve.memset(shifted[:], 0.0).then_inc(shifted_made, 1)
            dve.wait_ge(shifted_made, 1)
            root = float(P) ** 0.5
            dve.tensor_scalar(shifted[:, 0:16], table[:, 0:16], root, None, ALU.mult).then_inc(shifted_made, 1)
            for k in sorted(set(BUCKETS[16:])):
                first, many = BUCKETS.index(k), BUCKETS.count(k)
                dve.tensor_scalar(shifted[:, first:first + many], table[:, k:k + 1].to_broadcast([GROUP, many]), root,
                                  None, ALU.mult).then_inc(shifted_made, 1)
            dve.wait_ge(set_t, 1)
            dve.tensor_tensor(wg[:], wg[:], bank(6)[:, 0:EXPERTS], ALU.add).then_inc(set_v, 1)
            dve.wait_ge(set_t, 2)
            dve.tensor_tensor(w4s[:, 0:512], w4s[:, 0:512], bank(0), ALU.add).then_inc(set_v, 1)
            dve.tensor_tensor(w4s[:, 512:640], w4s[:, 512:640], bank(1)[:, 0:P], ALU.add).then_inc(set_v, 1)
            dve.tensor_copy(wff[:], wff_i).then_inc(set_v, 1)
            dve.tensor_copy(wdn[:], wdn_i).then_inc(set_v, 1)

            def heads(a):
                return a.rearrange("p (h d) -> p h d", h=HEADS)

            def byhead(a, i, c):
                return a[:, i, c, :].unsqueeze(2).to_broadcast([P, HEADS, HD])

            def convA(i):
                for half in range(2):
                    dve.wait_ge(tap_made, i * 2 + half + 1)
                    for k in range(1, 4):
                        if k > 1:
                            dve.wait_ge(conv_made, i * 6 + 3 * half + k - 1)
                        dve.scalar_tensor_tensor(u[:, half, k:], bank(half)[:, 0:TOK - k], convw[:, half, 3 - k:4 - k],
                                                 u[:, half, k:], ALU.mult, ALU.add).then_inc(conv_made, 1)

            def xcA(i):
                dve.wait_ge(yf_made, i * 2)
                for half in range(2):
                    dve.wait_ge(th_made, i * 2 + half + 1)
                    dve.scalar_tensor_tensor(xc[:, half], th[:, half], 1.0, u[:, half], ALU.add, ALU.mult)\
                       .then_inc(xc_made, 1)

            def gzA(i):
                for half in range(2):
                    dve.wait_ge(tz_made, i * 2 + half + 1)
                    dve.scalar_tensor_tensor(gz[:, half], gz[:, half], 1.0, bank(1 + half), ALU.add, ALU.mult)\
                       .then_inc(gz_made, 1)

            def chunk_in(i, c):
                t = i * CH + c
                dve.wait_ge(T_made, t + 1)
                dve.wait_ge(Y_made, i * CH + max(c - 1, 0))
                dve.wait_ge(wdtx_made, i * 3 + max(c - 1, 0))
                dve.tensor_tensor(heads(dtx[:, c % 2]), heads(bank(3)[:, 0:INNER]), byhead(dt_t, i, c), ALU.mult)\
                   .then_inc(dtx_made, 1)
                dve.wait_ge(E_made, t + 1)
                dve.wait_ge(G_made, i + 1)
                dve.tensor_tensor(Mdec[:, c % 2], Edec[:, c % 2],
                                  bank(5)[:, cols(c)].unsqueeze(1).to_broadcast([P, HEADS, P]), ALU.mult)\
                   .then_inc(M_made, 1)

            def midA(i):
                chunk_in(i, 0)
                for c in range(CH):
                    t = i * CH + c
                    if c + 1 < CH:
                        chunk_in(i, c + 1)
                    dve.wait_ge(Y_made, t + 1)
                    dve.wait_ge(YT_made, i)
                    if c == 0:
                        dve.tensor_copy(ytok[:, c], bank(6)[:, 0:INNER]).then_inc(y_made, 1)
                    else:
                        dve.tensor_tensor(heads(ytok[:, c]), heads(bank(6)[:, INNER:2 * INNER]), byhead(ecum_t, i, c), ALU.mult)\
                           .then_inc(y1_made, 1)
                        dve.wait_ge(y1_made, i * 3 + c)
                        dve.tensor_tensor(ytok[:, c], ytok[:, c], bank(6)[:, 0:INNER], ALU.add).then_inc(y_made, 1)
                    if c == 0:
                        dve.wait_ge(S_made, i * 3 + 1)
                        dve.tensor_copy(St[:], bank(7)[:, 0:INNER]).then_inc(st_made, 1)
                    elif c < CH - 1:
                        dve.wait_ge(S_made, i * 3 + c + 1)
                        dve.wait_ge(sd_made, i * 2 + c)
                        dve.tensor_tensor(St[:], Sd[:], bank(7)[:, 0:INNER], ALU.add).then_inc(st_made, 1)

            def yfA(i):
                dve.wait_ge(YT_made, i + 1)
                dve.wait_ge(out_made, i)
                for half in range(2):
                    dve.scalar_tensor_tensor(yf[:, half], xc[:, half], dskip[:, half:half + 1], bank(4 + half),
                                             ALU.mult, ALU.add).then_inc(yf_made, 1)

            def input_z(i, made):
                for c in range(CH):
                    dve.tensor_scalar(z1[:, c], X[:, i, c], x_mean[:, i, c:c + 1], x_rstd[:, i, c:c + 1],
                                      ALU.subtract, ALU.mult).then_inc(made, 1)

            def residA(i):
                input_z(i, z1_made)
                dve.wait_ge(z1_made, (i + 1) * CH)
                dve.wait_ge(out_made, i + 1)
                dve.tensor_tensor(RES[:, i], z1[:], bank(7).rearrange("p (c d) -> p c d", c=CH), ALU.add)\
                   .then_inc(res_made, 1)
                dve.wait_ge(res_made, i + 1)
                rstats(1, i)

            convA(0)
            xcA(0)
            gzA(0)
            with dve.Fori(0, SEQS - 1) as i:
                midA(i)
                convA(i + 1)
                yfA(i)
                xcA(i + 1)
                gzA(i + 1)
                residA(i)
            midA(SEQS - 1)
            yfA(SEQS - 1)
            residA(SEQS - 1)

            def gateB(i, par):
                dve.wait_ge(logits_made, i + 1)
                g = [i * GATE_STEPS]

                def step(ins):
                    g[0] = g[0] + 1
                    ins.then_inc(gate_v, 1)

                def after():
                    dve.wait_ge(gate_v, g[0])

                def bc(a):
                    return a.to_broadcast([P, CH, EXPERTS])

                below, sg1, sg2, ex = (ge[:, k] for k in range(4))
                step(dve.tensor_copy(lg[:], bank(4)[:, 0:CH * EXPERTS].rearrange("p (c e) -> p c e", c=CH)))
                apart(gate_v, g[0])
                for c in range(CH):
                    step(dve.max(top[:, c], lg[:, c]))
                after()
                step(dve.tensor_tensor(below[:, :, 0:EXPERTS], lg[:], bc(top[:, :, 0:1]), ALU.subtract))
                step(dve.tensor_tensor(below[:, :, EXPERTS:], top[:, :, 1:2], top[:, :, 0:1], ALU.subtract))
                for c in range(CH):
                    step(dve.max_index(topi[:, c], top[:, c], lg[:, c]))
                after()
                step(dve.tensor_copy(topf[:], topi[:, :, 0:2]))
                after()
                iota_b = iota8[:].unsqueeze(1).to_broadcast([P, CH, EXPERTS])
                step(dve.tensor_tensor(pick[:, 0], iota_b, bc(topf[:, :, 0:1]), ALU.is_equal))
                step(dve.tensor_tensor(pick[:, 1], iota_b, bc(topf[:, :, 1:2]), ALU.is_equal))
                dve.wait_ge(gate_a, (i + 1) * 2)
                step(dve.reciprocal(ex, sg2))
                after()
                step(dve.tensor_tensor(ex, ex, sg1, ALU.mult))
                after()
                total, both, first, second = (gs[:, k] for k in range(4))
                e2 = ex[:, :, EXPERTS]
                step(dve.reduce_sum(total, ex[:, :, 0:EXPERTS], AX.X))
                after()
                step(dve.scalar_tensor_tensor(both, total, TOP_EPS, e2, ALU.mult, ALU.add))
                after()
                step(dve.tensor_scalar(both, both, 1.0, None, ALU.add))
                after()
                step(dve.reciprocal(first, both))
                after()
                step(dve.tensor_tensor(second, e2, first, ALU.mult))
                after()
                step(dve.tensor_tensor(csum[par][:], first, second, ALU.add))
                step(dve.tensor_tensor(pick[:, 0], pick[:, 0], bc(first.unsqueeze(2)), ALU.mult))
                step(dve.tensor_tensor(pick[:, 1], pick[:, 1], bc(second.unsqueeze(2)), ALU.mult))
                after()
                step(dve.tensor_tensor(comb[par][:], pick[:, 0], pick[:, 1], ALU.add))
                after()

            def accB(t, k, free):
                dve.wait_ge(half_made, (t + 1) * 3)
                if free:
                    dve.wait_ge(accT_in_psum, t - 1)
                dve.tensor_tensor(acc[k][:], gb[:, k, 0], gb[:, k, 1], ALU.add).then_inc(acc_made, 1)

            def residB(i, par):
                dve.wait_ge(moe_made, (i + 1) * CH)
                for c in range(CH):
                    ins = dve.scalar_tensor_tensor(RES[:, i, c], bo_rows[:], csum[par][:, c:c + 1], bank(7)[:, cols(c)],
                                                   ALU.mult, ALU.add)
                ins.then_inc(res_made, 1)
                dve.wait_ge(res_made, SEQS + i + 1)
                rstats(2, i)

            def stageB(i, par, first=False, last=False):
                if not last:
                    apply(1, i + 1)
                    stats(1, i + 1)
                for c in range(CH):
                    t = i * CH + c
                    if c == 2:
                        if not last:
                            lo(1, i + 1, 1 - par)
                        if not first:
                            residB(i - 1, 1 - par)
                    for e in range(EXPERTS):
                        dve.wait_ge(sig_made, t * EXPERTS + e + 1)
                        dve.scalar_tensor_tensor(gb[:, c % 2, e], bank(e % 4)[:, 0:HID], comb[par][:, c, e:e + 1],
                                                 sig[:, e % 4], ALU.mult, ALU.mult).then_inc(g_made, 1)
                        if e == 5 and not (first and c == 0):
                            accB(t - 1, (c + 1) % 2, not (first and c < 3))
                    if c == 0 and not last:
                        z(1, i + 1)
                    if c == 2 and not last:
                        gateB(i + 1, 1 - par)

            apply(1, 0)
            stats(1, 0)
            z(1, 0)
            lo(1, 0, 0)
            gateB(0, 0)
            stageB(0, 0, first=True)
            with dve.Fori(1, SEQS - 2, 2) as i:
                stageB(i, 1)
                stageB(i + 1, 0)
            stageB(SEQS - 1, 1, last=True)
            accB(NT - 1, 1, True)
            residB(SEQS - 1, 1)

            def variants(i):
                dve.wait_ge(cact_made, i * 5 + 1)
                dve.wait_ge(o_made, i * 2)
                for k in (2, 0, 3, 1):
                    dve.tensor_scalar(qv[:, k], qkf[:], qkw[:, k:k + 1], qkb[:, k:k + 1], ALU.mult, ALU.add)\
                       .then_inc(var_made, 1)

            def stageC(i, par, last=0):
                if last < 1:
                    apply(2, i + 2)
                    stats(2, i + 2)
                quad = at[:, 0].rearrange("p (c i) -> p c i", c=CH)
                lin = at[:, 1].rearrange("p (c i) -> p c i", c=CH)
                dve.wait_ge(s1_made, i + 1)
                dve.scalar_tensor_tensor(quad, bank(6).rearrange("p (c i) -> p c i", c=CH), 1.0 / GROUP,
                                         near[:].unsqueeze(1).to_broadcast([P, CH, P]), ALU.mult, ALU.add)\
                   .then_inc(att_made, 1)
                dve.wait_ge(att_made, i * 4 + 1)
                dve.scalar_tensor_tensor(at[:, 0], at[:, 0], 0.0, at[:, 0], ALU.max, ALU.mult).then_inc(att_made, 1)
                dve.wait_ge(s2_made, i + 1)
                dve.tensor_tensor(lin, bank(7).rearrange("p (c i) -> p c i", c=CH),
                                  before[:].unsqueeze(1).to_broadcast([P, CH, P]), ALU.mult).then_inc(att_made, 1)
                dve.wait_ge(att_made, i * 4 + 3)
                dve.tensor_tensor(at[:, 0], at[:, 0], at[:, 1], ALU.add).then_inc(att_made, 1)
                input_z(i, cz_made)
                if last < 1:
                    z(2, i + 2)
                    lo(2, i + 2, par)
                for half in range(2):
                    dve.wait_ge(o_made, i * 2 + half + 1)
                    dve.wait_ge(cact_made, i * 5 + 4 + half)
                    dve.wait_ge(cout_made, i)
                    dve.tensor_tensor(og[:, half], bank(6 + half), gt[:, half], ALU.mult).then_inc(og_made, 1)
                if last < 2:
                    variants(i + 1)
                dve.wait_ge(czb_made, i + 1)
                dve.wait_ge(cout_made, i + 1)
                dve.tensor_tensor(RES[:, i], z1[:], bank(5).rearrange("p (c d) -> p c d", c=CH), ALU.add)\
                   .then_inc(res_made, 1)
                dve.wait_ge(res_made, 2 * SEQS + i + 1)
                rstats(3, i)

            for k in range(2):
                apply(2, k)
                stats(2, k)
                z(2, k)
                lo(2, k, k)
            variants(0)
            dve.wait_ge(fillers, 7)
            with dve.Fori(0, SEQS - 3, 2) as i:
                stageC(i, 0)
                stageC(i + 1, 1)
            stageC(SEQS - 2, 0, 1)
            stageC(SEQS - 1, 1, 2)

            def rstatsD(i):
                dve.wait_ge(resD_made, i + 1)
                rstats(4, i)

            def stageD(i, par, first=False, last=0):
                if last < 2:
                    z(3, i + 1)
                for m in range(3):
                    dve.wait_ge(sg_made, i * 3 + m + 1)
                    if not first:
                        dve.wait_ge(dn_made, i - 1)
                    dve.scalar_tensor_tensor(hf[par][:, m], bank((3, 4, 6)[m]), 1.0 / (127 * 127), sg[:, m],
                                             ALU.mult, ALU.mult).then_inc(hf_made, 1)
                if last < 2:
                    lo(3, i + 1, 1 - par)
                if last < 1:
                    apply(3, i + 2)
                    stats(3, i + 2)
                if not first:
                    rstatsD(i - 1)

            apply(3, 0)
            stats(3, 0)
            z(3, 0)
            lo(3, 0, 0)
            apply(3, 1)
            stats(3, 1)
            stageD(0, 0, first=True)
            with dve.Fori(1, SEQS - 4, 2) as i:
                stageD(i, 1)
                stageD(i + 1, 0)
            stageD(SEQS - 3, 1)
            stageD(SEQS - 2, 0, last=1)
            stageD(SEQS - 1, 1, last=2)
            rstatsD(SEQS - 1)
            with dve.Fori(0, SEQS) as i:
                apply(4, i)

        @block.tensor
        def _(pe):
            def split3(dst, lhs, rhs, start=True, stop=True):
                (lh, ll), (rh, rl) = lhs, rhs
                pe.matmul(dst, lh, rh, start=start, stop=False)
                pe.matmul(dst, lh, rl, start=False, stop=False)
                return pe.matmul(dst, ll, rh, start=False, stop=stop)

            def zT(stage, i, free, value):
                n = stage * SEQS + i
                pe.wait_ge(z_made, (n + 1) * CH)
                pe.wait_ge(lo_made, n)
                if free is not None:
                    pe.wait_ge(free, value)
                for c in range(CH):
                    ins = pe.transpose(bank(5)[:, cols(c)], Z[:, c], ident[:])
                ins.then_inc(zT_made, 1)

            def zt(par, c=None):
                part = slice(0, TOK) if c is None else cols(c)
                return ZT_hi[par][:, part], ZT_lo[par][:, part]

            pe.wait_ge(consts, 5)

            with pe.Fori(0, SEQS) as i:
                zT(0, i, None, None)
                pe.wait_ge(w1_loaded, (i + 1) * 16)
                pe.wait_ge(b1_loaded, (i + 1) * 16)
                pe.wait_ge(weights_loaded, 16 * NLOADS)
                pe.wait_ge(folded, i)
                pe.matmul(bank(1), negavg[:], w1[:], start=True, stop=False)
                pe.matmul(bank(1), avgrow[:], b1r[:], start=False, stop=True).then_inc(fold_made, 1)
                pe.wait_ge(lo_made, i + 1)
                pe.wait_ge(wlo_made, 1)
                for c in range(CH):
                    ins = split3(bank(2)[:, 0:NC].rearrange("p (s c h) -> p s c h", s=SEQS, c=CH)[:, i, c, :], zt(0, c),
                                 (w_in_hi[:, 768:772], w_in_lo[:, 768:772]))
                ins.then_inc(dt_made, 1)
            pe.wait_ge(step_v, 16)
            pe.matmul(bank(3)[:, 0:NC], cumneg[:], sm[:, 7], start=True, stop=True).then_inc(cum_in_psum, 1)
            pe.matmul(bank(4)[:, 0:NC], allneg[:], sm[:, 7], start=True, stop=True).then_inc(cum_in_psum, 1)
            pe.wait_ge(parts_made, 5)
            for q in range(3):
                ins = pe.transpose(bank(6).bitcast(BF16)[:, q * P:(q + 1) * P], cparts[:, q], identb[:])
            ins.then_inc(partsT_in_psum, 1)
            pe.wait_ge(parts_made, 6)
            pe.matmul(bank(6)[:, 0:EXPERTS], negavg[:], wg[:], start=True, stop=True).then_inc(set_t, 1)
            pe.wait_ge(set_v, 6)
            for b, part in ((0, slice(0, 512)), (1, slice(512, 640))):
                dst = bank(b)[:, 0:part.stop - part.start]
                pe.matmul(dst, lnb_avg[:], w4[:, part], start=True, stop=False)
                pe.matmul(dst, avgrow[:], b4r[:, part], start=False, stop=False)
                ins = pe.matmul(dst, negavg[:], w4s[:, part], start=False, stop=True)
            ins.then_inc(set_t, 1)

            PROJ = [(256, 0), (384, 1), (512, 2), (640, 0), (0, 1), (128, 2)]

            def frontA(i):
                free = [(bc_made, i * 2), (gz_made, i * 2), (gz_made, i * 2),
                        (conv_made, i * 6 + 3), (conv_made, i * 6 + 6), (bc_made, i * 2 + 1)]
                for (col, b), (s, v) in zip(PROJ, free):
                    pe.wait_ge(s, v)
                    split3(bank(b), (w_in_hi[:, col:col + P], w_in_lo[:, col:col + P]),
                           (XT_hi[:, i, :], XT_lo[:, i, :])).then_inc(proj_made, 1)

            def chunk_inA(i, c):
                t = i * CH + c
                pe.wait_ge(dtx_made, t)
                pe.wait_ge(btok_made, i * 3 + c)
                for half in range(2):
                    ins = pe.transpose(bank(3)[:, cols(half)], xc[:, half, cols(c)], ident[:])
                if c < CH - 1:
                    ins = pe.transpose(bank(3)[:, INNER:INNER + P], Bf[:, cols(c)], ident[:])
                ins.then_inc(T_made, 1)
                pe.wait_ge(E_made, t)
                pe.matmul(bank(4), identb[:], far4[:].rearrange("p h i -> p (h i)"), start=True, stop=False)
                pe.matmul(bank(4), parts[:, t, :], headrows_neg[:].rearrange("p h i -> p (h i)"), start=False, stop=False)
                for h in range(HEADS):
                    ins = pe.matmul(bank(4)[:, cols(h)], headrows[:, h, :], parts[:, t, :], start=False,
                                    stop=h == HEADS - 1)
                ins.then_inc(D_made, 1)

            def midA(i):
                pe.wait_ge(bc_made, i * 2 + 2)
                pe.wait_ge(xc_made, i * 2 + 2)
                pe.wait_ge(M_made, i * CH)
                pe.wait_ge(yf_made, i * 2)
                for c in range(CH):
                    ins = pe.matmul(bank(5)[:, cols(c)], Bf[:, cols(c)], Cf[:, cols(c)], start=True, stop=True)
                ins.then_inc(G_made, 1)
                chunk_inA(i, 0)
                chunk_inA(i, 1)
                for c in range(CH):
                    t = i * CH + c
                    pe.wait_ge(M_made, t + 1)
                    pe.wait_ge(y_made, t)
                    for h in range(HEADS):
                        ins = pe.matmul(bank(6)[:, h * HD:(h + 1) * HD], Mdec[:, c % 2, h],
                                        dtx[:, c % 2, h * HD:(h + 1) * HD], start=True, stop=True)
                    if c > 0:
                        pe.wait_ge(st_made, i * 3 + c)
                        ins = pe.matmul(bank(6)[:, INNER:2 * INNER], Cf[:, cols(c)], St[:], start=True, stop=True)
                    ins.then_inc(Y_made, 1)
                    if c < CH - 1:
                        pe.wait_ge(wdtx_made, i * 3 + c + 1)
                        pe.wait_ge(btok_made, i * 3 + c + 1)
                        if c == 0:
                            pe.wait_ge(res_made, i)
                        else:
                            pe.wait_ge(st_made, i * 3 + c)
                        pe.matmul(bank(7)[:, 0:INNER], Btok[:], wdtx[:], start=True, stop=True).then_inc(S_made, 1)
                    if c + 2 < CH:
                        chunk_inA(i, c + 2)

            def tailA(i):
                pe.wait_ge(y_made, (i + 1) * CH)
                pe.wait_ge(M_made, (i + 1) * CH)
                for c in range(CH):
                    for half in range(2):
                        ins = pe.transpose(bank(4 + half)[:, cols(c)], ytok[:, c, cols(half)], ident[:])
                ins.then_inc(YT_made, 1)
                pe.wait_ge(yg_made, i * 2 + 2)
                pe.wait_ge(st_made, i * 3 + 3)
                for c in range(CH):
                    for half in range(2):
                        ins = pe.matmul(bank(7)[:, cols(c)], yf[:, half, cols(c)], w_out[:, half],
                                        start=half == 0, stop=half == 1)
                ins.then_inc(out_made, 1)

            pe.wait_ge(zT_stashed, 32 * SEQS)
            pe.wait_ge(set_v, 11)
            frontA(0)
            pe.wait_ge(rows_moved, NROWS)
            pe.wait_ge(fillers, 1)
            pe.wait_ge(step_a, 5)
            with pe.Fori(0, SEQS - 1) as i:
                midA(i)
                frontA(i + 1)
                tailA(i)
            midA(SEQS - 1)
            tailA(SEQS - 1)

            def logitsB(i, par):
                pe.wait_ge(lo_made, SEQS + i + 1)
                pe.wait_ge(gate_v, i * GATE_STEPS)
                for c in range(CH):
                    ins = split3(bank(4)[:, c * EXPERTS:(c + 1) * EXPERTS], zt(par, c), (wg_hi[:], wg_lo[:]))
                ins.then_inc(logits_made, 1)

            def accT_B(t, k):
                pe.wait_ge(acc_made, t + 1)
                pe.wait_ge(accT_made, t)
                for h in range(2):
                    ins = pe.transpose(bank(6)[:, cols(h)], acc[k][:, cols(h)], ident[:])
                ins.then_inc(accT_in_psum, 1)

            def moe_out(t, i, c, guard):
                pe.wait_ge(accT_made, t + 1)
                if c == 0:
                    pe.wait_ge(res_made, SEQS + i)
                for h in range(2):
                    ins = pe.matmul(bank(7)[:, cols(c)], accT[:, h], w_o[:, h], start=h == 0, stop=h == 1)
                ins.then_inc(moe_made, 1)

            def stageB(i, par, first=False, last=False):
                for c in range(CH):
                    t = i * CH + c
                    for e in range(EXPERTS):
                        pe.wait_ge(g_made, t * EXPERTS + e + 1)
                        split3(bank(e % 4), zt(par, c), (w1_hi[:, e], w1_lo[:, e])).then_inc(h_made, 1)
                        if e == 1 and not (first and c < 2):
                            moe_out(t - 2, i if c >= 2 else i - 1, (c + 2) % 4, None)
                        if e == 3 and c == 1 and not last:
                            zT(1, i + 1, None, None)
                        if e == 3 and c == 2 and not last:
                            logitsB(i + 1, 1 - par)
                    if not (first and c == 0):
                        accT_B(t - 1, (c + 1) % 2)

            pe.wait_ge(w1lo_made, SEQS)
            pe.wait_ge(wlo_made, 2)
            zT(1, 0, None, None)
            logitsB(0, 0)
            stageB(0, 0, first=True)
            with pe.Fori(1, SEQS - 2, 2) as i:
                stageB(i, 1)
                stageB(i + 1, 0)
            stageB(SEQS - 1, 1, last=True)
            moe_out(NT - 2, SEQS - 1, 2, None)
            accT_B(NT - 1, 1)
            moe_out(NT - 1, SEQS - 1, 3, None)

            def w4p(a, b):
                return w4_hi[:, a:b], w4_lo[:, a:b]

            def projC(i, par):
                pe.wait_ge(lo_made, 2 * SEQS + i + 1)
                pe.wait_ge(lkt_made, i)
                split3(bank(2), w4p(512, 640), zt(par)).then_inc(cproj_made, 1)
                pe.wait_ge(cact_made, i * 5)
                pe.wait_ge(kvs_made, i * 3)
                for k in range(2):
                    for c in range(2):
                        ins = split3(bank(3 + k)[:, c * HID:(c + 1) * HID], zt(par, 2 * k + c), w4p(0, HID))
                    ins.then_inc(cproj_made, 1)
                for half in range(2):
                    split3(bank(half), w4p(HID + P * half, HID + P * half + P), zt(par)).then_inc(cproj_made, 1)

            def stageC(i, par, last=0):
                pe.wait_ge(var_made, i * 4 + 4)
                pe.wait_ge(og_made, i * 2)
                for c in range(CH):
                    ins = pe.matmul(bank(6)[:, cols(c)], qv[:, 2, cols(c)], qv[:, 0, cols(c)], start=True, stop=True)
                ins.then_inc(s1_made, 1)
                for c in range(CH):
                    ins = pe.matmul(bank(7)[:, cols(c)], qv[:, 3, cols(c)], qv[:, 1, cols(c)], start=True, stop=True)
                ins.then_inc(s2_made, 1)
                for c in range(CH):
                    ins = pe.transpose(bank(2)[:, cols(c)], qv[:, 3, cols(c)], ident[:])
                ins.then_inc(lkT_made, 1)
                pe.wait_ge(lkt_made, i + 1)
                pe.wait_ge(cact_made, i * 5 + 3)
                for c in range(3):
                    if c > 0:
                        pe.wait_ge(kvs_made, i * 3 + c)
                    pe.matmul(bank(3)[:, 0:HID], lkt[:, c], vt[:, c], start=c == 0, stop=True, skip_group_check=True)\
                      .then_inc(kv_made, 1)
                if last < 1:
                    zT(2, i + 2, res_made, 2 * SEQS + i)
                if last < 2:
                    projC(i + 1, 1 - par)
                pe.wait_ge(att_made, i * 4 + 4)
                pe.wait_ge(kvs_made, i * 3 + 3)
                for half in range(2):
                    for c in range(CH):
                        dst = bank(6 + half)[:, cols(c)]
                        ins = pe.matmul(dst, vt[:, c, cols(half)], at[:, 0, cols(c)], start=True, stop=c == 0)
                        if c > 0:
                            ins = pe.matmul(dst, kvs[:, c - 1, cols(half)], qv[:, 1, cols(c)], start=False, stop=True)
                    ins.then_inc(o_made, 1)
                pe.wait_ge(og_made, i * 2 + 2)
                pe.wait_ge(lo_made, 2 * SEQS + (i + 3 if last < 1 else SEQS))
                pe.wait_ge(res_made, 2 * SEQS + i)
                for c in range(CH):
                    for half in range(2):
                        ins = pe.matmul(bank(5)[:, cols(c)], og[:, half, cols(c)], w_att[:, half],
                                        start=half == 0, stop=half == 1)
                ins.then_inc(cout_made, 1)

            pe.wait_ge(wlo_made, 4)
            zT(2, 0, None, None)
            zT(2, 1, None, None)
            projC(0, 0)
            with pe.Fori(0, SEQS - 3, 2) as i:
                stageC(i, 0)
                stageC(i + 1, 1)
            stageC(SEQS - 2, 0, 1)
            stageC(SEQS - 1, 1, 2)

            def down(i, par):
                pe.wait_ge(hf_made, (i + 1) * 3 + DCREDIT)
                pe.wait_ge(resD_made, i)
                for c in range(CH):
                    for m in range(3):
                        ins = pe.matmul(bank(7)[:, cols(c)], hf[par][:, m, cols(c)], wdn[:, m], start=m == 0, stop=m == 2)
                ins.then_inc(dn_made, 1)

            def stageD(i, par, first=False, last=False):
                pe.wait_ge(lo_made, 3 * SEQS + i + 1)
                for m in range(3):
                    pe.wait_ge(hf_made, i * 3 + m + 1)
                    for b, col in ((m, m * P), ((3, 4, 6)[m], FFN + m * P)):
                        ins = split3(bank(b), (wff_hi[:, col:col + P], wff_lo[:, col:col + P]), zt(par))
                    ins.then_inc(gu_made, 1)
                    if m == 0 and not last:
                        zT(3, i + 1, None, None)
                if not first:
                    down(i - 1, 1 - par)

            zT(3, 0, res_made, 3 * SEQS)
            stageD(0, 0, first=True)
            with pe.Fori(1, SEQS - 2, 2) as i:
                stageD(i, 1)
                stageD(i + 1, 0)
            stageD(SEQS - 1, 1, last=True)
            down(SEQS - 1, 1)


_INS = ["x", "norm_w", "in_wT", "conv_w", "conv_b", "A_log", "D", "dt_bias", "out_wT", "WgT", "W1T", "b1", "WoT", "bo",
        "ln_w", "ln_b", "Wh", "bh", "Wqk", "bqk", "qk_w", "qk_b", "rel", "Wout", "bout", "wgT", "wuT", "wdT"]


def kernel(L0_attn_x, L0_attn_norm_w, L0_attn_in_proj_w, L0_attn_conv_w, L0_attn_conv_b, L0_attn_A_log, L0_attn_D,
           L0_attn_dt_bias, L0_attn_out_proj_w, L0_ffn_Wg, L0_ffn_W1, L0_ffn_b1, L0_ffn_Wo, L0_ffn_bo, L1_attn_ln_w,
           L1_attn_ln_b, L1_attn_Wh, L1_attn_bh, L1_attn_Wqk, L1_attn_bqk, L1_attn_qk_w, L1_attn_qk_b,
           L1_attn_rel_table, L1_attn_Wout, L1_attn_bout, L1_ffn_w_gate, L1_ffn_w_up, L1_ffn_w_down):
    import numpy as np
    import concourse.bacc as bacc
    from concourse.bass_utils import run_bass_kernel_spmd

    def row(a):
        return np.asarray(a).reshape(1, -1)

    def col(a):
        return np.asarray(a).reshape(-1, 1)

    def T(a):
        return np.asarray(a).T

    arrays = dict(
        x=L0_attn_x, norm_w=col(L0_attn_norm_w), in_wT=T(L0_attn_in_proj_w),
        conv_w=np.asarray(L0_attn_conv_w).reshape(2, P, 4).transpose(1, 0, 2),
        conv_b=np.asarray(L0_attn_conv_b).reshape(2, P).T, A_log=row(L0_attn_A_log), D=row(L0_attn_D),
        dt_bias=row(L0_attn_dt_bias), out_wT=T(L0_attn_out_proj_w), WgT=T(L0_ffn_Wg),
        W1T=np.asarray(L0_ffn_W1).transpose(0, 2, 1), b1=np.asarray(L0_ffn_b1).reshape(1, EXPERTS, 2 * HID),
        WoT=T(L0_ffn_Wo), bo=row(L0_ffn_bo), ln_w=col(L1_attn_ln_w), ln_b=col(L1_attn_ln_b), Wh=L1_attn_Wh,
        bh=row(L1_attn_bh), Wqk=L1_attn_Wqk, bqk=row(L1_attn_bqk), qk_w=T(L1_attn_qk_w), qk_b=T(L1_attn_qk_b),
        rel=row(L1_attn_rel_table), Wout=L1_attn_Wout, bout=row(L1_attn_bout), wgT=T(L1_ffn_w_gate),
        wuT=T(L1_ffn_w_up), wdT=T(L1_ffn_w_down))
    nc = bacc.Bacc("TRN2", target_bir_lowering=False, num_devices=1)
    in_map, args = {}, []
    for name in _INS:
        a = np.ascontiguousarray(arrays[name])
        in_map[f"in_{name}"] = a
        args.append(nc.dram_tensor(f"in_{name}", a.shape, mybir.dt.from_np(a.dtype), kind="ExternalInput").ap())
    out = nc.dram_tensor("out", (SEQS, TOK, P), F32, kind="ExternalOutput").ap()
    build(nc, *args, out)
    return run_bass_kernel_spmd(nc, [in_map], core_ids=[0]).results[0]["out"]
```

```python
import concourse.bass as bass
from concourse import mybir
from contextlib import ExitStack

ALU = mybir.AluOpType
ACT = mybir.ActivationFunctionType
AX = mybir.AxisListType
F32 = mybir.dt.float32
F32R = mybir.dt.float32r
BF16 = mybir.dt.bfloat16
I32 = mybir.dt.int32
U32 = mybir.dt.uint32

P = 128
SEQS, TOK = 8, 512
CH = TOK // P
NT = SEQS * CH
HEADS, HD = 4, 64
INNER = HEADS * HD
EXPERTS, HID = 8, 256
GROUP = 32
FFN = 384
LN_EPS, RMS_EPS, TOP_EPS = 1e-5, 1e-6, 1e-9
FAR = -1e30


GATE_AT = (0, 1, 5, 11, 12, 14, 15, 16, 17, 19)
GATE_STEPS = 25


def t5_buckets():
    import math
    return [n if n < 16 else min(31, 16 + int(math.log(n / 16) / math.log(8) * 16)) for n in range(GROUP)]


BUCKETS = t5_buckets()


def build(nc, x_in, norm_w, in_wT, conv_w, conv_b, A_log, D_skip, dt_bias, out_wT, WgT, W1T, b1, WoT, bo,
          ln_w, ln_b, Wh, bh, Wqk, bqk, qk_w, qk_b, rel, Wout, bout, wgT, wuT, wdT, out):
    ctx = ExitStack()
    with ctx:
        def sb(name, shape, dt=F32):
            return ctx.enter_context(nc.sbuf_tensor(name, shape, dt))

        def sem(name):
            return ctx.enter_context(nc.semaphore(name))

        X = sb("X", [P, SEQS, CH, P])
        RES = sb("RES", [P, SEQS, CH, P])
        res_shift = sb("res_shift", [P, SEQS, CH])
        res_rstd = sb("res_rstd", [P, SEQS, CH])
        ps = ctx.enter_context(nc.psum_tensor("ps", [P, 8, 512], F32))

        def bank(b):
            return ps[:, b, :]

        ident = sb("ident", [P, P])
        identb = sb("identb", [P, P], BF16)
        negavg = sb("negavg", [P, P])
        avgrow = sb("avgrow", [1, P])
        cumneg = sb("cumneg", [P, P])
        allneg = sb("allneg", [P, P])
        far4 = sb("far4", [P, HEADS, P], BF16)
        mhalf = sb("mhalf", [P, 2, CH])
        iota8 = sb("iota8", [P, EXPERTS])
        iota8i = sb("iota8i", [P, EXPERTS], I32)
        near = sb("near", [P, P])
        before = sb("before", [P, P])

        w_in = sb("w_in", [P, 772])
        w_in_hi = sb("w_in_hi", [P, 772], F32R)
        w_in_lo = sb("w_in_lo", [P, 772], F32R)
        normw = sb("normw", [P, 1])
        convw = sb("convw", [P, 2, 4])
        convb = sb("convb", [P, 2])
        dskip = sb("dskip", [P, 2])
        alog = sb("alog", [P, HEADS])
        dtb = sb("dtb", [P, HEADS])
        w_out = sb("w_out", [P, 2, P])
        w1 = RES[:].rearrange("p s c d -> p s (c d)")
        w1_hi = sb("w1_hi", [P, EXPERTS, 512], F32R)
        w1_lo = sb("w1_lo", [P, EXPERTS, 512], F32R)
        wg = sb("wg", [P, EXPERTS])
        wg_hi = sb("wg_hi", [P, EXPERTS], F32R)
        wg_lo = sb("wg_lo", [P, EXPERTS], F32R)
        w_o = sb("w_o", [P, 2, P])
        bo_rows = sb("bo_rows", [P, P])
        w4 = sb("w4", [P, 640])
        w4s = sb("w4s", [P, 640])
        w4_hi = sb("w4_hi", [P, 640], F32R)
        w4_lo = sb("w4_lo", [P, 640], F32R)
        b4r = sb("b4r", [1, 640])
        lnw = sb("lnw", [P, 1])
        lnb = sb("lnb", [P, 1])
        lnb_avg = sb("lnb_avg", [P, P])
        qkw = sb("qkw", [P, 4])
        qkb = sb("qkb", [P, 4])
        w_att = sb("w_att", [P, 2, P])
        bout_rows = sb("bout_rows", [P, P])
        table = sb("table", [GROUP, 32])
        shifted = sb("shifted", [GROUP, 65])
        wff = sb("wff", [P, 2 * FFN])
        wff_i = wff[:].bitcast(I32)
        wff_hi = sb("wff_hi", [P, 2 * FFN], F32R)
        wff_lo = sb("wff_lo", [P, 2 * FFN], F32R)
        wdn = sb("wdn", [P, 3, P])
        wdn_i = wdn[:].bitcast(I32)

        ZT_hi = [sb(f"ZT_hi{k}", [P, TOK], F32R) for k in range(2)]
        ZT_lo = [sb(f"ZT_lo{k}", [P, TOK], F32R) for k in range(2)]
        Z = sb("Z", [P, CH, P])
        add = sb("add", [P, CH, P])
        stats_t = sb("stats_t", [P, CH, 6])
        mv = sb("mv", [P, CH, 2])
        vars_t = sb("vars_t", [P, 2, CH])
        rstds = sb("rstds", [P, 2, CH])
        negmean = sb("negmean", [P, CH])
        prod = sb("prod", [P, CH])
        shift = sb("shift", [P, CH])
        credit = sb("credit", [1, 2])
        z1 = sb("z1", [P, CH, P])
        rstats_t = sb("rstats_t", [P, CH, 6])
        rmv = sb("rmv", [P, CH, 2])
        rvar = sb("rvar", [P, CH])
        rnegmean = sb("rnegmean", [P, CH])

        scratch = nc.dram_tensor("rel_scratch", [GROUP * 65], F32, kind="Internal").ap()

        early = ExitStack()

        def sb(name, shape, dt=F32):
            return early.enter_context(nc.sbuf_tensor(name, shape, dt))

        x_shift = sb("x_shift", [P, SEQS, CH])
        x_rstd = sb("x_rstd", [P, SEQS, CH])
        XT_hi = sb("XT_hi", [P, SEQS, TOK], F32R)
        XT_lo = sb("XT_lo", [P, SEQS, TOK], F32R)
        NC = NT * HEADS
        cpartsT = sb("cpartsT", [P, 3, P], BF16)
        dt_t, ecum_t, etail_t, dec_t = (sb(n, [P, SEQS, CH, HEADS]) for n in ("dt_t", "ecum_t", "etail_t", "dec_t"))
        expA = sb("expA", [P, HEADS])
        parts = sb("parts", [P, NT, P], BF16)
        headrows = sb("headrows", [P, HEADS, P], BF16)
        headrows_neg = sb("headrows_neg", [P, HEADS, P], BF16)
        work = sb("work", [P, 8, TOK])
        b1r = work[0:1]
        u = work[:, 0:2]
        xc = [work[:, 2:4], work[:, 4:6]]
        gz = [work[:, 6:8], sb("gz1", [P, 2, TOK])[:]]
        Bf = sb("Bf", [P, TOK])
        Cf = sb("Cf", [P, TOK])
        St = sb("St", [P, INNER])
        Sd = sb("Sd", [P, INNER])
        tails = sb("tails", [P, 8, P])
        ytok = tails[:, 0:4].rearrange("p (k c) d -> p k (c d)", k=2)
        yf = tails[:, 4:8].rearrange("p (k c) d -> p k c d", k=2)
        sm = tails
        assert NC == P

        dtx = sb("dtx", [P, 2, INNER])
        wdtx = sb("wdtx", [P, INNER])
        cparts = wdtx[:, 0:3 * NC // 2].bitcast(BF16).rearrange("p (q n) -> p q n", q=3)
        Btok = sb("Btok", [P, P])
        Edec = sb("Edec", [P, 2, HEADS, P])
        Mdec = Edec

        early.close()

        def sb(name, shape, dt=F32):
            return ctx.enter_context(nc.sbuf_tensor(name, shape, dt))

        lg = sb("lg", [P, CH, EXPERTS])
        top = sb("top", [P, CH, 8])
        topi = sb("topi", [P, CH, 8], U32)
        topf = sb("topf", [P, CH, 2])
        ge = sb("ge", [P, 4, CH, EXPERTS + 1])
        gs = sb("gs", [P, 6, CH])
        pick = sb("pick", [P, 2, CH, EXPERTS])
        comb = [sb(f"comb{k}", [P, CH, EXPERTS]) for k in range(2)]
        csum = [sb(f"csum{k}", [P, CH]) for k in range(2)]
        sig = sb("sig", [P, 4, HID])
        gb = sb("gb", [P, 2, EXPERTS, HID])
        acc = [sb(f"acc{k}", [P, HID]) for k in range(2)]
        accT = sb("accT", [P, 2, P])

        qkf = sb("qkf", [P, TOK])
        qv = sb("qv", [P, 4, TOK])
        vt = sb("vt", [P, CH, HID])
        gt = sb("gt", [P, 2, TOK])
        lkt = sb("lkt", [P, CH, P])
        at = sb("at", [P, 2, TOK])
        kvs = sb("kvs", [P, 3, HID])
        og = sb("og", [P, 2, TOK])

        sg = sb("sg", [P, 3, TOK])
        hf = [sb(f"hf{k}", [P, 3, TOK]) for k in range(2)]

        x_loaded, w1_loaded, weights_loaded, rel_written, rel_loaded = (
            sem(n) for n in ("x_loaded", "w1_loaded", "weights_loaded", "rel_written", "rel_loaded"))
        consts, zeroed, fillers = sem("consts"), sem("zeroed"), sem("fillers")
        set_v, set_t, set_a, set_g = sem("set_v"), sem("set_t"), sem("set_a"), sem("set_g")
        rows_moved, out_stored = sem("rows_moved"), sem("out_stored")
        zT_stashed = [sem(f"zT_stashed{k}") for k in range(2)]
        add_made, x_new, stats_made, mv_made, scale_made, z_made = (
            sem(n) for n in ("add_made", "x_new", "stats_made", "mv_made", "scale_made", "z_made"))
        zT_made, hi_made, lo_made = sem("zT_made"), sem("hi_made"), sem("lo_made")
        pool_step = sem("pool_step")
        res_made, rstats_made, rmv_made, rrstd_made = (
            sem(n) for n in ("res_made", "rstats_made", "rmv_made", "rrstd_made"))
        fold_made, folded, w1hi_made, w1lo_made, dt_made = (
            sem(n) for n in ("fold_made", "folded", "w1hi_made", "w1lo_made", "dt_made"))
        step_v, step_a = sem("step_v"), sem("step_a")
        expA_made, cum_in_psum, cum_copied, parts_made, partsT_in_psum, shifted_made, wlo_made, resD_made = (
            sem(n) for n in ("expA_made", "cum_in_psum", "cum_copied", "parts_made", "partsT_in_psum", "shifted_made",
                             "wlo_made", "resD_made"))
        xs_made = sem("xs_made")
        early_loaded, waited, resA_made, fill_v = sem("early_loaded"), sem("waited"), sem("resA_made"), sem("fill_v")
        proj_made, tap_made, conv_made, bc_made, th_made, xc_made, tz_made, gz_made = (
            sem("A_" + n) for n in ("proj", "tap", "conv", "bc", "th", "xc", "tz", "gz"))
        G_made, T_made, D_made, E_made, M_made, dtx_made, btok_made, wdtx_made = (
            sem("A_" + n) for n in ("G", "T", "D", "E", "M", "dtx", "btok", "wdtx"))
        Y_made, y1_made, y_made, S_made, sd_made, st_made, YT_made, yf_made, yg_made, out_made, z1_made = (
            sem("A_" + n) for n in ("Y", "y1", "y", "S", "sd", "st", "YT", "yf", "yg", "out", "z1"))
        h_made, sig_made, g_made, half_made, acc_made, accT_in_psum, accT_made, moe_made = (
            sem("B_" + n) for n in ("h", "sig", "g", "half", "acc", "accTp", "accT", "moe"))
        logits_made, gate_v, gate_a = sem("B_logits"), sem("B_gate_v"), sem("B_gate_a")
        cproj_made, cact_made, var_made, s1_made, s2_made, lkT_made, lkt_made, att_made = (
            sem("C_" + n) for n in ("proj", "act", "var", "s1", "s2", "lkT", "lkt", "att"))
        kv_made, kvs_made, o_made, og_made, cout_made, cz_made, czb_made = (
            sem("C_" + n) for n in ("kv", "kvs", "o", "og", "out", "cz", "czb"))
        gu_made, sg_made, hf_made, dn_made = (
            sem("D_" + n) for n in ("gu", "sg", "hf", "dn"))

        block = ctx.enter_context(nc.Block())

        def cols(c):
            return slice(c * P, (c + 1) * P)

        NEARLY, NLOADS = 5, 24
        BCREDIT = 4
        DCREDIT = 3

        def wait_apart(engine, semaphore, value):
            engine.wait_ge(semaphore, value).then_inc(waited, 1)

        @block.sync
        def _(sp):
            def x_pair(j):
                sp.dma_start(X[:].rearrange("p (j two) c d -> p j (two c) d", two=2)[:, j],
                             x_pairs[j].rearrange("(c p) d -> p c d", p=P)).then_inc(x_loaded, 16)

            def w1_pair(j):
                sp.dma_start(w1.rearrange("p (j two) n -> p j two n", two=2)[:, j], w1_pairs[j].rearrange("e p n -> p e n")).then_inc(w1_loaded, 16)

            def stash(i, par):
                sp.wait_ge(hi_made, i + 1)
                sp.dma_start(XT_hi[:, i, :].bitcast(F32), ZT_hi[par][:].bitcast(F32)).then_inc(zT_stashed[par], 16)
                wait_apart(sp, lo_made, i + 1)
                sp.dma_start(XT_lo[:, i, :].bitcast(F32), ZT_lo[par][:].bitcast(F32)).then_inc(zT_stashed[par], 16)

            x_pairs = x_in.rearrange("(j two) t d -> j (two t) d", two=2)
            w1_pairs = W1T.rearrange("(j two) p n -> j two p n", two=2)
            x_pair(0)
            for dst, src in ((normw[:], norm_w), (w_in[:], in_wT), (b1r.rearrange("p e n -> p (e n)"), b1),
                             (alog[:], A_log.to_broadcast([P, HEADS])), (dtb[:], dt_bias.to_broadcast([P, HEADS]))):
                sp.dma_start(dst, src).then_inc(early_loaded, 16)
            w1_pair(0)
            with sp.Fori(0, SEQS // 2 - 1) as j:
                wait_apart(sp, x_loaded, (j + 1) * 16)
                x_pair(j + 1)
                wait_apart(sp, w1_loaded, (j + 1) * 16)
                w1_pair(j + 1)
                for par in range(2):
                    stash(2 * j + par, par)
            for par in range(2):
                stash(SEQS - 2 + par, par)
            sp.wait_ge(fillers, 1)
            sp.wait_ge(parts_made, 6)
            for head in range(HEADS):
                for q in range(3):
                    sp.dma_start(parts[3 * head + q:3 * head + q + 1, :, :], cpartsT[head:P:HEADS, q, :])\
                      .then_inc(rows_moved, 16)
            sp.wait_ge(shifted_made, 2 + len(set(BUCKETS[16:])))
            sp.dma_start(scratch.rearrange("(p n) -> p n", n=65), shifted[:]).then_inc(rel_written, 16)
            sp.wait_ge(rel_written, 16)
            sp.wait_ge(fillers, 1)
            for g in range(P // GROUP):
                sp.dma_start(near[GROUP * g:GROUP * (g + 1), GROUP * g:GROUP * (g + 1)],
                             scratch[0:GROUP * 64].rearrange("(p n) -> p n", n=64)[:, 0:GROUP])\
                  .then_inc(rel_loaded, 16)
            with sp.Fori(0, SEQS) as i:
                sp.wait_ge(x_new, 3 * SEQS + i + 1)
                sp.dma_start(out[i].rearrange("(c p) d -> p c d", p=P), X[:, i]).then_inc(out_stored, 16)
            sp.wait_ge(out_stored, 16 * SEQS)

        NROWS = 16 * 3 * HEADS

        STEPS, STEPS_RES = (4, 4, 5, 3), 3

        @block.gpsimd
        def _(pool):
            pool.memset(ident[:], 0.0).then_inc(set_g, 1)
            pool.memset(negavg[:], -1.0 / P).then_inc(set_g, 1)
            pool.memset(avgrow[:], 1.0 / P).then_inc(set_g, 1)
            pool.memset(mhalf[:], -0.5).then_inc(set_g, 1)
            pool.memset(allneg[:], -1.0).then_inc(set_g, 1)
            pool.wait_ge(set_g, 5)
            pool.affine_select(out=ident[:], in_=ident[:], compare_op=ALU.not_equal, fill=1.0, base=0,
                               pattern=[[-1, P]], channel_multiplier=1).then_inc(consts, 1)
            pool.affine_select(out=cumneg[:], in_=allneg[:], compare_op=ALU.is_ge, fill=0.0, base=0,
                               pattern=[[1, P]], channel_multiplier=-1).then_inc(consts, 1)
            pool.iota(iota8i[:], pattern=[[1, EXPERTS]], base=0, channel_multiplier=0).then_inc(consts, 1)
            pool.wait_ge(consts, 3)
            pool.tensor_copy(iota8[:], iota8i[:]).then_inc(consts, 1)
            pool.tensor_copy(identb[:], ident[:]).then_inc(consts, 1)

            def scales(stage, i, done):
                n = stage * SEQS + i
                twice = stage in (0, 2)
                k = 2 if twice else 1
                wait_apart(pool, mv_made, (n + 1) * CH)
                wait_apart(pool, scale_made, n)
                if twice:
                    wait_apart(pool, xs_made, 2 * (i if stage == 0 else SEQS + i))
                m, v = mv[:, :, 0], mv[:, :, 1]
                pool.tensor_scalar(negmean[:], m, -1.0, None, ALU.mult).then_inc(pool_step, 1)
                pool.tensor_scalar(vars_t[:, 0], v, LN_EPS, None, ALU.add).then_inc(pool_step, 1)
                if twice:
                    eps2 = RMS_EPS if stage == 0 else LN_EPS
                    pool.tensor_scalar(vars_t[:, 1], v, 1.0 + eps2, LN_EPS * eps2, ALU.mult, ALU.add)\
                        .then_inc(pool_step, 1)
                pool.wait_ge(pool_step, done + k + 1)
                pool.wait_ge(z_made, n * CH)
                pool.tensor_tensor(rstds[:, 0:k], vars_t[:, 0:k], mhalf[:, 0:k], ALU.pow).then_inc(pool_step, 1)
                done = done + k + 2
                pool.wait_ge(pool_step, done)
                if stage in (0, 3):
                    pool.tensor_tensor(shift[:], negmean[:], rstds[:, k - 1], ALU.mult).then_inc(scale_made, 1)
                else:
                    pool.tensor_tensor(prod[:], negmean[:], rstds[:, k - 1], ALU.mult).then_inc(pool_step, 1)
                    done = done + 1
                    wait_apart(pool, pool_step, done)
                    pool.tensor_scalar(shift[:], prod[:], 1.0, None, ALU.add).then_inc(scale_made, 1)
                if twice:
                    pool.tensor_copy(x_rstd[:, i, :], rstds[:, 0]).then_inc(xs_made, 1)
                    pool.tensor_tensor(x_shift[:, i, :], negmean[:], rstds[:, 0], ALU.mult).then_inc(xs_made, 1)
                return done

            def res_scales(stage, i, done):
                n = (stage - 1) * SEQS + i
                wait_apart(pool, rmv_made, (n + 1) * CH)
                wait_apart(pool, rrstd_made, n)
                pool.tensor_scalar(rnegmean[:], rmv[:, :, 0], -1.0, None, ALU.mult).then_inc(pool_step, 1)
                pool.tensor_scalar(rvar[:], rmv[:, :, 1], LN_EPS, None, ALU.add).then_inc(pool_step, 1)
                wait_apart(pool, pool_step, done + 2)
                pool.tensor_tensor(res_rstd[:, i, :], rvar[:], mhalf[:, 0], ALU.pow).then_inc(pool_step, 1)
                wait_apart(pool, pool_step, done + 3)
                pool.tensor_tensor(res_shift[:, i, :], rnegmean[:], res_rstd[:, i, :], ALU.mult).then_inc(rrstd_made, 1)
                return done + STEPS_RES

            done = scales(0, 0, 0)
            pool.wait_ge(set_a, 1)
            pool.tensor_tensor(w_in_lo[:], w_in[:], w_in_hi[:].bitcast(F32), ALU.subtract).then_inc(wlo_made, 1)
            with pool.Fori(1, SEQS) as i:
                scales(0, i, i * STEPS[0])
            done = SEQS * STEPS[0]

            pool.memset(parts[:].bitcast(F32), 0.0).then_inc(set_g, 1)
            pool.memset(headrows[:], 1.0).then_inc(set_g, 1)
            pool.memset(far4[:], 0.0).then_inc(set_g, 1)
            pool.wait_ge(set_g, 8)
            pool.affine_select(out=headrows[:], in_=headrows[:], compare_op=ALU.is_ge, fill=0.0, base=0,
                               pattern=[[-3, HEADS], [0, P]], channel_multiplier=1).then_inc(set_g, 1)
            pool.affine_select(out=far4[:], in_=far4[:], compare_op=ALU.is_ge, fill=FAR, base=0,
                               pattern=[[0, HEADS], [1, P]], channel_multiplier=-1).then_inc(set_g, 1)
            pool.wait_ge(set_g, 10)
            pool.affine_select(out=headrows[:], in_=headrows[:], compare_op=ALU.is_ge, fill=0.0, base=2,
                               pattern=[[3, HEADS], [0, P]], channel_multiplier=-1).then_inc(set_g, 1)
            pool.wait_ge(set_g, 11)
            pool.tensor_scalar(headrows_neg[:], headrows[:], -1.0, None, ALU.mult).then_inc(set_g, 1)
            pool.wait_ge(set_g, 12)
            pool.memset(near[:], FAR).then_inc(fillers, 1)
            pool.memset(before[:], 1.0 / GROUP).then_inc(fillers, 1)
            pool.wait_ge(fillers, 2)
            for g in range(P // GROUP):
                pool.memset(before[GROUP * g:GROUP * (g + 1), 0:GROUP * (g + 1)], 0.0).then_inc(fillers, 1)
            pool.wait_ge(fillers, 2 + P // GROUP)
            for n, (lo, w, hi) in enumerate(((wg_lo, wg, wg_hi), (w4_lo, w4s, w4_hi), (wff_lo, wff, wff_hi))):
                pool.wait_ge(set_a, n + 2)
                pool.tensor_tensor(lo[:], w[:], hi[:].bitcast(F32), ALU.subtract).then_inc(wlo_made, 1)
            pool.wait_ge(rel_loaded, 16 * (P // GROUP))
            pool.affine_select(out=near[:], in_=near[:], compare_op=ALU.is_ge, fill=FAR, base=0,
                               pattern=[[1, P]], channel_multiplier=-1).then_inc(fillers, 1)

            def decayedA(i, c):
                pool.wait_ge(dtx_made, i * CH + c + 1)
                pool.wait_ge(S_made, i * 3 + c)
                pool.tensor_tensor(wdtx[:].rearrange("p (h d) -> p h d", h=HEADS),
                                   dtx[:, c % 2].rearrange("p (h d) -> p h d", h=HEADS),
                                   etail_t[:, i, c, :].unsqueeze(2).to_broadcast([P, HEADS, HD]), ALU.mult)\
                    .then_inc(wdtx_made, 1)

            def stepA(i, c, par, done, first=False, last=False):
                if c + 1 < CH - 1:
                    decayedA(i, c + 1)
                    pool.wait_ge(st_made, i * 3 + c + 1)
                    pool.tensor_tensor(Sd[:].rearrange("p (h d) -> p h d", h=HEADS),
                                       St[:].rearrange("p (h d) -> p h d", h=HEADS),
                                       dec_t[:, i, c + 1, :].unsqueeze(2).to_broadcast([P, HEADS, HD]), ALU.mult)\
                        .then_inc(sd_made, 1)
                elif c == CH - 1 and not last:
                    decayedA(i + 1, 0)
                if not (first and c == 0):
                    gateA(i * CH + c - 1, (c + 3) % CH, par if c > 0 else 1 - par)
                if c == 1 and not first:
                    done = res_scales(1, i - 1, done)
                return done

            def gateA(t, c, par):
                pool.wait_ge(yf_made, 2 * t + 2)
                pool.tensor_tensor(yf[:, c % 2], yf[:, c % 2], gz[par][:, :, cols(c)], ALU.mult).then_inc(yg_made, 1)

            def stageA(i, par, done, first=False, last=False):
                for c in range(CH):
                    done = stepA(i, c, par, done, first, last)
                return done

            decayedA(0, 0)
            done = stageA(0, 0, done, first=True)
            with pool.Fori(1, SEQS - 2, 2) as i:
                stageA(i, 1, done + (i - 1) * STEPS_RES)
                stageA(i + 1, 0, done + i * STEPS_RES)
            done += (SEQS - 2) * STEPS_RES
            done = stageA(SEQS - 1, 1, done, last=True)
            gateA(NT - 1, CH - 1, 1)
            done = res_scales(1, SEQS - 1, done)

            def stageB(i, par, done, first=False, last=False):
                if not last:
                    done = scales(1, i + 1, done)
                for c in range(CH):
                    t = i * CH + c
                    pool.wait_ge(g_made, t * EXPERTS + 4 + BCREDIT)
                    b = gb[:, c % 2]
                    pool.tensor_tensor(b[:, 0:2], b[:, 0:2], b[:, 2:4], ALU.add).then_inc(half_made, 1)
                    pool.wait_ge(g_made, t * EXPERTS + 8 + BCREDIT)
                    pool.tensor_tensor(b[:, 4:6], b[:, 4:6], b[:, 6:8], ALU.add).then_inc(half_made, 1)
                    pool.wait_ge(half_made, t * 3 + 2)
                    pool.tensor_tensor(b[:, 0:2], b[:, 0:2], b[:, 4:6], ALU.add).then_inc(half_made, 1)
                    if c == 2 and not first:
                        done = res_scales(2, i - 1, done)
                return done

            done = scales(1, 0, done)
            done = stageB(0, 0, done, first=True)
            both = STEPS[1] + STEPS_RES
            with pool.Fori(1, SEQS - 2, 2) as i:
                for par in (1, 0):
                    k = 1 - par
                    stageB(i + k, par, done + (i - 1 + k) * both)
            done += (SEQS - 2) * both
            done = stageB(SEQS - 1, 1, done, last=True)
            done = res_scales(2, SEQS - 1, done)

            def stageC(i, done, last=0):
                if last < 1:
                    done = scales(2, i + 2, done)
                pool.wait_ge(cz_made, (i + 1) * CH)
                pool.tensor_tensor(z1[:], z1[:], bout_rows[:].unsqueeze(1).to_broadcast([P, CH, P]), ALU.add)\
                    .then_inc(czb_made, 1)
                return res_scales(3, i, done)

            done = scales(2, 0, done)
            done = scales(2, 1, done)
            both = STEPS[2] + STEPS_RES
            with pool.Fori(0, SEQS - 2) as i:
                stageC(i, done + i * both)
            done += (SEQS - 2) * both
            done = stageC(SEQS - 2, done, 1)
            done = stageC(SEQS - 1, done, 2)

            def stageD(i, done, first=False, last=0):
                if last < 1:
                    done = scales(3, i + 2, done)
                if not first:
                    done = res_scales(4, i - 1, done)
                return done

            done = scales(3, 0, done)
            done = scales(3, 1, done)
            both = STEPS[3] + STEPS_RES
            done = stageD(0, done, first=True)
            with pool.Fori(1, SEQS - 2) as i:
                stageD(i, done + (i - 1) * both)
            done += (SEQS - 3) * both
            done = stageD(SEQS - 2, done, last=1)
            done = stageD(SEQS - 1, done, last=2)
            res_scales(4, SEQS - 1, done)

        @block.scalar
        def _(act):
            def hi(stage, i, par, free, value):
                act.wait_ge(zT_made, stage * SEQS + i + 1)
                if free is not None:
                    act.wait_ge(free, value)
                act.activation(ZT_hi[par][:], bank(5), ACT.Copy).then_inc(hi_made, 1)

            def z(stage, i):
                n = stage * SEQS + i
                wait_apart(act, scale_made, n + 1)
                wait_apart(act, zT_made, n)
                k = 1 if stage in (0, 2) else 0
                for c in range(CH):
                    act.activation(Z[:, c], X[:, i, c], ACT.Identity, bias=shift[:, c:c + 1],
                                   scale=rstds[:, k, c:c + 1]).then_inc(z_made, 1)

            def residual(stage, i):
                n = (stage - 1) * SEQS + i
                wait_apart(act, rrstd_made, n + 1)
                wait_apart(act, x_new, n)
                for c in range(CH):
                    act.activation(add[:, c], RES[:, i, c], ACT.Identity, bias=res_shift[:, i, c:c + 1],
                                   scale=res_rstd[:, i, c:c + 1]).then_inc(add_made, 1)

            def input_z(i, c, made):
                act.activation(z1[:, c], X[:, i, c], ACT.Identity, bias=x_shift[:, i, c:c + 1],
                               scale=x_rstd[:, i, c:c + 1]).then_inc(made, 1)

            loads = [
                (convw[:], conv_w), (convb[:], conv_b),
                (w_out[:], out_wT.rearrange("(k p) n -> p k n", p=P)), (wg[:], WgT),
                (w_o[:], WoT.rearrange("(k p) n -> p k n", p=P)),
                (bo_rows[:], bo.to_broadcast([P, P])), (bout_rows[:], bout.to_broadcast([P, P])),
                (table[:], rel.to_broadcast([GROUP, 32])),
                (w4[:, 0:512], Wh), (w4[:, 512:640], Wqk), (b4r[:, 0:512], bh), (b4r[:, 512:640], bqk),
                (lnw[:], ln_w), (lnb[:], ln_b), (qkw[:], qk_w), (qkb[:], qk_b),
                (wff_i[:, 0:FFN], wgT), (wff_i[:, FFN:2 * FFN], wuT),
                (wdn_i, wdT.rearrange("(k p) n -> p k n", p=P)),
                (w_att[:], Wout.rearrange("(k p) n -> p k n", p=P)),
            ]
            for half in range(2):
                for q in range(2):
                    head = 2 * half + q
                    loads.append((dskip[HD * q:HD * q + HD, half:half + 1],
                                  D_skip[:, head:head + 1].to_broadcast([HD, 1])))
            assert len(loads) == NLOADS
            act.wait_ge(early_loaded, 16 * NEARLY)
            act.activation(expA[:], alog[:], ACT.Exp).then_inc(expA_made, 1)
            act.wait_ge(set_v, 1)
            act.activation(w_in_hi[:], w_in[:], ACT.Copy).then_inc(set_a, 1)
            for dst, src in loads:
                act.dma_start(dst, src).then_inc(weights_loaded, 16)

            def w1_part(i):
                wait_apart(act, folded, i + 1)
                act.activation(w1_hi[:, i, :], w1[:, i, :], ACT.Copy).then_inc(w1hi_made, 1)

            def stage0(i, par, first=False, last=False):
                if not first:
                    act.wait_ge(dt_made, i - 1)
                hi(0, i, par, None if first else zT_stashed[par], (i - par) * 16)
                if not last:
                    z(0, i + 1)
                w1_part(i)

            z(0, 0)
            for par in range(2):
                stage0(par, par, first=True)
            with act.Fori(2, SEQS - 3, 2) as i:
                stage0(i, 0)
                stage0(i + 1, 1)
            stage0(SEQS - 2, 0)
            stage0(SEQS - 1, 1, last=True)
            act.wait_ge(step_v, 1)
            act.activation(sm[:, 1], sm[:, 0], ACT.Abs).then_inc(step_a, 1)
            act.wait_ge(step_a, 1)
            act.activation(sm[:, 2], sm[:, 1], ACT.Exp, scale=-1.0).then_inc(step_a, 1)

            def small(a):
                return a[:].rearrange("p s c h -> p (s c h)")

            act.wait_ge(cum_copied, 2)
            act.activation(small(ecum_t), sm[:, 3], ACT.Exp).then_inc(step_a, 1)
            act.activation(small(etail_t), sm[:, 4], ACT.Exp).then_inc(step_a, 1)
            act.activation(small(dec_t), bank(4)[:, 0:NC], ACT.Exp).then_inc(step_a, 1)

            for n, (h, w) in enumerate(((wg_hi, wg), (w4_hi, w4s), (wff_hi, wff))):
                act.wait_ge(set_v, (7, 9, 10)[n])
                act.activation(h[:], w[:], ACT.Copy).then_inc(set_a, 1)

            def tapA(i, half):
                act.wait_ge(proj_made, i * 6 + half + 1)
                act.wait_ge(xc_made, i * 2)
                act.activation(u[:, half], bank(half), ACT.Identity, bias=convb[:, half:half + 1],
                               scale=convw[:, half, 3:4]).then_inc(tap_made, 1)

            def tanhA(i, half, par, free):
                act.wait_ge(conv_made, i * 6 + 3 * half + 3)
                if free is not None:
                    act.wait_ge(yf_made, free)
                act.activation(xc[par][:, half], u[:, half], ACT.Tanh).then_inc(th_made, 1)

            def bcA(i, n):
                act.wait_ge(proj_made, i * 6 + (3, 6)[n])
                if n == 0:
                    act.wait_ge(T_made, i * CH)
                    act.wait_ge(G_made, i)
                else:
                    act.wait_ge(Y_made, i * CH)
                act.activation((Bf, Cf)[n][:], bank(n), ACT.Copy).then_inc(bc_made, 1)

            def tzA(i, half, par, free):
                act.wait_ge(proj_made, i * 6 + 4 + half)
                if free is not None:
                    act.wait_ge(yg_made, free)
                act.activation(gz[par][:, half], bank(1 - half), ACT.Tanh, scale=0.5).then_inc(tz_made, 1)

            def decayA(i, c):
                act.wait_ge(D_made, i * CH + c + 1)
                act.wait_ge(Y_made, i * CH + max(c - 1, 0))
                act.activation(Edec[:, c % 2].rearrange("p h i -> p (h i)"), bank(4), ACT.Exp).then_inc(E_made, 1)
                if c < CH - 1:
                    act.wait_ge(dtx_made, i * CH + c + 1)
                    act.wait_ge(S_made, i * 3 + c)
                    act.activation(Btok[:], bank(3)[:, INNER:INNER + P], ACT.Copy).then_inc(btok_made, 1)

            def stepA(i, c, par, first=False, last=False):
                if c < CH - 1:
                    decayA(i, c + 1)
                elif not last:
                    decayA(i + 1, 0)
                if not last:
                    if c < 2:
                        tapA(i + 1, c)
                    if c in (1, 2):
                        tanhA(i + 1, c - 1, 1 - par, i * CH * 2)
                    if c == 2:
                        bcA(i + 1, 0)
                        tzA(i + 1, 0, 1 - par, i * CH)
                        tzA(i + 1, 1, 1 - par, i * CH)
                    if c == 3:
                        bcA(i + 1, 1)
                if not first:
                    wait_apart(act, resA_made, (i - 1) * CH + c + 1)
                input_z(i, c, z1_made)

            def stageA(i, par, first=False, last=False):
                for c in range(CH):
                    stepA(i, c, par, first, last)

            for half in range(2):
                tapA(0, half)
            for half in range(2):
                tanhA(0, half, 0, None)
            bcA(0, 0)
            tzA(0, 0, 0, None)
            tzA(0, 1, 0, None)
            bcA(0, 1)
            decayA(0, 0)
            stageA(0, 0, first=True)
            with act.Fori(1, SEQS - 2, 2) as i:
                stageA(i, 1)
                stageA(i + 1, 0)
            stageA(SEQS - 1, 1, last=True)

            def gateB(i):
                act.wait_ge(gate_v, i * GATE_STEPS + 7)
                act.activation(ge[:, 1], ge[:, 0], ACT.Sigmoid).then_inc(gate_a, 1)
                act.activation(ge[:, 2], ge[:, 0], ACT.Sigmoid, scale=-1.0).then_inc(gate_a, 1)

            def accT_copy(t):
                act.wait_ge(accT_in_psum, t + 1)
                act.wait_ge(moe_made, t)
                act.activation(accT[:], bank(6)[:, 0:HID].rearrange("p (k n) -> p k n", k=2), ACT.Copy)\
                    .then_inc(accT_made, 1)

            def stageB(i, par, first=False, last=False):
                for c in range(CH):
                    t = i * CH + c
                    for e in range(EXPERTS):
                        n = t * EXPERTS + e
                        act.wait_ge(h_made, n + 1)
                        act.wait_ge(g_made, n + 1)
                        act.activation(sig[:, e % 4], bank(e % 4)[:, HID:2 * HID], ACT.Sigmoid).then_inc(sig_made, 1)
                        if e == 0 and not (first and c < 2):
                            accT_copy(t - 2)
                        if not last:
                            if (c, e) == (0, 0):
                                residual(1, i + 1)
                            if (c, e) == (1, 3):
                                z(1, i + 1)
                            if (c, e) == (1, 7):
                                hi(1, i + 1, 1 - par, h_made, i * 32)
                            if (c, e) == (3, 2):
                                gateB(i + 1)

            residual(1, 0)
            z(1, 0)
            hi(1, 0, 0, zT_stashed[0], 16 * SEQS)
            gateB(0)
            stageB(0, 0, first=True)
            with act.Fori(1, SEQS - 2, 2) as i:
                stageB(i, 1)
                stageB(i + 1, 0)
            stageB(SEQS - 1, 1, last=True)
            accT_copy(NT - 2)
            accT_copy(NT - 1)

            def frontC(i):
                act.wait_ge(cproj_made, i * 5 + 1)
                act.wait_ge(var_made, i * 4)
                act.activation(qkf[:], bank(2), ACT.Silu).then_inc(cact_made, 1)
                act.wait_ge(o_made, i * 2)
                for k in range(2):
                    act.wait_ge(cproj_made, i * 5 + 2 + k)
                    act.activation(vt[:, 2 * k:2 * k + 2, :], bank(3 + k).rearrange("p (c n) -> p c n", c=2), ACT.Silu)\
                        .then_inc(cact_made, 1)
                for half in range(2):
                    act.wait_ge(cproj_made, i * 5 + 4 + half)
                    act.wait_ge(og_made, i * 2)
                    act.activation(gt[:, half], bank(half), ACT.Silu).then_inc(cact_made, 1)

            def stageC(i, par, last=0):
                if last < 1:
                    residual(2, i + 2)
                act.wait_ge(lkT_made, i + 1)
                act.wait_ge(kv_made, i * 3)
                act.activation(lkt[:].rearrange("p c d -> p (c d)"), bank(2), ACT.Copy).then_inc(lkt_made, 1)
                for c in range(3):
                    act.wait_ge(kv_made, i * 3 + c + 1)
                    act.wait_ge(o_made, i * 2)
                    act.activation(kvs[:, c], bank(3)[:, 0:HID], ACT.Copy, scale=1.0 / GROUP).then_inc(kvs_made, 1)
                wait_apart(act, res_made, SEQS + i)
                for c in range(CH):
                    input_z(i, c, cz_made)
                if last < 1:
                    z(2, i + 2)
                    hi(2, i + 2, par, cproj_made, (i + 1) * 5)
                if last < 2:
                    frontC(i + 1)

            for k in range(2):
                residual(2, k)
                z(2, k)
                hi(2, k, k, None, 0)
            frontC(0)
            with act.Fori(0, SEQS - 3, 2) as i:
                stageC(i, 0)
                stageC(i + 1, 1)
            stageC(SEQS - 2, 0, 1)
            stageC(SEQS - 1, 1, 2)

            def stageD(i, par, first=False, last=0):
                if last < 2:
                    z(3, i + 1)
                    hi(3, i + 1, 1 - par, gu_made, i * 3)
                for m in range(3):
                    act.wait_ge(gu_made, i * 3 + m + 1)
                    act.wait_ge(hf_made, i * 3 + m + 1)
                    act.activation(sg[:, m], bank(m), ACT.Silu, scale=1.0 / 127).then_inc(sg_made, 1)
                    if m == 0 and last < 1:
                        residual(3, i + 2)
                if not first:
                    residD(i - 1)

            def residD(i):
                wait_apart(act, dn_made, i + 1)
                act.activation(RES[:, i].rearrange("p c d -> p (c d)"), bank(7), ACT.Copy).then_inc(resD_made, 1)

            residual(3, 0)
            z(3, 0)
            hi(3, 0, 0, None, 0)
            residual(3, 1)
            stageD(0, 0, first=True)
            with act.Fori(1, SEQS - 4, 2) as i:
                stageD(i, 1)
                stageD(i + 1, 0)
            stageD(SEQS - 3, 1)
            stageD(SEQS - 2, 0, last=1)
            stageD(SEQS - 1, 1, last=2)
            residD(SEQS - 1)
            with act.Fori(0, SEQS) as i:
                residual(4, i)

        @block.vector
        def _(dve):
            def apart(semaphore, value):
                wait_apart(dve, semaphore, value)

            def stats(stage, i):
                bn_stats(stage, i)
                bn_aggr(stage, i)

            def bn_stats(stage, i):
                n = stage * SEQS + i
                apart(mv_made, n * CH)
                if stage > 0:
                    apart(x_new, n - SEQS + 1)
                for c in range(CH):
                    dve.bn_stats(stats_t[:, c], X[:, i, c]).then_inc(stats_made, 1)

            def bn_aggr(stage, i):
                n = stage * SEQS + i
                apart(stats_made, (n + 1) * CH)
                apart(scale_made, n)
                for c in range(CH):
                    dve.bn_aggr(mv[:, c], stats_t[:, c]).then_inc(mv_made, 1)

            def x_add(stage, i):
                n = (stage - 1) * SEQS + i
                dve.wait_ge(add_made, (n + 1) * CH)
                dve.tensor_tensor(X[:, i], X[:, i], add[:], ALU.add).then_inc(x_new, 1)

            def lo(stage, i, par):
                dve.wait_ge(hi_made, stage * SEQS + i + 1)
                dve.tensor_tensor(ZT_lo[par][:], bank(5), ZT_hi[par][:].bitcast(F32), ALU.subtract).then_inc(lo_made, 1)

            def rstats(stage, i):
                rbn_stats(stage, i)
                rbn_aggr(stage, i)

            def rbn_stats(stage, i):
                n = (stage - 1) * SEQS + i
                apart(rmv_made, n * CH)
                if stage == 1:
                    apart(resA_made, (i + 1) * CH)
                elif stage < 4:
                    apart(res_made, n - SEQS + 1)
                else:
                    apart(resD_made, i + 1)
                for c in range(CH):
                    dve.bn_stats(rstats_t[:, c], RES[:, i, c]).then_inc(rstats_made, 1)

            def rbn_aggr(stage, i):
                n = (stage - 1) * SEQS + i
                apart(rstats_made, (n + 1) * CH)
                apart(rrstd_made, n)
                for c in range(CH):
                    dve.bn_aggr(rmv[:, c], rstats_t[:, c]).then_inc(rmv_made, 1)

            dve.memset(credit[:, 0:1], 0.0).then_inc(g_made, BCREDIT)
            dve.memset(credit[:, 1:2], 0.0).then_inc(hf_made, DCREDIT)

            dve.wait_ge(x_loaded, 16)
            stats(0, 0)
            dve.wait_ge(early_loaded, 16 * NEARLY)
            dve.tensor_scalar(w_in[:], w_in[:], normw[:], None, ALU.mult).then_inc(set_v, 1)

            def w1lo(i):
                dve.wait_ge(w1hi_made, i + 1)
                dve.tensor_tensor(w1_lo[:, i, :], w1[:, i, :], w1_hi[:, i, :].bitcast(F32), ALU.subtract)\
                   .then_inc(w1lo_made, 1)

            def stage0(i, par, first=False, last=False):
                if not last:
                    if par == 1:
                        dve.wait_ge(x_loaded, (i + 3) * 8)
                    stats(0, i + 1)
                lo(0, i, par)
                if not first:
                    w1lo(i - 1)
                dve.wait_ge(fold_made, i + 1)
                dve.tensor_tensor(w1[:, i, :], w1[:, i, :], bank(par), ALU.add).then_inc(folded, 1)

            stage0(0, 0, first=True)
            stage0(1, 1)
            with dve.Fori(2, SEQS - 3, 2) as i:
                stage0(i, 0)
                stage0(i + 1, 1)
            stage0(SEQS - 2, 0)
            stage0(SEQS - 1, 1, last=True)
            w1lo(SEQS - 1)

            cb = lambda a: a.unsqueeze(1).to_broadcast([P, NT, HEADS])
            th3 = lambda a: a.rearrange("p (t h) -> p t h", h=HEADS)
            flat = lambda a: a[:].rearrange("p s c h -> p (s c h)")
            steps = [0]

            def step(ins):
                steps[0] += 1
                ins.then_inc(step_v, 1)
                dve.wait_ge(step_v, steps[0])

            dve.wait_ge(dt_made, SEQS)
            step(dve.tensor_tensor(th3(sm[:, 0]), th3(bank(2)[:, 0:NC]), cb(dtb[:]), ALU.add))
            dve.wait_ge(step_a, 2)
            step(dve.tensor_scalar(sm[:, 5], sm[:, 2], 2.0, None, ALU.add))
            step(dve.reciprocal(sm[:, 6], sm[:, 5]))
            step(dve.tensor_tensor(sm[:, 7], sm[:, 2], sm[:, 6], ALU.mult))
            step(dve.tensor_tensor(sm[:, 5], sm[:, 7], sm[:, 7], ALU.mult))
            step(dve.tensor_scalar(sm[:, 6], sm[:, 5], 1.0 / 15, None, ALU.mult))
            for k in (13, 11, 9, 7, 5, 3):
                step(dve.scalar_tensor_tensor(sm[:, 6], sm[:, 6], 1.0 / k, sm[:, 5], ALU.add, ALU.mult))
            step(dve.scalar_tensor_tensor(sm[:, 6], sm[:, 6], 1.0, sm[:, 7], ALU.add, ALU.mult))
            step(dve.tensor_scalar(sm[:, 1], sm[:, 0], 0.0, None, ALU.max))
            step(dve.scalar_tensor_tensor(flat(dt_t), sm[:, 6], 2.0, sm[:, 1], ALU.mult, ALU.add))
            dve.wait_ge(expA_made, 1)
            step(dve.tensor_tensor(th3(sm[:, 7]), th3(flat(dt_t)), cb(expA[:]), ALU.mult))
            assert steps[0] == 16
            dve.wait_ge(cum_in_psum, 2)
            dve.tensor_copy(sm[:, 3], bank(3)[:, 0:NC]).then_inc(cum_copied, 1)
            dve.wait_ge(cum_copied, 1)
            dve.tensor_tensor(sm[:, 4], bank(4)[:, 0:NC], sm[:, 3], ALU.subtract).then_inc(cum_copied, 1)
            dve.tensor_copy(cparts[:, 0], sm[:, 3]).then_inc(parts_made, 1)
            dve.wait_ge(parts_made, 1)
            dve.tensor_tensor(sm[:, 5], sm[:, 3], cparts[:, 0], ALU.subtract).then_inc(parts_made, 1)
            dve.wait_ge(parts_made, 2)
            dve.tensor_copy(cparts[:, 1], sm[:, 5]).then_inc(parts_made, 1)
            dve.wait_ge(parts_made, 3)
            dve.tensor_tensor(sm[:, 6], sm[:, 5], cparts[:, 1], ALU.subtract).then_inc(parts_made, 1)
            dve.wait_ge(parts_made, 4)
            dve.tensor_copy(cparts[:, 2], sm[:, 6]).then_inc(parts_made, 1)
            dve.wait_ge(partsT_in_psum, 1)
            dve.tensor_copy(cpartsT[:], bank(6).bitcast(BF16)[:, 0:3 * P].rearrange("p (q n) -> p q n", q=3))\
               .then_inc(parts_made, 1)

            dve.wait_ge(weights_loaded, 16 * NLOADS)
            dve.tensor_scalar(convw[:], convw[:], 0.5, None, ALU.mult).then_inc(set_v, 1)
            dve.tensor_scalar(convb[:], convb[:], 0.5, None, ALU.mult).then_inc(set_v, 1)
            dve.tensor_scalar(w_out[:], w_out[:], 0.5, None, ALU.mult).then_inc(set_v, 1)
            dve.tensor_scalar(w4s[:], w4[:], lnw[:], None, ALU.mult).then_inc(set_v, 1)
            dve.tensor_scalar(lnb_avg[:], allneg[:], lnb[:], -1.0 / P, ALU.mult, ALU.mult).then_inc(set_v, 1)
            dve.memset(shifted[:], 0.0).then_inc(shifted_made, 1)
            dve.wait_ge(shifted_made, 1)
            root = float(P) ** 0.5
            dve.tensor_scalar(shifted[:, 0:16], table[:, 0:16], root, None, ALU.mult).then_inc(shifted_made, 1)
            for k in sorted(set(BUCKETS[16:])):
                first, many = BUCKETS.index(k), BUCKETS.count(k)
                dve.tensor_scalar(shifted[:, first:first + many], table[:, k:k + 1].to_broadcast([GROUP, many]), root,
                                  None, ALU.mult).then_inc(shifted_made, 1)
            dve.wait_ge(set_t, 1)
            dve.tensor_tensor(wg[:], wg[:], bank(6)[:, 0:EXPERTS], ALU.add).then_inc(set_v, 1)
            dve.wait_ge(set_t, 2)
            dve.tensor_tensor(w4s[:, 0:512], w4s[:, 0:512], bank(0), ALU.add).then_inc(set_v, 1)
            dve.tensor_tensor(w4s[:, 512:640], w4s[:, 512:640], bank(1)[:, 0:P], ALU.add).then_inc(set_v, 1)
            dve.tensor_copy(wff[:], wff_i).then_inc(set_v, 1)
            dve.tensor_copy(wdn[:], wdn_i).then_inc(set_v, 1)

            def heads(a):
                return a.rearrange("p (h d) -> p h d", h=HEADS)

            def byhead(a, i, c):
                return a[:, i, c, :].unsqueeze(2).to_broadcast([P, HEADS, HD])

            def convA(i, half):
                dve.wait_ge(tap_made, i * 2 + half + 1)
                for k in range(1, 4):
                    if k > 1:
                        dve.wait_ge(conv_made, i * 6 + 3 * half + k - 1)
                    dve.scalar_tensor_tensor(u[:, half, k:], bank(half)[:, 0:TOK - k], convw[:, half, 3 - k:4 - k],
                                             u[:, half, k:], ALU.mult, ALU.add).then_inc(conv_made, 1)

            def xcA(i, par):
                for half in range(2):
                    dve.wait_ge(th_made, i * 2 + half + 1)
                    dve.scalar_tensor_tensor(xc[par][:, half], xc[par][:, half], 1.0, u[:, half], ALU.add, ALU.mult)\
                       .then_inc(xc_made, 1)

            def gzA(i, par, half):
                dve.wait_ge(tz_made, i * 2 + half + 1)
                dve.scalar_tensor_tensor(gz[par][:, half], gz[par][:, half], 1.0, bank(1 - half), ALU.add, ALU.mult)\
                   .then_inc(gz_made, 1)

            def chunk_in(i, c):
                t = i * CH + c
                dve.wait_ge(T_made, t + 1)
                dve.wait_ge(Y_made, i * CH + max(c - 1, 0))
                dve.wait_ge(wdtx_made, i * 3 + max(c - 1, 0))
                dve.tensor_tensor(heads(dtx[:, c % 2]), heads(bank(3)[:, 0:INNER]), byhead(dt_t, i, c), ALU.mult)\
                   .then_inc(dtx_made, 1)

            def decayed(i, c):
                dve.wait_ge(E_made, i * CH + c + 1)
                dve.wait_ge(G_made, i + 1)
                dve.tensor_tensor(Mdec[:, c % 2], Edec[:, c % 2],
                                  bank(5)[:, cols(c)].unsqueeze(1).to_broadcast([P, HEADS, P]), ALU.mult)\
                   .then_inc(M_made, 1)

            def residA(t, i, c):
                dve.wait_ge(out_made, t + 1)
                dve.wait_ge(z1_made, t + 1)
                dve.tensor_tensor(RES[:, i, c], z1[:, c], bank(7)[:, 0:P], ALU.add).then_inc(resA_made, 1)

            def yfA(t, c, par, ring):
                dve.wait_ge(YT_made, t + 1)
                if ring:
                    dve.wait_ge(out_made, t - 1)
                for half in range(2):
                    dve.scalar_tensor_tensor(yf[:, c % 2, half], xc[par][:, half, cols(c)], dskip[:, half:half + 1],
                                             bank(2)[:, cols(half)], ALU.mult, ALU.add).then_inc(yf_made, 1)

            def stepA(i, c, par, first=False, last=False):
                t = i * CH + c
                if c < CH - 1:
                    chunk_in(i, c + 1)
                    decayed(i, c + 1)
                elif not last:
                    chunk_in(i + 1, 0)
                dve.wait_ge(Y_made, t + 1)
                if not (first and c < 2):
                    dve.wait_ge(YT_made, t - 1)
                if c == 0:
                    dve.tensor_copy(ytok[:, c % 2], bank(6)[:, 0:INNER]).then_inc(y_made, 1)
                else:
                    dve.tensor_tensor(heads(ytok[:, c % 2]), heads(bank(6)[:, INNER:2 * INNER]), byhead(ecum_t, i, c),
                                      ALU.mult).then_inc(y1_made, 1)
                if c == 0:
                    dve.wait_ge(S_made, i * 3 + 1)
                    dve.tensor_copy(St[:], bank(7)[:, 0:INNER]).then_inc(st_made, 1)
                elif c < CH - 1:
                    dve.wait_ge(S_made, i * 3 + c + 1)
                    dve.wait_ge(sd_made, i * 2 + c)
                    dve.tensor_tensor(St[:], Sd[:], bank(7)[:, 0:INNER], ALU.add).then_inc(st_made, 1)
                if c > 0:
                    dve.wait_ge(y1_made, i * 3 + c)
                    dve.tensor_tensor(ytok[:, c % 2], ytok[:, c % 2], bank(6)[:, 0:INNER], ALU.add).then_inc(y_made, 1)
                if c < 2 and not last:
                    convA(i + 1, c)
                elif c == 2 and not last:
                    xcA(i + 1, 1 - par)
                    gzA(i + 1, 1 - par, 0)
                elif not last:
                    gzA(i + 1, 1 - par, 1)
                if not (first and c < 2):
                    residA(t - 2, i if c >= 2 else i - 1, (c + 2) % CH)
                if not (first and c == 0):
                    yfA(t - 1, (c + 3) % CH, par if c > 0 else 1 - par, not (first and c < 3))
                if c == CH - 1 and not last:
                    decayed(i + 1, 0)
                if c == 1 and not first:
                    rbn_stats(1, i - 1)
                if c == 2 and not first:
                    rbn_aggr(1, i - 1)

            def stageA(i, par, first=False, last=False):
                for c in range(CH):
                    stepA(i, c, par, first, last)

            for half in range(2):
                convA(0, half)
            xcA(0, 0)
            gzA(0, 0, 0)
            gzA(0, 0, 1)
            chunk_in(0, 0)
            decayed(0, 0)
            stageA(0, 0, first=True)
            with dve.Fori(1, SEQS - 2, 2) as i:
                stageA(i, 1)
                stageA(i + 1, 0)
            stageA(SEQS - 1, 1, last=True)
            residA(NT - 2, SEQS - 1, CH - 2)
            yfA(NT - 1, CH - 1, 1, True)
            residA(NT - 1, SEQS - 1, CH - 1)
            rstats(1, SEQS - 1)

            def gateB(i, par, part):
                g = [i * GATE_STEPS + GATE_AT[part]]

                def step(ins):
                    g[0] = g[0] + 1
                    ins.then_inc(gate_v, 1)

                def after():
                    dve.wait_ge(gate_v, g[0])

                def bc(a):
                    return a.to_broadcast([P, CH, EXPERTS])

                below, sg1, sg2, ex = (ge[:, k] for k in range(4))
                total, both, first, second = (gs[:, k] for k in range(4))
                e2 = ex[:, :, EXPERTS]
                if part == 0:
                    dve.wait_ge(logits_made, i + 1)
                    step(dve.tensor_copy(lg[:], bank(4)[:, 0:CH * EXPERTS].rearrange("p (c e) -> p c e", c=CH)))
                elif part == 1:
                    apart(gate_v, g[0])
                    for c in range(CH):
                        step(dve.max(top[:, c], lg[:, c]))
                elif part == 2:
                    after()
                    step(dve.tensor_tensor(below[:, :, 0:EXPERTS], lg[:], bc(top[:, :, 0:1]), ALU.subtract))
                    step(dve.tensor_tensor(below[:, :, EXPERTS:], top[:, :, 1:2], top[:, :, 0:1], ALU.subtract))
                    for c in range(CH):
                        step(dve.max_index(topi[:, c], top[:, c], lg[:, c]))
                elif part == 3:
                    after()
                    step(dve.tensor_copy(topf[:], topi[:, :, 0:2]))
                elif part == 4:
                    after()
                    iota_b = iota8[:].unsqueeze(1).to_broadcast([P, CH, EXPERTS])
                    step(dve.tensor_tensor(pick[:, 0], iota_b, bc(topf[:, :, 0:1]), ALU.is_equal))
                    step(dve.tensor_tensor(pick[:, 1], iota_b, bc(topf[:, :, 1:2]), ALU.is_equal))
                elif part == 5:
                    dve.wait_ge(gate_a, (i + 1) * 2)
                    step(dve.reciprocal(ex, sg2))
                elif part == 6:
                    after()
                    step(dve.tensor_tensor(ex, ex, sg1, ALU.mult))
                elif part == 7:
                    after()
                    step(dve.reduce_sum(total, ex[:, :, 0:EXPERTS], AX.X))
                elif part == 8:
                    after()
                    step(dve.scalar_tensor_tensor(both, total, TOP_EPS, e2, ALU.mult, ALU.add))
                    after()
                    step(dve.tensor_scalar(both, both, 1.0, None, ALU.add))
                elif part == 9:
                    after()
                    step(dve.reciprocal(first, both))
                    after()
                    step(dve.tensor_tensor(second, e2, first, ALU.mult))
                    after()
                    step(dve.tensor_tensor(csum[par][:], first, second, ALU.add))
                    step(dve.tensor_tensor(pick[:, 0], pick[:, 0], bc(first.unsqueeze(2)), ALU.mult))
                    step(dve.tensor_tensor(pick[:, 1], pick[:, 1], bc(second.unsqueeze(2)), ALU.mult))
                    after()
                    step(dve.tensor_tensor(comb[par][:], pick[:, 0], pick[:, 1], ALU.add))
                    after()

            def accB(t, k, free):
                dve.wait_ge(half_made, (t + 1) * 3)
                if free:
                    dve.wait_ge(accT_in_psum, t - 1)
                dve.tensor_tensor(acc[k][:], gb[:, k, 0], gb[:, k, 1], ALU.add).then_inc(acc_made, 1)

            def residB(i, par, tiles, done):
                dve.wait_ge(moe_made, (i + 1) * CH)
                for c in tiles:
                    ins = dve.scalar_tensor_tensor(RES[:, i, c], bo_rows[:], csum[par][:, c:c + 1], bank(7)[:, cols(c)],
                                                   ALU.mult, ALU.add)
                if done:
                    ins.then_inc(res_made, 1)

            GATE_PLACES = [(2, 6), (2, 7), (3, 0), (3, 1), (3, 2), (3, 4), (3, 5), (3, 6), (3, 7), (3, 7)]

            def stageB(i, par, first=False, last=False):
                for c in range(CH):
                    t = i * CH + c
                    for e in range(EXPERTS):
                        dve.wait_ge(sig_made, t * EXPERTS + e + 1)
                        dve.scalar_tensor_tensor(gb[:, c % 2, e], bank(e % 4)[:, 0:HID], comb[par][:, c, e:e + 1],
                                                 sig[:, e % 4], ALU.mult, ALU.mult).then_inc(g_made, 1)
                        if e == 5 and not (first and c == 0):
                            accB(t - 1, (c + 1) % 2, not (first and c < 3))
                        if not last:
                            if (c, e) == (0, 1):
                                x_add(1, i + 1)
                            if (c, e) == (0, 3):
                                bn_stats(1, i + 1)
                            if (c, e) == (0, 6):
                                bn_aggr(1, i + 1)
                            if (c, e) == (2, 1):
                                lo(1, i + 1, 1 - par)
                            for part, place in enumerate(GATE_PLACES):
                                if place == (c, e):
                                    gateB(i + 1, 1 - par, part)
                        if not first:
                            if (c, e) == (1, 3):
                                residB(i - 1, 1 - par, (0, 1), False)
                            if (c, e) == (1, 4):
                                residB(i - 1, 1 - par, (2, 3), True)
                            if (c, e) == (1, 6):
                                rbn_stats(2, i - 1)
                            if (c, e) == (2, 0):
                                rbn_aggr(2, i - 1)

            x_add(1, 0)
            stats(1, 0)
            lo(1, 0, 0)
            for part in range(len(GATE_PLACES)):
                gateB(0, 0, part)
            stageB(0, 0, first=True)
            with dve.Fori(1, SEQS - 2, 2) as i:
                stageB(i, 1)
                stageB(i + 1, 0)
            stageB(SEQS - 1, 1, last=True)
            accB(NT - 1, 1, True)
            residB(SEQS - 1, 1, range(CH), True)
            rstats(2, SEQS - 1)

            def variants(i):
                dve.wait_ge(cact_made, i * 5 + 1)
                dve.wait_ge(o_made, i * 2)
                for k in (2, 0, 3, 1):
                    dve.tensor_scalar(qv[:, k], qkf[:], qkw[:, k:k + 1], qkb[:, k:k + 1], ALU.mult, ALU.add)\
                       .then_inc(var_made, 1)

            def stageC(i, par, last=0):
                if last < 1:
                    x_add(2, i + 2)
                    stats(2, i + 2)
                quad = at[:, 0].rearrange("p (c i) -> p c i", c=CH)
                lin = at[:, 1].rearrange("p (c i) -> p c i", c=CH)
                dve.wait_ge(s1_made, i + 1)
                dve.scalar_tensor_tensor(quad, bank(6).rearrange("p (c i) -> p c i", c=CH), 1.0 / GROUP,
                                         near[:].unsqueeze(1).to_broadcast([P, CH, P]), ALU.mult, ALU.add)\
                   .then_inc(att_made, 1)
                dve.wait_ge(att_made, i * 4 + 1)
                dve.scalar_tensor_tensor(at[:, 0], at[:, 0], 0.0, at[:, 0], ALU.max, ALU.mult).then_inc(att_made, 1)
                dve.wait_ge(s2_made, i + 1)
                dve.tensor_tensor(lin, bank(7).rearrange("p (c i) -> p c i", c=CH),
                                  before[:].unsqueeze(1).to_broadcast([P, CH, P]), ALU.mult).then_inc(att_made, 1)
                dve.wait_ge(att_made, i * 4 + 3)
                dve.tensor_tensor(at[:, 0], at[:, 0], at[:, 1], ALU.add).then_inc(att_made, 1)
                if last < 1:
                    lo(2, i + 2, par)
                for half in range(2):
                    dve.wait_ge(o_made, i * 2 + half + 1)
                    dve.wait_ge(cact_made, i * 5 + 4 + half)
                    dve.wait_ge(cout_made, i)
                    dve.tensor_tensor(og[:, half], bank(6 + half), gt[:, half], ALU.mult).then_inc(og_made, 1)
                if last < 2:
                    variants(i + 1)
                dve.wait_ge(czb_made, i + 1)
                dve.wait_ge(cout_made, i + 1)
                dve.tensor_tensor(RES[:, i], z1[:], bank(5).rearrange("p (c d) -> p c d", c=CH), ALU.add)\
                   .then_inc(res_made, 1)
                rstats(3, i)

            for k in range(2):
                x_add(2, k)
                stats(2, k)
                lo(2, k, k)
            variants(0)
            dve.wait_ge(fillers, 7)
            with dve.Fori(0, SEQS - 3, 2) as i:
                stageC(i, 0)
                stageC(i + 1, 1)
            stageC(SEQS - 2, 0, 1)
            stageC(SEQS - 1, 1, 2)

            def stageD(i, par, first=False, last=0):
                if last < 1:
                    x_add(3, i + 2)
                for m in range(3):
                    dve.wait_ge(sg_made, i * 3 + m + 1)
                    if not first:
                        dve.wait_ge(dn_made, i - 1)
                    dve.scalar_tensor_tensor(hf[par][:, m], bank((3, 4, 6)[m]), 1.0 / (127 * 127), sg[:, m],
                                             ALU.mult, ALU.mult).then_inc(hf_made, 1)
                    if m == 0 and last < 2:
                        lo(3, i + 1, 1 - par)
                if last < 1:
                    stats(3, i + 2)
                if not first:
                    rstats(4, i - 1)

            for k in range(2):
                x_add(3, k)
                stats(3, k)
                if k == 0:
                    lo(3, 0, 0)
            stageD(0, 0, first=True)
            with dve.Fori(1, SEQS - 4, 2) as i:
                stageD(i, 1)
                stageD(i + 1, 0)
            stageD(SEQS - 3, 1)
            stageD(SEQS - 2, 0, last=1)
            stageD(SEQS - 1, 1, last=2)
            rstats(4, SEQS - 1)
            with dve.Fori(0, SEQS) as i:
                x_add(4, i)

        @block.tensor
        def _(pe):
            def split3(dst, lhs, rhs, start=True, stop=True):
                (lh, ll), (rh, rl) = lhs, rhs
                pe.matmul(dst, lh, rh, start=start, stop=False)
                pe.matmul(dst, lh, rl, start=False, stop=False)
                return pe.matmul(dst, ll, rh, start=False, stop=stop)

            def zT(stage, i, free, value):
                n = stage * SEQS + i
                pe.wait_ge(z_made, (n + 1) * CH)
                pe.wait_ge(lo_made, n)
                if free is not None:
                    pe.wait_ge(free, value)
                for c in range(CH):
                    ins = pe.transpose(bank(5)[:, cols(c)], Z[:, c], ident[:])
                ins.then_inc(zT_made, 1)

            def zt(par, c=None):
                part = slice(0, TOK) if c is None else cols(c)
                return ZT_hi[par][:, part], ZT_lo[par][:, part]

            pe.wait_ge(consts, 5)

            def stage0(i, par):
                zT(0, i, None, None)
                pe.wait_ge(w1_loaded, (i + 2) * 8 if par == 0 else (i + 1) * 8)
                pe.wait_ge(early_loaded, 16 * NEARLY)
                pe.wait_ge(folded, max(i - 1, 0) if isinstance(i, int) else i - 1)
                pe.matmul(bank(par), negavg[:], w1[:, i, :], start=True, stop=False)
                pe.matmul(bank(par), avgrow[:], b1r[:, i, :], start=False, stop=True).then_inc(fold_made, 1)
                pe.wait_ge(lo_made, i + 1)
                pe.wait_ge(wlo_made, 1)
                for c in range(CH):
                    ins = split3(bank(2)[:, 0:NC].rearrange("p (s c h) -> p s c h", s=SEQS, c=CH)[:, i, c, :], zt(par, c),
                                 (w_in_hi[:, 768:772], w_in_lo[:, 768:772]))
                ins.then_inc(dt_made, 1)

            for par in range(2):
                stage0(par, par)
            with pe.Fori(2, SEQS - 1, 2) as i:
                stage0(i, 0)
                stage0(i + 1, 1)
            pe.wait_ge(step_v, 16)
            pe.matmul(bank(3)[:, 0:NC], cumneg[:], sm[:, 7], start=True, stop=True).then_inc(cum_in_psum, 1)
            pe.matmul(bank(4)[:, 0:NC], allneg[:], sm[:, 7], start=True, stop=True).then_inc(cum_in_psum, 1)
            pe.wait_ge(parts_made, 5)
            for q in range(3):
                ins = pe.transpose(bank(6).bitcast(BF16)[:, q * P:(q + 1) * P], cparts[:, q], identb[:])
            ins.then_inc(partsT_in_psum, 1)
            pe.wait_ge(weights_loaded, 16 * NLOADS)
            pe.wait_ge(parts_made, 6)
            pe.matmul(bank(6)[:, 0:EXPERTS], negavg[:], wg[:], start=True, stop=True).then_inc(set_t, 1)
            pe.wait_ge(set_v, 6)
            for b, part in ((0, slice(0, 512)), (1, slice(512, 640))):
                dst = bank(b)[:, 0:part.stop - part.start]
                pe.matmul(dst, lnb_avg[:], w4[:, part], start=True, stop=False)
                pe.matmul(dst, avgrow[:], b4r[:, part], start=False, stop=False)
                ins = pe.matmul(dst, negavg[:], w4s[:, part], start=False, stop=True)
            ins.then_inc(set_t, 1)

            PROJ = [256, 384, 512, 0, 128, 640]

            def projA(i, k):
                used = [(gz_made, i * 2), (bc_made, i * 2), (conv_made, i * 6 + 3), (conv_made, i * 6 + 6),
                        (bc_made, i * 2 + 1), (gz_made, i * 2 + 1)][k]
                if not (k < 2 and isinstance(i, int) and i == 0):
                    pe.wait_ge(*used)
                col = PROJ[k]
                split3(bank(k % 2), (w_in_hi[:, col:col + P], w_in_lo[:, col:col + P]),
                       (XT_hi[:, i, :], XT_lo[:, i, :])).then_inc(proj_made, 1)

            def chunk_in(i, c, par):
                t = i * CH + c
                if c == 0:
                    pe.wait_ge(xc_made, i * 2 + 2)
                    pe.wait_ge(bc_made, i * 2 + 1)
                pe.wait_ge(dtx_made, t)
                pe.wait_ge(btok_made, i * 3 + c)
                for half in range(2):
                    ins = pe.transpose(bank(3)[:, cols(half)], xc[par][:, half, cols(c)], ident[:])
                if c < CH - 1:
                    ins = pe.transpose(bank(3)[:, INNER:INNER + P], Bf[:, cols(c)], ident[:])
                ins.then_inc(T_made, 1)
                pe.wait_ge(E_made, t)
                pe.matmul(bank(4), identb[:], far4[:].rearrange("p h i -> p (h i)"), start=True, stop=False)
                pe.matmul(bank(4), parts[:, t, :], headrows_neg[:].rearrange("p h i -> p (h i)"), start=False, stop=False)
                for h in range(HEADS):
                    ins = pe.matmul(bank(4)[:, cols(h)], headrows[:, h, :], parts[:, t, :], start=False,
                                    stop=h == HEADS - 1)
                ins.then_inc(D_made, 1)

            def pairsA(i):
                pe.wait_ge(bc_made, i * 2 + 2)
                pe.wait_ge(M_made, i * CH)
                for c in range(CH):
                    ins = pe.matmul(bank(5)[:, cols(c)], Bf[:, cols(c)], Cf[:, cols(c)], start=True, stop=True)
                ins.then_inc(G_made, 1)

            def outA(t, c):
                pe.wait_ge(yg_made, t + 1)
                for half in range(2):
                    ins = pe.matmul(bank(7)[:, 0:P], yf[:, c % 2, half], w_out[:, half], start=half == 0, stop=half == 1)
                ins.then_inc(out_made, 1)

            def yT_A(t, c):
                pe.wait_ge(y_made, t + 1)
                pe.wait_ge(yf_made, 2 * t)
                for half in range(2):
                    ins = pe.transpose(bank(2)[:, cols(half)], ytok[:, c % 2, cols(half)], ident[:])
                ins.then_inc(YT_made, 1)

            def stepA(i, c, par, first=False, last=False):
                t = i * CH + c
                if c < CH - 1:
                    chunk_in(i, c + 1, par)
                elif not last:
                    chunk_in(i + 1, 0, 1 - par)
                pe.wait_ge(M_made, t + 1)
                pe.wait_ge(y_made, t)
                for h in range(HEADS):
                    ins = pe.matmul(bank(6)[:, h * HD:(h + 1) * HD], Mdec[:, c % 2, h],
                                    dtx[:, c % 2, h * HD:(h + 1) * HD], start=True, stop=True)
                if c > 0:
                    pe.wait_ge(st_made, i * 3 + c)
                    ins = pe.matmul(bank(6)[:, INNER:2 * INNER], Cf[:, cols(c)], St[:], start=True, stop=True)
                ins.then_inc(Y_made, 1)
                if c < CH - 1:
                    pe.wait_ge(wdtx_made, i * 3 + c + 1)
                    pe.wait_ge(btok_made, i * 3 + c + 1)
                    if not (first and c < 3):
                        pe.wait_ge(resA_made, t - 2)
                    pe.matmul(bank(7)[:, 0:INNER], Btok[:], wdtx[:], start=True, stop=True).then_inc(S_made, 1)
                if not last:
                    for k in ((0,), (1,), (2, 3, 4), (5,))[c]:
                        projA(i + 1, k)
                if not (first and c < 2):
                    if c < CH - 1:
                        pe.wait_ge(st_made, i * 3 + c + 1)
                    else:
                        pe.wait_ge(resA_made, t - 2)
                    outA(t - 2, (c + 2) % CH)
                if not (first and c == 0):
                    yT_A(t - 1, (c + 3) % CH)
                if c == CH - 1 and not last:
                    pairsA(i + 1)

            def stageA(i, par, first=False, last=False):
                for c in range(CH):
                    stepA(i, c, par, first, last)

            for k in range(2):
                pe.wait_ge(zT_stashed[k], 16 * SEQS)
            pe.wait_ge(set_v, 11)
            for k in range(6):
                projA(0, k)
            pairsA(0)
            pe.wait_ge(rows_moved, NROWS)
            pe.wait_ge(fillers, 1)
            pe.wait_ge(step_a, 5)
            chunk_in(0, 0, 0)
            stageA(0, 0, first=True)
            with pe.Fori(1, SEQS - 2, 2) as i:
                stageA(i, 1)
                stageA(i + 1, 0)
            stageA(SEQS - 1, 1, last=True)
            pe.wait_ge(resA_made, NT - 2)
            outA(NT - 2, CH - 2)
            yT_A(NT - 1, CH - 1)
            pe.wait_ge(resA_made, NT - 1)
            outA(NT - 1, CH - 1)

            def logitsB(i, par):
                pe.wait_ge(lo_made, SEQS + i + 1)
                pe.wait_ge(gate_v, i * GATE_STEPS)
                for c in range(CH):
                    ins = split3(bank(4)[:, c * EXPERTS:(c + 1) * EXPERTS], zt(par, c), (wg_hi[:], wg_lo[:]))
                ins.then_inc(logits_made, 1)

            def accT_B(t, k):
                pe.wait_ge(acc_made, t + 1)
                pe.wait_ge(accT_made, t)
                for h in range(2):
                    ins = pe.transpose(bank(6)[:, cols(h)], acc[k][:, cols(h)], ident[:])
                ins.then_inc(accT_in_psum, 1)

            def moe_out(t, i, c, guard):
                pe.wait_ge(accT_made, t + 1)
                if c == 0:
                    pe.wait_ge(res_made, i)
                for h in range(2):
                    ins = pe.matmul(bank(7)[:, cols(c)], accT[:, h], w_o[:, h], start=h == 0, stop=h == 1)
                ins.then_inc(moe_made, 1)

            def stageB(i, par, first=False, last=False):
                for c in range(CH):
                    t = i * CH + c
                    for e in range(EXPERTS):
                        pe.wait_ge(g_made, t * EXPERTS + e + 1)
                        split3(bank(e % 4), zt(par, c), (w1_hi[:, e], w1_lo[:, e])).then_inc(h_made, 1)
                        if e == 1 and not (first and c < 2):
                            moe_out(t - 2, i if c >= 2 else i - 1, (c + 2) % 4, None)
                        if e == 5 and c == 1 and not last:
                            zT(1, i + 1, None, None)
                        if e == 4 and c == 2 and not last:
                            logitsB(i + 1, 1 - par)
                    if not (first and c == 0):
                        accT_B(t - 1, (c + 1) % 2)

            pe.wait_ge(w1lo_made, SEQS)
            pe.wait_ge(wlo_made, 2)
            zT(1, 0, None, None)
            logitsB(0, 0)
            stageB(0, 0, first=True)
            with pe.Fori(1, SEQS - 2, 2) as i:
                stageB(i, 1)
                stageB(i + 1, 0)
            stageB(SEQS - 1, 1, last=True)
            moe_out(NT - 2, SEQS - 1, 2, None)
            accT_B(NT - 1, 1)
            moe_out(NT - 1, SEQS - 1, 3, None)

            def w4p(a, b):
                return w4_hi[:, a:b], w4_lo[:, a:b]

            def projC(i, par):
                pe.wait_ge(lo_made, 2 * SEQS + i + 1)
                pe.wait_ge(lkt_made, i)
                split3(bank(2), w4p(512, 640), zt(par)).then_inc(cproj_made, 1)
                pe.wait_ge(cact_made, i * 5)
                pe.wait_ge(kvs_made, i * 3)
                for k in range(2):
                    for c in range(2):
                        ins = split3(bank(3 + k)[:, c * HID:(c + 1) * HID], zt(par, 2 * k + c), w4p(0, HID))
                    ins.then_inc(cproj_made, 1)
                for half in range(2):
                    split3(bank(half), w4p(HID + P * half, HID + P * half + P), zt(par)).then_inc(cproj_made, 1)

            def stageC(i, par, last=0):
                pe.wait_ge(var_made, i * 4 + 4)
                pe.wait_ge(og_made, i * 2)
                for c in range(CH):
                    ins = pe.matmul(bank(6)[:, cols(c)], qv[:, 2, cols(c)], qv[:, 0, cols(c)], start=True, stop=True)
                ins.then_inc(s1_made, 1)
                for c in range(CH):
                    ins = pe.matmul(bank(7)[:, cols(c)], qv[:, 3, cols(c)], qv[:, 1, cols(c)], start=True, stop=True)
                ins.then_inc(s2_made, 1)
                for c in range(CH):
                    ins = pe.transpose(bank(2)[:, cols(c)], qv[:, 3, cols(c)], ident[:])
                ins.then_inc(lkT_made, 1)
                pe.wait_ge(lkt_made, i + 1)
                pe.wait_ge(cact_made, i * 5 + 3)
                for c in range(3):
                    if c > 0:
                        pe.wait_ge(kvs_made, i * 3 + c)
                    pe.matmul(bank(3)[:, 0:HID], lkt[:, c], vt[:, c], start=c == 0, stop=True, skip_group_check=True)\
                      .then_inc(kv_made, 1)
                if last < 1:
                    zT(2, i + 2, res_made, SEQS + i)
                if last < 2:
                    projC(i + 1, 1 - par)
                pe.wait_ge(att_made, i * 4 + 4)
                pe.wait_ge(kvs_made, i * 3 + 3)
                for half in range(2):
                    for c in range(CH):
                        dst = bank(6 + half)[:, cols(c)]
                        ins = pe.matmul(dst, vt[:, c, cols(half)], at[:, 0, cols(c)], start=True, stop=c == 0)
                        if c > 0:
                            ins = pe.matmul(dst, kvs[:, c - 1, cols(half)], qv[:, 1, cols(c)], start=False, stop=True)
                    ins.then_inc(o_made, 1)
                pe.wait_ge(og_made, i * 2 + 2)
                pe.wait_ge(lo_made, 2 * SEQS + (i + 3 if last < 1 else SEQS))
                pe.wait_ge(res_made, SEQS + i)
                for c in range(CH):
                    for half in range(2):
                        ins = pe.matmul(bank(5)[:, cols(c)], og[:, half, cols(c)], w_att[:, half],
                                        start=half == 0, stop=half == 1)
                ins.then_inc(cout_made, 1)

            pe.wait_ge(wlo_made, 4)
            zT(2, 0, None, None)
            zT(2, 1, None, None)
            projC(0, 0)
            with pe.Fori(0, SEQS - 3, 2) as i:
                stageC(i, 0)
                stageC(i + 1, 1)
            stageC(SEQS - 2, 0, 1)
            stageC(SEQS - 1, 1, 2)

            def down(i, par):
                pe.wait_ge(hf_made, (i + 1) * 3 + DCREDIT)
                pe.wait_ge(resD_made, i)
                for c in range(CH):
                    for m in range(3):
                        ins = pe.matmul(bank(7)[:, cols(c)], hf[par][:, m, cols(c)], wdn[:, m], start=m == 0, stop=m == 2)
                ins.then_inc(dn_made, 1)

            def stageD(i, par, first=False, last=False):
                pe.wait_ge(lo_made, 3 * SEQS + i + 1)
                for m in range(3):
                    pe.wait_ge(hf_made, i * 3 + m + 1)
                    for b, col in ((m, m * P), ((3, 4, 6)[m], FFN + m * P)):
                        ins = split3(bank(b), (wff_hi[:, col:col + P], wff_lo[:, col:col + P]), zt(par))
                    ins.then_inc(gu_made, 1)
                    if m == 0 and not last:
                        zT(3, i + 1, None, None)
                if not first:
                    down(i - 1, 1 - par)

            zT(3, 0, res_made, 2 * SEQS)
            stageD(0, 0, first=True)
            with pe.Fori(1, SEQS - 2, 2) as i:
                stageD(i, 1)
                stageD(i + 1, 0)
            stageD(SEQS - 1, 1, last=True)
            down(SEQS - 1, 1)


_INS = ["x", "norm_w", "in_wT", "conv_w", "conv_b", "A_log", "D", "dt_bias", "out_wT", "WgT", "W1T", "b1", "WoT", "bo",
        "ln_w", "ln_b", "Wh", "bh", "Wqk", "bqk", "qk_w", "qk_b", "rel", "Wout", "bout", "wgT", "wuT", "wdT"]


def kernel(L0_attn_x, L0_attn_norm_w, L0_attn_in_proj_w, L0_attn_conv_w, L0_attn_conv_b, L0_attn_A_log, L0_attn_D,
           L0_attn_dt_bias, L0_attn_out_proj_w, L0_ffn_Wg, L0_ffn_W1, L0_ffn_b1, L0_ffn_Wo, L0_ffn_bo, L1_attn_ln_w,
           L1_attn_ln_b, L1_attn_Wh, L1_attn_bh, L1_attn_Wqk, L1_attn_bqk, L1_attn_qk_w, L1_attn_qk_b,
           L1_attn_rel_table, L1_attn_Wout, L1_attn_bout, L1_ffn_w_gate, L1_ffn_w_up, L1_ffn_w_down):
    import numpy as np
    import concourse.bacc as bacc
    from concourse.bass_utils import run_bass_kernel_spmd

    def row(a):
        return np.asarray(a).reshape(1, -1)

    def col(a):
        return np.asarray(a).reshape(-1, 1)

    def T(a):
        return np.asarray(a).T

    arrays = dict(
        x=L0_attn_x, norm_w=col(L0_attn_norm_w), in_wT=T(L0_attn_in_proj_w),
        conv_w=np.asarray(L0_attn_conv_w).reshape(2, P, 4).transpose(1, 0, 2),
        conv_b=np.asarray(L0_attn_conv_b).reshape(2, P).T, A_log=row(L0_attn_A_log), D=row(L0_attn_D),
        dt_bias=row(L0_attn_dt_bias), out_wT=T(L0_attn_out_proj_w), WgT=T(L0_ffn_Wg),
        W1T=np.asarray(L0_ffn_W1).transpose(0, 2, 1), b1=np.asarray(L0_ffn_b1).reshape(1, EXPERTS, 2 * HID),
        WoT=T(L0_ffn_Wo), bo=row(L0_ffn_bo), ln_w=col(L1_attn_ln_w), ln_b=col(L1_attn_ln_b), Wh=L1_attn_Wh,
        bh=row(L1_attn_bh), Wqk=L1_attn_Wqk, bqk=row(L1_attn_bqk), qk_w=T(L1_attn_qk_w), qk_b=T(L1_attn_qk_b),
        rel=row(L1_attn_rel_table), Wout=L1_attn_Wout, bout=row(L1_attn_bout), wgT=T(L1_ffn_w_gate),
        wuT=T(L1_ffn_w_up), wdT=T(L1_ffn_w_down))
    nc = bacc.Bacc("TRN2", target_bir_lowering=False, num_devices=1)
    in_map, args = {}, []
    for name in _INS:
        a = np.ascontiguousarray(arrays[name])
        in_map[f"in_{name}"] = a
        args.append(nc.dram_tensor(f"in_{name}", a.shape, mybir.dt.from_np(a.dtype), kind="ExternalInput").ap())
    out = nc.dram_tensor("out", (SEQS, TOK, P), F32, kind="ExternalOutput").ap()
    build(nc, *args, out)
    return run_bass_kernel_spmd(nc, [in_map], core_ids=[0]).results[0]["out"]
```

```python
import concourse.bass as bass
from concourse import mybir
from contextlib import ExitStack

ALU = mybir.AluOpType
ACT = mybir.ActivationFunctionType
AX = mybir.AxisListType
F32 = mybir.dt.float32
F32R = mybir.dt.float32r
BF16 = mybir.dt.bfloat16
I32 = mybir.dt.int32
U32 = mybir.dt.uint32

P = 128
SEQS, TOK = 8, 512
CH = TOK // P
NT = SEQS * CH
HEADS, HD = 4, 64
INNER = HEADS * HD
EXPERTS, HID = 8, 256
GROUP = 32
FFN = 384
LN_EPS, RMS_EPS, TOP_EPS = 1e-5, 1e-6, 1e-9
FAR = -1e30


GATE_AT = (0, 1, 6, 12, 13, 15, 16, 17, 18, 20, 23, 24)
GATE_STEPS = 26


def t5_buckets():
    import math
    return [n if n < 16 else min(31, 16 + int(math.log(n / 16) / math.log(8) * 16)) for n in range(GROUP)]


BUCKETS = t5_buckets()


def build(nc, x_in, vectors, rows, in_wT, W1T, b1, squares, W4, b4, Wff, out):
    ctx = ExitStack()
    with ctx:
        def sb(name, shape, dt=F32):
            return ctx.enter_context(nc.sbuf_tensor(name, shape, dt))

        def sem(name):
            return ctx.enter_context(nc.semaphore(name))

        X = sb("X", [P, SEQS, CH, P])
        RES = sb("RES", [P, SEQS, CH, P])
        res_shift = sb("res_shift", [P, SEQS, CH])
        res_rstd = sb("res_rstd", [P, SEQS, CH])
        ps = ctx.enter_context(nc.psum_tensor("ps", [P, 8, 512], F32))

        def bank(b):
            return ps[:, b, :]

        ident = sb("ident", [P, P])
        identb = sb("identb", [P, P], BF16)
        negavg = sb("negavg", [P, P])
        avgrow = sb("avgrow", [1, P])
        cumneg = sb("cumneg", [P, P])
        allneg = sb("allneg", [P, P])
        far4 = sb("far4", [P, HEADS, P], BF16)
        mhalf = sb("mhalf", [P, 2, CH])
        iota8 = sb("iota8", [P, EXPERTS])
        iota8i = sb("iota8i", [P, EXPERTS], I32)
        near = sb("near", [P, P])
        before = sb("before", [P, P])

        w_in = sb("w_in", [P, 772])
        w_in_hi = sb("w_in_hi", [P, 772], F32R)
        w_in_lo = sb("w_in_lo", [P, 772], F32R)
        w_dt = sb("w_dt", [P, 2, HEADS], F32R)
        w1 = RES[:].rearrange("p s c d -> p s (c d)")
        w1_hi = sb("w1_hi", [P, EXPERTS, 512], F32R)
        w1_lo = sb("w1_lo", [P, EXPERTS, 512], F32R)
        wg_parts = sb("wg_parts", [P, 2, EXPERTS], F32R)
        wg_hi, wg_lo = wg_parts[:, 0], wg_parts[:, 1]
        columns = sb("columns", [P, 23])
        normw, convb, dskip, lnw, lnb = (columns[:, a:b] for a, b in ((0, 1), (9, 11), (11, 13), (13, 14), (14, 15)))
        convw = columns[:, 1:9].rearrange("p (h k) -> p h k", h=2)
        qkw, qkb = columns[:, 15:19], columns[:, 19:23]
        shared = sb("shared", [P, 296])
        alog, dtb, table = shared[:, 0:4], shared[:, 4:8], shared[0:GROUP, 8:40]
        bo_rows, bout_rows = shared[:, 40:168], shared[:, 168:296]
        out_weights = sb("out_weights", [P, 6, P])
        w_out, w_o, w_att = (out_weights[:, 2 * k:2 * k + 2] for k in range(3))
        w4 = sb("w4", [P, 648])
        wg = w4[:, 640:648]
        w4s = sb("w4s", [P, 640])
        w4_hi = sb("w4_hi", [P, 640], F32R)
        w4_lo = sb("w4_lo", [P, 640], F32R)
        b4r = sb("b4r", [1, 640])
        lnb_avg = sb("lnb_avg", [P, P])
        shifted = sb("shifted", [GROUP, 65])
        wffn = sb("wffn", [P, 3 * FFN])
        wffn_i = wffn[:].bitcast(I32)
        wff, wdn = wffn[:, 0:2 * FFN], wffn[:, 2 * FFN:].rearrange("p (m n) -> p m n", m=3)
        wff_hi = sb("wff_hi", [P, 2 * FFN], F32R)
        wff_lo = sb("wff_lo", [P, 2 * FFN], F32R)

        ZT_hi = [sb(f"ZT_hi{k}", [P, TOK], F32R) for k in range(2)]
        ZT_lo = [sb(f"ZT_lo{k}", [P, TOK], F32R) for k in range(2)]
        Z = sb("Z", [P, CH, P])
        add = sb("add", [P, CH, P])
        stats_t = sb("stats_t", [P, CH, 6])
        mv = sb("mv", [P, CH, 2])
        vars_t = sb("vars_t", [P, 2, CH])
        rstds = sb("rstds", [P, 2, CH])
        negmean = sb("negmean", [P, CH])
        prod = sb("prod", [P, CH])
        shift = sb("shift", [P, CH])
        credit = sb("credit", [1, 5])
        z1 = sb("z1", [P, CH, P])
        rstats_t = sb("rstats_t", [P, CH, 6])
        rmv = sb("rmv", [P, CH, 2])
        rvar = sb("rvar", [P, CH])
        rnegmean = sb("rnegmean", [P, CH])

        scratch = nc.dram_tensor("rel_scratch", [GROUP * 65], F32, kind="Internal").ap()
        parts_scratch = nc.dram_tensor("parts_scratch", [P * 3 * P], BF16, kind="Internal").ap()

        early = ExitStack()

        def sb(name, shape, dt=F32):
            return early.enter_context(nc.sbuf_tensor(name, shape, dt))

        x_shift = sb("x_shift", [P, SEQS, CH])
        x_rstd = sb("x_rstd", [P, SEQS, CH])
        XT_hi = sb("XT_hi", [P, SEQS, TOK], F32R)
        XT_lo = sb("XT_lo", [P, SEQS, TOK], F32R)
        NC = NT * HEADS
        cpartsT = sb("cpartsT", [P, 3, P], BF16)
        dt_t, ecum_t, etail_t, dec_t = (sb(n, [P, SEQS, CH, HEADS]) for n in ("dt_t", "ecum_t", "etail_t", "dec_t"))
        expA = sb("expA", [P, HEADS])
        parts = sb("parts", [P, NT, P], BF16)
        headrows = sb("headrows", [P, HEADS, P], BF16)
        headrows_neg = sb("headrows_neg", [P, HEADS, P], BF16)
        work = sb("work", [P, 8, TOK])
        b1r = work[0:1]
        u = work[:, 0:2]
        xc = [work[:, 2:4], work[:, 4:6]]
        gz = [work[:, 6:8], sb("gz1", [P, 2, TOK])[:]]
        Bf = sb("Bf", [P, TOK])
        Cf = [sb(f"Cf{k}", [P, TOK]) for k in range(2)]
        taps = [sb("taps", [P, TOK])[:], add[:].rearrange("p c d -> p (c d)"), Z[:].rearrange("p c d -> p (c d)")]
        St = sb("St", [P, INNER])
        Sd = sb("Sd", [P, INNER])
        tails = sb("tails", [P, 8, P])
        ytok = tails[:, 0:4].rearrange("p (k c) d -> p k (c d)", k=2)
        yf = tails[:, 4:8].rearrange("p (k c) d -> p k c d", k=2)
        sm = tails
        assert NC == P

        dtx = sb("dtx", [P, 2, INNER])
        wdtx = sb("wdtx", [P, INNER])
        cparts = wdtx[:, 0:3 * NC // 2].bitcast(BF16).rearrange("p (q n) -> p q n", q=3)
        Btok = sb("Btok", [P, P])
        Edec = sb("Edec", [P, 2, HEADS, P])
        Mdec = Edec

        early.close()

        def sb(name, shape, dt=F32):
            return ctx.enter_context(nc.sbuf_tensor(name, shape, dt))

        lg = sb("lg", [P, CH, EXPERTS])
        top = sb("top", [P, CH, 8])
        topi = sb("topi", [P, CH, 8], U32)
        topf = sb("topf", [P, CH, 2])
        ge = sb("ge", [P, 4, CH, EXPERTS + 1])
        gs = sb("gs", [P, 6, CH])
        pick = sb("pick", [P, 2, CH, EXPERTS])
        comb = [sb(f"comb{k}", [P, CH, EXPERTS]) for k in range(2)]
        csum = [sb(f"csum{k}", [P, CH]) for k in range(2)]
        sig = sb("sig", [P, 4, HID])
        gb = sb("gb", [P, 2, EXPERTS, HID])
        acc = [sb(f"acc{k}", [P, HID]) for k in range(2)]
        accT = sb("accT", [P, 2, P])

        qkf = sb("qkf", [P, TOK])
        qv = [sb(f"qv{k}", [P, 4, TOK]) for k in range(2)]
        vt = [sb(f"vt{k}", [P, CH, HID]) for k in range(2)]
        gt = [sb(f"gt{k}", [P, 2, TOK]) for k in range(2)]
        lkt = sb("lkt", [P, CH, P])
        at = sb("at", [P, 2, TOK])
        kvs = sb("kvs", [P, 3, HID])
        og = sb("og", [P, 2, TOK])

        sg = sb("sg", [P, 3, TOK])
        hf = [gb[:].rearrange("p a e d -> p (a e d)")[:, k * 3 * TOK:(k + 1) * 3 * TOK].rearrange("p (m t) -> p m t", m=3)
              for k in range(2)]
        last_add = sb("last_add", [P, CH, P])

        x_loaded, w1_loaded, weights_loaded, rel_written, rel_loaded = (
            sem(n) for n in ("x_loaded", "w1_loaded", "weights_loaded", "rel_written", "rel_loaded"))
        consts, fillers = sem("consts"), sem("fillers")
        set_v, set_t, set_a, set_g = sem("set_v"), sem("set_t"), sem("set_a"), sem("set_g")
        parts_written, rows_moved, out_stored = sem("parts_written"), sem("rows_moved"), sem("out_stored")
        zT_stashed = [sem(f"zT_stashed{k}") for k in range(2)]
        add_made, x_new, stats_made, mv_made, scale_made, z_made = (
            sem(n) for n in ("add_made", "x_new", "stats_made", "mv_made", "scale_made", "z_made"))
        zT_made, hi_made, lo_made = sem("zT_made"), sem("hi_made"), sem("lo_made")
        pool_step = sem("pool_step")
        res_made, rstats_made, rmv_made, rrstd_made = (
            sem(n) for n in ("res_made", "rstats_made", "rmv_made", "rrstd_made"))
        fold_made, folded, w1hi_made, w1lo_made, dt_made = (
            sem(n) for n in ("fold_made", "folded", "w1hi_made", "w1lo_made", "dt_made"))
        step_v, step_a = sem("step_v"), sem("step_a")
        expA_made, cum_in_psum, cum_copied, parts_made, partsT_in_psum, shifted_made, wlo_made, resD_made = (
            sem(n) for n in ("expA_made", "cum_in_psum", "cum_copied", "parts_made", "partsT_in_psum", "shifted_made",
                             "wlo_made", "resD_made"))
        xs_made, ladd_made, x_final = sem("xs_made"), sem("ladd_made"), sem("x_final")
        taps_made, conv2_made = sem("A_taps"), sem("A_conv2")
        early_loaded, waited, resA_made = sem("early_loaded"), sem("waited"), sem("resA_made")
        proj_made, tap_made, conv_made, bc_made, th_made, xc_made, tz_made, gz_made = (
            sem("A_" + n) for n in ("proj", "tap", "conv", "bc", "th", "xc", "tz", "gz"))
        G_made, T_made, D_made, E_made, M_made, dtx_made, btok_made, wdtx_made = (
            sem("A_" + n) for n in ("G", "T", "D", "E", "M", "dtx", "btok", "wdtx"))
        Y_made, y1_made, y_made, S_made, sd_made, st_made, YT_made, yf_made, yg_made, out_made, z1_made = (
            sem("A_" + n) for n in ("Y", "y1", "y", "S", "sd", "st", "YT", "yf", "yg", "out", "z1"))
        h_made, sig_made, g_made, half_made, acc_made, accT_in_psum, accT_made, moe_made = (
            sem("B_" + n) for n in ("h", "sig", "g", "half", "acc", "accTp", "accT", "moe"))
        logits_made, gate_v, gate_a = sem("B_logits"), sem("B_gate_v"), sem("B_gate_a")
        cproj_made, cact_made, var_made, s1_made, s2_made, lkT_made, lkt_made, att_made = (
            sem("C_" + n) for n in ("proj", "act", "var", "s1", "s2", "lkT", "lkt", "att"))
        kv_made, kvs_made, o_made, og_made, cout_made, cz_made, czb_made = (
            sem("C_" + n) for n in ("kv", "kvs", "o", "og", "out", "cz", "czb"))
        gu_made, sg_made, hf_made, dn_made = (
            sem("D_" + n) for n in ("gu", "sg", "hf", "dn"))

        block = ctx.enter_context(nc.Block())

        def cols(c):
            return slice(c * P, (c + 1) * P)

        NEARLY, NLOADS = 4, 4
        BCREDIT = 4
        DCREDIT = 3
        LCREDIT = 1

        GATE_BANKS, UP_BANKS = (0, 4, 3), (1, 2, 6)
        EARLY_D = 2

        def wait_apart(engine, semaphore, value):
            engine.wait_ge(semaphore, value).then_inc(waited, 1)

        @block.sync
        def _(sp):
            def x_pair(j):
                sp.dma_start(X[:].rearrange("p (j two) c d -> p j (two c) d", two=2)[:, j],
                             x_pairs[j].rearrange("(c p) d -> p c d", p=P)).then_inc(x_loaded, 16)

            def w1_pair(j):
                sp.dma_start(w1.rearrange("p (j two) n -> p j two n", two=2)[:, j],
                             w1_pairs[j].rearrange("e p n -> p e n")).then_inc(w1_loaded, 16)

            def stash(i, par):
                sp.wait_ge(hi_made, i + 1)
                sp.dma_start(XT_hi[:, i, :].bitcast(F32), ZT_hi[par][:].bitcast(F32)).then_inc(zT_stashed[par], 16)
                wait_apart(sp, lo_made, i + 1)
                sp.dma_start(XT_lo[:, i, :].bitcast(F32), ZT_lo[par][:].bitcast(F32)).then_inc(zT_stashed[par], 16)

            x_pairs = x_in.rearrange("(j two) t d -> j (two t) d", two=2)
            w1_pairs = W1T.rearrange("(j two) p n -> j two p n", two=2)
            def next_x(j):
                sp.wait_ge(x_loaded, 16 * j)
                x_pair(j)

            def next_w1(j):
                sp.wait_ge(w1_loaded, 16 * j)
                w1_pair(j)

            x_pair(0)
            for dst, src in ((columns[:], vectors), (w_in[:], in_wT), (shared[:], rows.to_broadcast([P, 296])),
                             (b1r.rearrange("p e n -> p (e n)"), b1)):
                sp.dma_start(dst, src).then_inc(early_loaded, 16)
            w1_pair(0)
            next_x(1)
            next_w1(1)
            next_x(2)
            for dst, src in ((out_weights[:], squares.rearrange("k p n -> p k n")), (w4[:], W4), (b4r[:], b4),
                             (wffn_i, Wff)):
                sp.dma_start(dst, src).then_inc(weights_loaded, 16)
            stash(0, 0)
            next_w1(2)
            stash(1, 1)
            next_x(3)
            next_w1(3)
            with sp.Fori(2, SEQS - 1, 2) as i:
                stash(i, 0)
                stash(i + 1, 1)
            sp.wait_ge(fillers, 1)
            sp.wait_ge(parts_made, 6)
            sp.dma_start(parts_scratch.rearrange("(p q n) -> p q n", q=3, n=P), cpartsT[:]).then_inc(parts_written, 16)
            sp.wait_ge(parts_written, 16)
            sp.dma_start(parts[0:3 * HEADS, :, :], parts_scratch.rearrange("(t r n) -> r t n", r=3 * HEADS, n=P))\
              .then_inc(rows_moved, 16)
            sp.wait_ge(shifted_made, 2 + len(set(BUCKETS[16:])))
            sp.dma_start(scratch.rearrange("(p n) -> p n", n=65), shifted[:]).then_inc(rel_written, 16)
            sp.wait_ge(rel_written, 16)
            sp.wait_ge(fillers, 1)
            for g in range(P // GROUP):
                sp.dma_start(near[GROUP * g:GROUP * (g + 1), GROUP * g:GROUP * (g + 1)],
                             scratch[0:GROUP * 64].rearrange("(p n) -> p n", n=64)[:, 0:GROUP])\
                  .then_inc(rel_loaded, 16)
            with sp.Fori(0, SEQS) as i:
                sp.wait_ge(x_final, i + 1 + LCREDIT)
                sp.dma_start(out[i].rearrange("(c p) d -> p c d", p=P), X[:, i]).then_inc(out_stored, 16)
            sp.wait_ge(out_stored, 16 * SEQS)

        STEPS, STEPS_RES = (4, 4, 5, 3), 3

        @block.gpsimd
        def _(pool):
            pool.memset(ident[:], 0.0).then_inc(set_g, 1)
            pool.memset(negavg[:], -1.0 / P).then_inc(set_g, 1)
            pool.memset(avgrow[:], 1.0 / P).then_inc(set_g, 1)
            pool.memset(mhalf[:], -0.5).then_inc(set_g, 1)
            pool.memset(allneg[:], -1.0).then_inc(set_g, 1)
            pool.wait_ge(set_g, 5)
            pool.affine_select(out=ident[:], in_=ident[:], compare_op=ALU.not_equal, fill=1.0, base=0,
                               pattern=[[-1, P]], channel_multiplier=1).then_inc(consts, 1)
            pool.affine_select(out=cumneg[:], in_=allneg[:], compare_op=ALU.is_ge, fill=0.0, base=0,
                               pattern=[[1, P]], channel_multiplier=-1).then_inc(consts, 1)
            pool.iota(iota8i[:], pattern=[[1, EXPERTS]], base=0, channel_multiplier=0).then_inc(consts, 1)
            pool.wait_ge(consts, 3)
            pool.tensor_copy(iota8[:], iota8i[:]).then_inc(consts, 1)
            pool.tensor_copy(identb[:], ident[:]).then_inc(consts, 1)

            def scales(stage, i, done):
                n = stage * SEQS + i
                twice = stage in (0, 2)
                k = 2 if twice else 1
                wait_apart(pool, mv_made, (n + 1) * CH)
                wait_apart(pool, scale_made, n)
                if twice:
                    wait_apart(pool, xs_made, 2 * (i if stage == 0 else SEQS + i))
                m, v = mv[:, :, 0], mv[:, :, 1]
                pool.tensor_scalar(negmean[:], m, -1.0, None, ALU.mult).then_inc(pool_step, 1)
                pool.tensor_scalar(vars_t[:, 0], v, LN_EPS, None, ALU.add).then_inc(pool_step, 1)
                if twice:
                    eps2 = RMS_EPS if stage == 0 else LN_EPS
                    pool.tensor_scalar(vars_t[:, 1], v, 1.0 + eps2, LN_EPS * eps2, ALU.mult, ALU.add)\
                        .then_inc(pool_step, 1)
                pool.wait_ge(pool_step, done + k + 1)
                pool.wait_ge(z_made, n * CH)
                pool.tensor_tensor(rstds[:, 0:k], vars_t[:, 0:k], mhalf[:, 0:k], ALU.pow).then_inc(pool_step, 1)
                done = done + k + 2
                pool.wait_ge(pool_step, done)
                if stage in (0, 3):
                    pool.tensor_tensor(shift[:], negmean[:], rstds[:, k - 1], ALU.mult).then_inc(scale_made, 1)
                else:
                    pool.tensor_tensor(prod[:], negmean[:], rstds[:, k - 1], ALU.mult).then_inc(pool_step, 1)
                    done = done + 1
                    wait_apart(pool, pool_step, done)
                    pool.tensor_scalar(shift[:], prod[:], 1.0, None, ALU.add).then_inc(scale_made, 1)
                if twice:
                    pool.tensor_copy(x_rstd[:, i, :], rstds[:, 0]).then_inc(xs_made, 1)
                    pool.tensor_tensor(x_shift[:, i, :], negmean[:], rstds[:, 0], ALU.mult).then_inc(xs_made, 1)
                return done

            def res_scales(stage, i, done):
                n = (stage - 1) * SEQS + i
                wait_apart(pool, rmv_made, (n + 1) * CH + LCREDIT)
                wait_apart(pool, rrstd_made, n + LCREDIT)
                pool.tensor_scalar(rnegmean[:], rmv[:, :, 0], -1.0, None, ALU.mult).then_inc(pool_step, 1)
                pool.tensor_scalar(rvar[:], rmv[:, :, 1], LN_EPS, None, ALU.add).then_inc(pool_step, 1)
                wait_apart(pool, pool_step, done + 2)
                pool.tensor_tensor(res_rstd[:, i, :], rvar[:], mhalf[:, 0], ALU.pow).then_inc(pool_step, 1)
                wait_apart(pool, pool_step, done + 3)
                pool.tensor_tensor(res_shift[:, i, :], rnegmean[:], res_rstd[:, i, :], ALU.mult).then_inc(rrstd_made, 1)
                return done + STEPS_RES

            done = scales(0, 0, 0)
            pool.wait_ge(set_a, 2)
            pool.tensor_tensor(w_dt[:, 1], w_in[:, 768:772], w_dt[:, 0].bitcast(F32), ALU.subtract).then_inc(wlo_made, 1)
            pool.tensor_tensor(w_in_lo[:], w_in[:], w_in_hi[:].bitcast(F32), ALU.subtract).then_inc(wlo_made, 1)
            with pool.Fori(1, SEQS) as i:
                scales(0, i, i * STEPS[0])
            done = SEQS * STEPS[0]

            pool.memset(parts[:].bitcast(F32), 0.0).then_inc(set_g, 1)
            pool.memset(headrows[:], 1.0).then_inc(set_g, 1)
            pool.memset(far4[:], 0.0).then_inc(set_g, 1)
            pool.wait_ge(set_g, 8)
            pool.affine_select(out=headrows[:], in_=headrows[:], compare_op=ALU.is_ge, fill=0.0, base=0,
                               pattern=[[-3, HEADS], [0, P]], channel_multiplier=1).then_inc(set_g, 1)
            pool.affine_select(out=far4[:], in_=far4[:], compare_op=ALU.is_ge, fill=FAR, base=0,
                               pattern=[[0, HEADS], [1, P]], channel_multiplier=-1).then_inc(set_g, 1)
            pool.wait_ge(set_g, 10)
            pool.affine_select(out=headrows[:], in_=headrows[:], compare_op=ALU.is_ge, fill=0.0, base=2,
                               pattern=[[3, HEADS], [0, P]], channel_multiplier=-1).then_inc(set_g, 1)
            pool.wait_ge(set_g, 11)
            pool.tensor_scalar(headrows_neg[:], headrows[:], -1.0, None, ALU.mult).then_inc(set_g, 1)
            pool.wait_ge(set_g, 12)
            pool.memset(near[:], FAR).then_inc(fillers, 1)
            pool.memset(before[:], 1.0 / GROUP).then_inc(fillers, 1)
            pool.wait_ge(fillers, 2)
            for g in range(P // GROUP):
                pool.memset(before[GROUP * g:GROUP * (g + 1), 0:GROUP * (g + 1)], 0.0).then_inc(fillers, 1)
            pool.wait_ge(fillers, 2 + P // GROUP)
            def decayedA(i, c):
                pool.wait_ge(dtx_made, i * CH + c + 1)
                pool.wait_ge(S_made, i * 3 + c)
                pool.tensor_tensor(wdtx[:].rearrange("p (h d) -> p h d", h=HEADS),
                                   dtx[:, c % 2].rearrange("p (h d) -> p h d", h=HEADS),
                                   etail_t[:, i, c, :].unsqueeze(2).to_broadcast([P, HEADS, HD]), ALU.mult)\
                    .then_inc(wdtx_made, 1)

            def convA(i, k):
                if k == 1:
                    pool.wait_ge(tap_made, i * 2 + 2)
                else:
                    pool.wait_ge(conv2_made, i * 3 + k - 1)
                pool.wait_ge(taps_made, i * 3 + k)
                pool.tensor_tensor(u[:, 1, k:], u[:, 1, k:], taps[k - 1][:, 0:TOK - k], ALU.add).then_inc(conv2_made, 1)

            def stepA(i, c, par, done, first=False, last=False):
                if c + 1 < CH - 1:
                    decayedA(i, c + 1)
                    pool.wait_ge(st_made, i * 3 + c + 1)
                    pool.tensor_tensor(Sd[:].rearrange("p (h d) -> p h d", h=HEADS),
                                       St[:].rearrange("p (h d) -> p h d", h=HEADS),
                                       dec_t[:, i, c + 1, :].unsqueeze(2).to_broadcast([P, HEADS, HD]), ALU.mult)\
                        .then_inc(sd_made, 1)
                elif c == CH - 1 and not last:
                    decayedA(i + 1, 0)
                if c == 1 and not last:
                    convA(i + 1, 1)
                if not (first and c == 0):
                    gateA(i * CH + c - 1, (c + 3) % CH, par if c > 0 else 1 - par)
                if c == 1 and not last:
                    convA(i + 1, 2)
                    convA(i + 1, 3)
                if c == 2 and not first:
                    done = res_scales(1, i - 1, done)
                if c == 1 and last:
                    done = scales(1, 0, done)
                return done

            def gateA(t, c, par):
                pool.wait_ge(yf_made, 2 * t + 2)
                pool.tensor_tensor(yf[:, c % 2], yf[:, c % 2], gz[par][:, :, cols(c)], ALU.mult).then_inc(yg_made, 1)

            def stageA(i, par, done, first=False, last=False):
                for c in range(CH):
                    done = stepA(i, c, par, done, first, last)
                return done

            for k in range(1, 4):
                convA(0, k)
            decayedA(0, 0)
            done = stageA(0, 0, done, first=True)
            for n, (lo, w, hi) in enumerate(((wff_lo, wff, wff_hi), (w4_lo, w4s, w4_hi), (wg_lo, wg, wg_hi))):
                pool.wait_ge(set_a, n + 3)
                pool.tensor_tensor(lo[:], w[:], hi[:].bitcast(F32), ALU.subtract).then_inc(wlo_made, 1)
            pool.wait_ge(rel_loaded, 16 * (P // GROUP))
            pool.affine_select(out=near[:], in_=near[:], compare_op=ALU.is_ge, fill=FAR, base=0,
                               pattern=[[1, P]], channel_multiplier=-1).then_inc(fillers, 1)

            with pool.Fori(1, SEQS - 2, 2) as i:
                stageA(i, 1, done + (i - 1) * STEPS_RES)
                stageA(i + 1, 0, done + i * STEPS_RES)
            done += (SEQS - 2) * STEPS_RES
            done = stageA(SEQS - 1, 1, done, last=True)
            gateA(NT - 1, CH - 1, 1)

            def stageB(i, done, nxt, first=False, last=False):
                for c in range(CH):
                    t = i * CH + c
                    pool.wait_ge(g_made, t * EXPERTS + 4 + BCREDIT)
                    b = gb[:, c % 2]
                    pool.tensor_tensor(b[:, 0:2], b[:, 0:2], b[:, 2:4], ALU.add).then_inc(half_made, 1)
                    if c == 0:
                        done = scales(*nxt, done)
                    pool.wait_ge(g_made, t * EXPERTS + 8 + BCREDIT)
                    pool.tensor_tensor(b[:, 4:6], b[:, 4:6], b[:, 6:8], ALU.add).then_inc(half_made, 1)
                    pool.wait_ge(half_made, t * 3 + 2)
                    pool.tensor_tensor(b[:, 0:2], b[:, 0:2], b[:, 4:6], ALU.add).then_inc(half_made, 1)
                    if c == 1 and first:
                        done = res_scales(1, SEQS - 1, done)
                    if c == 2 and last:
                        done = scales(2, 1, done)
                    elif c == 2 and not first:
                        done = res_scales(2, i - 1, done)
                return done

            both = STEPS[1] + STEPS_RES
            done = stageB(0, done, (1, 1), first=True)
            with pool.Fori(1, SEQS - 2, 2) as i:
                stageB(i, done + (i - 1) * both, (1, i + 1))
                stageB(i + 1, done + i * both, (1, i + 2))
            done += (SEQS - 2) * both
            done = stageB(SEQS - 1, done, (2, 0), last=True)
            done = res_scales(2, SEQS - 2, done)

            def stageC(i, done, nxt, first=False):
                done = scales(*nxt, done)
                if not first:
                    done = res_scales(3, i - 1, done)
                pool.wait_ge(cz_made, (i + 1) * CH)
                pool.tensor_tensor(z1[:], z1[:], bout_rows[:].unsqueeze(1).to_broadcast([P, CH, P]), ALU.add)\
                    .then_inc(czb_made, 1)
                return done

            both = STEPS[2] + STEPS_RES
            done = res_scales(2, SEQS - 1, done)
            done = stageC(0, done, (2, 2), first=True)
            with pool.Fori(1, SEQS - 2) as i:
                stageC(i, done + (i - 1) * both, (2, i + 2))
            done += (SEQS - 3) * both
            done = stageC(SEQS - 2, done, (3, 0))
            done = stageC(SEQS - 1, done, (3, 1))
            done = scales(3, 2, done)
            done = res_scales(3, SEQS - 1, done)

            def lastD(i):
                pool.wait_ge(ladd_made, (i + 1) * CH)
                pool.tensor_tensor(X[:, i], X[:, i], last_add[:], ALU.add).then_inc(x_final, 1)

            def stageD(i, done, first=0, last=False):
                if not last and first < 2:
                    done = scales(3, i + 2, done)
                if first < 1:
                    lastD(i - 2)
                if first < 2:
                    done = res_scales(4, i - 1, done)
                return done

            both = STEPS[3] + STEPS_RES
            done = stageD(0, done, first=2)
            done = stageD(1, done, first=1)
            with pool.Fori(2, SEQS - 2) as i:
                stageD(i, done + (i - 2) * both)
            done += (SEQS - 4) * both
            done = stageD(SEQS - 2, done, last=True)
            done = stageD(SEQS - 1, done, last=True)
            res_scales(4, SEQS - 1, done)
            lastD(SEQS - 2)

        @block.scalar
        def _(act):
            def hi(stage, i, par, free, value):
                act.wait_ge(zT_made, stage * SEQS + i + 1)
                if free is not None:
                    act.wait_ge(free, value)
                act.activation(ZT_hi[par][:], bank(5), ACT.Copy).then_inc(hi_made, 1)

            def z(stage, i, tiles=range(CH)):
                n = stage * SEQS + i
                if tiles[0] == 0:
                    wait_apart(act, scale_made, n + 1)
                    wait_apart(act, zT_made, n)
                k = 1 if stage in (0, 2) else 0
                for c in tiles:
                    act.activation(Z[:, c], X[:, i, c], ACT.Identity, bias=shift[:, c:c + 1],
                                   scale=rstds[:, k, c:c + 1]).then_inc(z_made, 1)

            def residual(stage, i, tiles=range(CH)):
                n = (stage - 1) * SEQS + i
                if tiles[0] == 0:
                    wait_apart(act, rrstd_made, n + 1 + LCREDIT)
                    wait_apart(act, x_new, n)
                for c in tiles:
                    act.activation(add[:, c], RES[:, i, c], ACT.Identity, bias=res_shift[:, i, c:c + 1],
                                   scale=res_rstd[:, i, c:c + 1]).then_inc(add_made, 1)

            def input_z(i, c, made):
                act.activation(z1[:, c], X[:, i, c], ACT.Identity, bias=x_shift[:, i, c:c + 1],
                               scale=x_rstd[:, i, c:c + 1]).then_inc(made, 1)

            act.wait_ge(early_loaded, 16 * NEARLY)
            act.activation(expA[:], alog[:], ACT.Exp).then_inc(expA_made, 1)
            act.wait_ge(set_v, 1)
            act.activation(w_in_hi[:], w_in[:], ACT.Copy).then_inc(set_a, 1)
            act.activation(w_dt[:, 0], w_in[:, 768:772], ACT.Copy).then_inc(set_a, 1)

            def w1_part(i):
                wait_apart(act, folded, i + 1)
                act.activation(w1_hi[:, i, :], w1[:, i, :], ACT.Copy).then_inc(w1hi_made, 1)

            def stage0(i, par, first=False, last=False):
                if not first:
                    act.wait_ge(dt_made, i - 1)
                hi(0, i, par, None if first else zT_stashed[par], (i - par) * 16)
                if not last:
                    z(0, i + 1)
                w1_part(i)

            z(0, 0)
            for par in range(2):
                stage0(par, par, first=True)
            with act.Fori(2, SEQS - 3, 2) as i:
                stage0(i, 0)
                stage0(i + 1, 1)
            stage0(SEQS - 2, 0)
            stage0(SEQS - 1, 1, last=True)
            act.wait_ge(step_v, 2)
            act.activation(sm[:, 1], sm[:, 0], ACT.Abs).then_inc(step_a, 1)
            act.wait_ge(step_a, 1)
            act.activation(sm[:, 2], sm[:, 1], ACT.Exp, scale=-1.0).then_inc(step_a, 1)

            def tapA(i, half):
                act.wait_ge(proj_made, i * 6 + half + 1)
                act.wait_ge(xc_made, i * 2)
                act.activation(u[:, half], bank(half), ACT.Identity, bias=convb[:, half:half + 1],
                               scale=convw[:, half, 3:4]).then_inc(tap_made, 1)
                if half == 1:
                    act.wait_ge(conv2_made, i * 3)
                    for k in range(1, 4):
                        act.activation(taps[k - 1], bank(1), ACT.Identity,
                                       scale=convw[:, 1, 3 - k:4 - k]).then_inc(taps_made, 1)

            act.wait_ge(set_v, 3)
            for half in range(2):
                tapA(0, half)

            def small(a):
                return a[:].rearrange("p s c h -> p (s c h)")

            act.wait_ge(cum_copied, 2)
            act.activation(small(ecum_t), sm[:, 3], ACT.Exp).then_inc(step_a, 1)
            act.activation(small(etail_t), sm[:, 4], ACT.Exp).then_inc(step_a, 1)
            act.activation(small(dec_t), bank(4)[:, 0:NC], ACT.Exp).then_inc(step_a, 1)

            def tanhA(i, half, par, free):
                act.wait_ge((conv_made, conv2_made)[half], i * 3 + 3)
                if free is not None:
                    act.wait_ge(yf_made, free)
                act.activation(xc[par][:, half], u[:, half], ACT.Tanh).then_inc(th_made, 1)

            def bcA(i, n, par):
                act.wait_ge(proj_made, i * 6 + 3 + n)
                if n == 0:
                    act.wait_ge(T_made, i * CH)
                    act.wait_ge(G_made, i)
                elif not isinstance(i, int) or i > 0:
                    act.wait_ge(Y_made, (i - 1) * CH)
                act.activation((Bf, Cf[par])[n][:], bank(n), ACT.Copy).then_inc(bc_made, 1)

            def tzA(i, half, par, free):
                act.wait_ge(proj_made, i * 6 + 5 + half)
                if free is not None:
                    act.wait_ge(yg_made, free)
                act.activation(gz[par][:, half], bank(half), ACT.Tanh, scale=0.5).then_inc(tz_made, 1)

            def decayA(i, c):
                act.wait_ge(D_made, i * CH + c + 1)
                act.wait_ge(Y_made, i * CH + max(c - 1, 0))
                act.activation(Edec[:, c % 2].rearrange("p h i -> p (h i)"), bank(4), ACT.Exp).then_inc(E_made, 1)
                if c < CH - 1:
                    act.wait_ge(dtx_made, i * CH + c + 1)
                    act.wait_ge(S_made, i * 3 + c)
                    act.activation(Btok[:], bank(3)[:, INNER:INNER + P], ACT.Copy).then_inc(btok_made, 1)

            def stepA(i, c, par, first=False, last=False):
                if c < CH - 1:
                    decayA(i, c + 1)
                if c == 0:
                    act.wait_ge(Y_made, i * CH + 1)
                    if not first:
                        act.wait_ge(YT_made, i * CH - 1)
                    act.activation(ytok[:, 0], bank(6)[:, 0:INNER], ACT.Copy).then_inc(y_made, 1)
                    act.wait_ge(S_made, i * 3 + 1)
                    act.activation(St[:], bank(7)[:, 0:INNER], ACT.Copy).then_inc(st_made, 1)
                if c == CH - 1 and not last:
                    decayA(i + 1, 0)
                if not last:
                    if c < 2:
                        tapA(i + 1, c)
                    if c == 2:
                        bcA(i + 1, 0, 1 - par)
                        bcA(i + 1, 1, 1 - par)
                    if c in (1, 2):
                        tanhA(i + 1, c - 1, 1 - par, i * CH * 2)
                    if c == 3:
                        tzA(i + 1, 0, 1 - par, i * CH)
                        tzA(i + 1, 1, 1 - par, i * CH)
                if last:
                    if c == 0:
                        residual(1, 0)
                    if c == 2:
                        z(1, 0)
                    if c == 3:
                        hi(1, 0, 0, zT_stashed[0], 16 * SEQS)
                if not first:
                    wait_apart(act, resA_made, (i - 1) * CH + c + 1)
                input_z(i, c, z1_made)

            def stageA(i, par, first=False, last=False):
                for c in range(CH):
                    stepA(i, c, par, first, last)

            for half in range(2):
                tanhA(0, half, 0, None)
            bcA(0, 0, 0)
            bcA(0, 1, 0)
            tzA(0, 0, 0, None)
            tzA(0, 1, 0, None)
            decayA(0, 0)
            for n, (h, w) in enumerate(((wff_hi, wff), (w4_hi, w4s), (wg_hi, wg))):
                act.wait_ge(set_v, (7, 9, 10)[n])
                act.activation(h[:], w[:], ACT.Copy).then_inc(set_a, 1)
            stageA(0, 0, first=True)
            with act.Fori(1, SEQS - 2, 2) as i:
                stageA(i, 1)
                stageA(i + 1, 0)
            stageA(SEQS - 1, 1, last=True)

            def gateB(i):
                act.wait_ge(gate_v, i * GATE_STEPS + 8)
                act.activation(ge[:, 1], ge[:, 0], ACT.Sigmoid).then_inc(gate_a, 1)
                act.activation(ge[:, 2], ge[:, 0], ACT.Sigmoid, scale=-1.0).then_inc(gate_a, 1)

            def accT_copy(t):
                act.wait_ge(accT_in_psum, t + 1)
                act.wait_ge(moe_made, t)
                act.activation(accT[:], bank(6)[:, 0:HID].rearrange("p (k n) -> p k n", k=2), ACT.Copy)\
                    .then_inc(accT_made, 1)

            def stageB(i, par, nxt, after, first=False, last=False):
                for c in range(CH):
                    t = i * CH + c
                    for e in range(EXPERTS):
                        n = t * EXPERTS + e
                        act.wait_ge(h_made, n + 1)
                        act.wait_ge(g_made, n + 1)
                        act.activation(sig[:, e % 4], bank(e % 4)[:, HID:2 * HID], ACT.Sigmoid).then_inc(sig_made, 1)
                        if e == 3 and not (first and c < 2):
                            accT_copy(t - 2)
                        if c == (2 if last else 3) and e < 4:
                            residual(*after, (e,))
                        if (c, e) in ((0, 7), (1, 0), (1, 1), (1, 2)):
                            z(*nxt, ((e + 1) % EXPERTS,))
                        if (c, e) == (1, 6):
                            hi(*nxt, 1 - par, h_made, i * 32)
                        if (c, e) == (2, 7) and not last:
                            gateB(i + 1)

            gateB(0)
            residual(1, 1)
            stageB(0, 0, (1, 1), (1, 2), first=True)
            with act.Fori(1, SEQS - 4, 2) as i:
                stageB(i, 1, (1, i + 1), (1, i + 2))
                stageB(i + 1, 0, (1, i + 2), (1, i + 3))
            stageB(SEQS - 3, 1, (1, SEQS - 2), (1, SEQS - 1))
            stageB(SEQS - 2, 0, (1, SEQS - 1), (2, 0))
            stageB(SEQS - 1, 1, (2, 0), (2, 1), last=True)
            accT_copy(NT - 2)

            def siluC(i, par, n):
                act.wait_ge(cproj_made, i * 5 + n + 1)
                if n == 0:
                    act.wait_ge(var_made, i * 4)
                    act.activation(qkf[:], bank(2), ACT.Silu).then_inc(cact_made, 1)
                elif n in (1, 4):
                    k = 1 if n == 1 else 0
                    if not isinstance(i, int) or i > 0:
                        act.wait_ge(o_made, (i - 1) * 2)
                    act.activation(vt[par][:, 2 * k:2 * k + 2, :], bank(3 + k).rearrange("p (c n) -> p c n", c=2),
                                   ACT.Silu).then_inc(cact_made, 1)
                else:
                    if not isinstance(i, int) or i > 0:
                        act.wait_ge(og_made, (i - 1) * 2)
                    act.activation(gt[par][:, n - 2], bank(n - 2), ACT.Silu).then_inc(cact_made, 1)

            def kvC(i, c):
                act.wait_ge(kv_made, i * 3 + c + 1)
                act.wait_ge(o_made, i * 2)
                act.activation(kvs[:, c], bank(3)[:, 0:HID], ACT.Copy, scale=1.0 / GROUP).then_inc(kvs_made, 1)

            def siluD(i, m):
                act.wait_ge(gu_made, i * 3 + m + 1)
                act.wait_ge(hf_made, i * 3 + m + 1)
                act.activation(sg[:, m], bank(GATE_BANKS[m]), ACT.Silu, scale=1.0 / 127).then_inc(sg_made, 1)

            def stageC(i, par, nxt, first=False, last=False):
                if not first:
                    residual(*nxt)
                act.wait_ge(lkT_made, i + 1)
                act.wait_ge(kv_made, i * 3)
                act.activation(lkt[:].rearrange("p c d -> p (c d)"), bank(2), ACT.Copy).then_inc(lkt_made, 1)
                if first:
                    residual(*nxt)
                for c in range(3):
                    kvC(i, c)
                    if c < 2 and not last:
                        siluC(i + 1, 1 - par, c)
                    if c < EARLY_D and last:
                        siluD(0, c)
                if not last:
                    siluC(i + 1, 1 - par, 2)
                    siluC(i + 1, 1 - par, 3)
                wait_apart(act, res_made, SEQS + i)
                for c in range(CH):
                    input_z(i, c, cz_made)
                z(*nxt)
                if not last:
                    siluC(i + 1, 1 - par, 4)
                hi(*nxt, par, cproj_made, (i + 1) * 5)

            for n in range(5):
                siluC(0, 0, n)
                if n == 1:
                    z(2, 1)
            hi(2, 1, 1, None, 0)
            accT_copy(NT - 1)
            stageC(0, 0, (2, 2), first=True)
            with act.Fori(1, SEQS - 4, 2) as i:
                stageC(i, 1, (2, i + 2))
                stageC(i + 1, 0, (2, i + 3))
            stageC(SEQS - 3, 1, (2, SEQS - 1))
            stageC(SEQS - 2, 0, (3, 0))
            stageC(SEQS - 1, 1, (3, 1), last=True)

            def residD(i):
                wait_apart(act, dn_made, i + 1)
                act.activation(RES[:, i].rearrange("p c d -> p (c d)"), bank(7), ACT.Copy).then_inc(resD_made, 1)

            def stageD(i, par, first=0, last=0):
                if last < 1:
                    residual(3, i + 2)
                if first < 2 and last < 2:
                    z(3, i + 1)
                for m in range(EARLY_D if first == 2 else 0, 3):
                    siluD(i, m)
                if first < 2 and last < 2:
                    hi(3, i + 1, 1 - par, gu_made, i * 3)
                if first < 2:
                    residD(i - 1)

            stageD(0, 0, first=2)
            stageD(1, 1, first=1)
            with act.Fori(2, SEQS - 3, 2) as i:
                stageD(i, 0)
                stageD(i + 1, 1)
            stageD(SEQS - 2, 0, last=1)
            stageD(SEQS - 1, 1, last=2)
            residD(SEQS - 1)

        @block.vector
        def _(dve):
            def apart(semaphore, value):
                wait_apart(dve, semaphore, value)

            def stats(stage, i):
                bn_stats(stage, i)
                bn_aggr(stage, i)

            def bn_stats(stage, i):
                n = stage * SEQS + i
                apart(mv_made, n * CH)
                if stage > 0:
                    apart(x_new, n - SEQS + 1)
                for c in range(CH):
                    dve.bn_stats(stats_t[:, c], X[:, i, c]).then_inc(stats_made, 1)

            def bn_aggr(stage, i):
                n = stage * SEQS + i
                apart(stats_made, (n + 1) * CH)
                apart(scale_made, n)
                for c in range(CH):
                    dve.bn_aggr(mv[:, c], stats_t[:, c]).then_inc(mv_made, 1)

            def x_add(stage, i):
                n = (stage - 1) * SEQS + i
                dve.wait_ge(add_made, (n + 1) * CH)
                dve.tensor_tensor(X[:, i], X[:, i], add[:], ALU.add).then_inc(x_new, 1)

            def lo(stage, i, par):
                dve.wait_ge(hi_made, stage * SEQS + i + 1)
                dve.tensor_tensor(ZT_lo[par][:], bank(5), ZT_hi[par][:].bitcast(F32), ALU.subtract).then_inc(lo_made, 1)

            def rstats(stage, i):
                rbn_stats(stage, i)
                rbn_aggr(stage, i)

            def rbn_stats(stage, i):
                n = (stage - 1) * SEQS + i
                apart(rmv_made, n * CH + LCREDIT)
                if stage == 1:
                    apart(resA_made, (i + 1) * CH)
                elif stage < 4:
                    apart(res_made, n - SEQS + 1)
                else:
                    apart(resD_made, i + 1)
                for c in range(CH):
                    dve.bn_stats(rstats_t[:, c], RES[:, i, c]).then_inc(rstats_made, 1)

            def rbn_aggr(stage, i):
                n = (stage - 1) * SEQS + i
                apart(rstats_made, (n + 1) * CH)
                apart(rrstd_made, n + LCREDIT)
                for c in range(CH):
                    dve.bn_aggr(rmv[:, c], rstats_t[:, c]).then_inc(rmv_made, 1)

            dve.memset(credit[:, 0:1], 0.0).then_inc(g_made, BCREDIT)
            dve.memset(credit[:, 1:2], 0.0).then_inc(hf_made, DCREDIT)
            dve.memset(credit[:, 2:3], 0.0).then_inc(rmv_made, LCREDIT)
            dve.memset(credit[:, 3:4], 0.0).then_inc(rrstd_made, LCREDIT)
            dve.memset(credit[:, 4:5], 0.0).then_inc(x_final, LCREDIT)

            dve.wait_ge(x_loaded, 16)
            stats(0, 0)
            dve.wait_ge(early_loaded, 16 * NEARLY)
            dve.tensor_scalar(w_in[:], w_in[:], normw[:], None, ALU.mult).then_inc(set_v, 1)
            stats(0, 1)

            def w1lo(i):
                dve.wait_ge(w1hi_made, i + 1)
                dve.tensor_tensor(w1_lo[:, i, :], w1[:, i, :], w1_hi[:, i, :].bitcast(F32), ALU.subtract)\
                   .then_inc(w1lo_made, 1)

            def stage0(i, par, first=False, last=False):
                if not last:
                    if par == 0:
                        dve.wait_ge(x_loaded, (i + 4) * 8)
                    stats(0, i + 2)
                lo(0, i, par)
                if not first:
                    w1lo(i - 1)
                dve.wait_ge(fold_made, i + 1)
                dve.tensor_tensor(w1[:, i, :], w1[:, i, :], bank(par), ALU.add).then_inc(folded, 1)

            stage0(0, 0, first=True)
            stage0(1, 1)
            with dve.Fori(2, SEQS - 3, 2) as i:
                stage0(i, 0)
                stage0(i + 1, 1)
            dve.tensor_scalar(convw[:], convw[:], 0.5, None, ALU.mult).then_inc(set_v, 1)
            dve.tensor_scalar(convb[:], convb[:], 0.5, None, ALU.mult).then_inc(set_v, 1)

            def other_weights():
                dve.wait_ge(weights_loaded, 16 * NLOADS)
                dve.tensor_scalar(w_out[:], w_out[:], 0.5, None, ALU.mult).then_inc(set_v, 1)
                dve.tensor_scalar(w4s[:], w4[:, 0:640], lnw[:], None, ALU.mult).then_inc(set_v, 1)
                dve.tensor_scalar(lnb_avg[:], allneg[:], lnb[:], -1.0 / P, ALU.mult, ALU.mult).then_inc(set_v, 1)
                dve.memset(shifted[:], 0.0).then_inc(shifted_made, 1)
                dve.wait_ge(shifted_made, 1)
                root = float(P) ** 0.5
                dve.tensor_scalar(shifted[:, 0:16], table[:, 0:16], root, None, ALU.mult).then_inc(shifted_made, 1)
                for k in sorted(set(BUCKETS[16:])):
                    first, many = BUCKETS.index(k), BUCKETS.count(k)
                    dve.tensor_scalar(shifted[:, first:first + many], table[:, k:k + 1].to_broadcast([GROUP, many]),
                                      root, None, ALU.mult).then_inc(shifted_made, 1)
                dve.tensor_copy(wffn[:], wffn_i).then_inc(set_v, 1)

            other_weights()
            stage0(SEQS - 2, 0, last=True)
            stage0(SEQS - 1, 1, last=True)
            w1lo(SEQS - 1)

            cb = lambda a: a.unsqueeze(1).to_broadcast([P, NT, HEADS])
            th3 = lambda a: a.rearrange("p (t h) -> p t h", h=HEADS)
            flat = lambda a: a[:].rearrange("p s c h -> p (s c h)")
            steps = [0]

            def step(ins):
                steps[0] += 1
                ins.then_inc(step_v, 1)
                dve.wait_ge(step_v, steps[0])

            dve.wait_ge(dt_made, SEQS)
            dt_raw = bank(2)[:, 0:2 * NC].rearrange("p (t k h) -> p t k h", k=2, h=HEADS)
            step(dve.tensor_tensor(th3(sm[:, 0]), dt_raw[:, :, 0], cb(dtb[:]), ALU.add))
            step(dve.tensor_tensor(th3(sm[:, 0]), th3(sm[:, 0]), dt_raw[:, :, 1], ALU.add))
            dve.wait_ge(step_a, 2)
            step(dve.tensor_scalar(sm[:, 5], sm[:, 2], 2.0, None, ALU.add))
            step(dve.reciprocal(sm[:, 6], sm[:, 5]))
            step(dve.tensor_tensor(sm[:, 7], sm[:, 2], sm[:, 6], ALU.mult))
            step(dve.tensor_tensor(sm[:, 5], sm[:, 7], sm[:, 7], ALU.mult))
            step(dve.tensor_scalar(sm[:, 6], sm[:, 5], 1.0 / 15, None, ALU.mult))
            for k in (13, 11, 9, 7, 5, 3):
                step(dve.scalar_tensor_tensor(sm[:, 6], sm[:, 6], 1.0 / k, sm[:, 5], ALU.add, ALU.mult))
            step(dve.scalar_tensor_tensor(sm[:, 6], sm[:, 6], 1.0, sm[:, 7], ALU.add, ALU.mult))
            step(dve.tensor_scalar(sm[:, 1], sm[:, 0], 0.0, None, ALU.max))
            step(dve.scalar_tensor_tensor(flat(dt_t), sm[:, 6], 2.0, sm[:, 1], ALU.mult, ALU.add))
            dve.wait_ge(expA_made, 1)
            step(dve.tensor_tensor(th3(sm[:, 7]), th3(flat(dt_t)), cb(expA[:]), ALU.mult))
            assert steps[0] == 17
            def convA(i, k):
                if k == 1:
                    dve.wait_ge(tap_made, i * 2 + 1)
                else:
                    dve.wait_ge(conv_made, i * 3 + k - 1)
                dve.scalar_tensor_tensor(u[:, 0, k:], bank(0)[:, 0:TOK - k], convw[:, 0, 3 - k:4 - k],
                                         u[:, 0, k:], ALU.mult, ALU.add).then_inc(conv_made, 1)

            convA(0, 1)
            dve.wait_ge(cum_in_psum, 2)
            dve.tensor_copy(sm[:, 3], bank(3)[:, 0:NC]).then_inc(cum_copied, 1)
            dve.wait_ge(cum_copied, 1)
            dve.tensor_tensor(sm[:, 4], bank(4)[:, 0:NC], sm[:, 3], ALU.subtract).then_inc(cum_copied, 1)
            dve.tensor_copy(cparts[:, 0], sm[:, 3]).then_inc(parts_made, 1)
            dve.wait_ge(parts_made, 1)
            dve.tensor_tensor(sm[:, 5], sm[:, 3], cparts[:, 0], ALU.subtract).then_inc(parts_made, 1)
            dve.wait_ge(parts_made, 2)
            dve.tensor_copy(cparts[:, 1], sm[:, 5]).then_inc(parts_made, 1)
            dve.wait_ge(parts_made, 3)
            dve.tensor_tensor(sm[:, 6], sm[:, 5], cparts[:, 1], ALU.subtract).then_inc(parts_made, 1)
            dve.wait_ge(parts_made, 4)
            dve.tensor_copy(cparts[:, 2], sm[:, 6]).then_inc(parts_made, 1)
            convA(0, 2)
            dve.wait_ge(partsT_in_psum, 1)
            dve.tensor_copy(cpartsT[:], bank(5).bitcast(BF16)[:, 0:3 * P].rearrange("p (q n) -> p q n", q=3))\
               .then_inc(parts_made, 1)

            def add_biases():
                dve.wait_ge(set_t, 1)
                dve.tensor_tensor(w4s[:, 0:512], w4s[:, 0:512], bank(7), ALU.add).then_inc(set_v, 1)
                dve.tensor_tensor(w4s[:, 512:640], w4s[:, 512:640], bank(6)[:, 0:P], ALU.add).then_inc(set_v, 1)
                dve.tensor_tensor(wg[:], wg[:], bank(6)[:, P:P + EXPERTS], ALU.add).then_inc(set_v, 1)

            def heads(a):
                return a.rearrange("p (h d) -> p h d", h=HEADS)

            def byhead(a, i, c):
                return a[:, i, c, :].unsqueeze(2).to_broadcast([P, HEADS, HD])

            def xcA(i, par, half):
                dve.wait_ge(th_made, i * 2 + half + 1)
                dve.scalar_tensor_tensor(xc[par][:, half], xc[par][:, half], 1.0, u[:, half], ALU.add, ALU.mult)\
                   .then_inc(xc_made, 1)

            def gzA(i, par, half):
                dve.wait_ge(tz_made, i * 2 + half + 1)
                dve.scalar_tensor_tensor(gz[par][:, half], gz[par][:, half], 1.0, bank(half), ALU.add, ALU.mult)\
                   .then_inc(gz_made, 1)

            def chunk_in(i, c):
                t = i * CH + c
                dve.wait_ge(T_made, t + 1)
                dve.wait_ge(Y_made, i * CH + max(c - 1, 0))
                dve.wait_ge(wdtx_made, i * 3 + max(c - 1, 0))
                dve.tensor_tensor(heads(dtx[:, c % 2]), heads(bank(3)[:, 0:INNER]), byhead(dt_t, i, c), ALU.mult)\
                   .then_inc(dtx_made, 1)

            def decayed(i, c):
                dve.wait_ge(E_made, i * CH + c + 1)
                dve.wait_ge(G_made, i + 1)
                dve.tensor_tensor(Mdec[:, c % 2], Edec[:, c % 2],
                                  bank(5)[:, cols(c)].unsqueeze(1).to_broadcast([P, HEADS, P]), ALU.mult)\
                   .then_inc(M_made, 1)

            def residA(t, i, c):
                dve.wait_ge(out_made, t + 1)
                dve.wait_ge(z1_made, t + 1)
                dve.tensor_tensor(RES[:, i, c], z1[:, c], bank(7)[:, 0:P], ALU.add).then_inc(resA_made, 1)

            def yfA(t, c, par, ring):
                dve.wait_ge(YT_made, t + 1)
                if ring:
                    dve.wait_ge(out_made, t - 1)
                for half in range(2):
                    dve.scalar_tensor_tensor(yf[:, c % 2, half], xc[par][:, half, cols(c)], dskip[:, half:half + 1],
                                             bank(2)[:, cols(half)], ALU.mult, ALU.add).then_inc(yf_made, 1)

            def stepA(i, c, par, first=False, last=False):
                t = i * CH + c
                if c < CH - 1:
                    chunk_in(i, c + 1)
                    decayed(i, c + 1)
                if c > 0:
                    dve.wait_ge(Y_made, t + 1)
                    if not (first and c < 2):
                        dve.wait_ge(YT_made, t - 1)
                    dve.tensor_tensor(heads(ytok[:, c % 2]), heads(bank(6)[:, INNER:2 * INNER]), byhead(ecum_t, i, c),
                                      ALU.mult).then_inc(y1_made, 1)
                    if c < CH - 1:
                        dve.wait_ge(S_made, i * 3 + c + 1)
                        dve.wait_ge(sd_made, i * 2 + c)
                        dve.tensor_tensor(St[:], Sd[:], bank(7)[:, 0:INNER], ALU.add).then_inc(st_made, 1)
                    dve.wait_ge(y1_made, i * 3 + c)
                    dve.tensor_tensor(ytok[:, c % 2], ytok[:, c % 2], bank(6)[:, 0:INNER], ALU.add).then_inc(y_made, 1)
                if c == 0 and not last:
                    convA(i + 1, 1)
                if c == CH - 1 and not last:
                    chunk_in(i + 1, 0)
                    decayed(i + 1, 0)
                if not (first and c < 2):
                    residA(t - 2, i if c >= 2 else i - 1, (c + 2) % CH)
                if c == 0 and not last:
                    convA(i + 1, 2)
                if not (first and c == 0):
                    yfA(t - 1, (c + 3) % CH, par if c > 0 else 1 - par, not (first and c < 3))
                if c == 0 and not last:
                    convA(i + 1, 3)
                if c == 1 and not last:
                    xcA(i + 1, 1 - par, 0)
                if c == 2 and not last:
                    xcA(i + 1, 1 - par, 1)
                if c == CH - 1 and not last:
                    gzA(i + 1, 1 - par, 0)
                    gzA(i + 1, 1 - par, 1)
                if last:
                    if c == 0:
                        x_add(1, 0)
                        bn_stats(1, 0)
                    if c == 1:
                        bn_aggr(1, 0)
                    if c == 3:
                        lo(1, 0, 0)
                if c == 1 and not first:
                    rbn_stats(1, i - 1)
                if c == 2 and not first:
                    rbn_aggr(1, i - 1)

            def stageA(i, par, first=False, last=False):
                for c in range(CH):
                    stepA(i, c, par, first, last)

            convA(0, 3)
            xcA(0, 0, 0)
            xcA(0, 0, 1)
            add_biases()
            gzA(0, 0, 0)
            gzA(0, 0, 1)
            chunk_in(0, 0)
            decayed(0, 0)
            stageA(0, 0, first=True)
            with dve.Fori(1, SEQS - 2, 2) as i:
                stageA(i, 1)
                stageA(i + 1, 0)
            stageA(SEQS - 1, 1, last=True)
            residA(NT - 2, SEQS - 1, CH - 2)
            yfA(NT - 1, CH - 1, 1, True)

            def gateB(i, par, part):
                g = [i * GATE_STEPS + GATE_AT[part]]

                def step(ins):
                    g[0] = g[0] + 1
                    ins.then_inc(gate_v, 1)

                def after():
                    dve.wait_ge(gate_v, g[0])

                def bc(a):
                    return a.to_broadcast([P, CH, EXPERTS])

                below, sg1, sg2, ex = (ge[:, k] for k in range(4))
                total, both, first, sum2 = (gs[:, k] for k in range(4))
                e2 = ex[:, :, EXPERTS]
                sides = bank(4)[:, 0:CH * 2 * EXPERTS].rearrange("p (c k e) -> p c k e", c=CH, k=2)
                if part == 0:
                    dve.wait_ge(logits_made, i + 1)
                    step(dve.tensor_copy(lg[:], sides[:, :, 0]))
                elif part == 1:
                    after()
                    step(dve.tensor_tensor(lg[:], lg[:], sides[:, :, 1], ALU.add))
                    apart(gate_v, g[0])
                    for c in range(CH):
                        step(dve.max(top[:, c], lg[:, c]))
                elif part == 2:
                    after()
                    step(dve.tensor_tensor(below[:, :, 0:EXPERTS], lg[:], bc(top[:, :, 0:1]), ALU.subtract))
                    step(dve.tensor_tensor(below[:, :, EXPERTS:], top[:, :, 1:2], top[:, :, 0:1], ALU.subtract))
                    for c in range(CH):
                        step(dve.max_index(topi[:, c], top[:, c], lg[:, c]))
                elif part == 3:
                    after()
                    step(dve.tensor_copy(topf[:], topi[:, :, 0:2]))
                elif part == 4:
                    after()
                    iota_b = iota8[:].unsqueeze(1).to_broadcast([P, CH, EXPERTS])
                    step(dve.tensor_tensor(pick[:, 0], iota_b, bc(topf[:, :, 0:1]), ALU.is_equal))
                    step(dve.tensor_tensor(pick[:, 1], iota_b, bc(topf[:, :, 1:2]), ALU.is_equal))
                elif part == 5:
                    dve.wait_ge(gate_a, (i + 1) * 2)
                    step(dve.reciprocal(ex, sg2))
                elif part == 6:
                    after()
                    step(dve.tensor_tensor(ex, ex, sg1, ALU.mult))
                elif part == 7:
                    after()
                    step(dve.reduce_sum(total, ex[:, :, 0:EXPERTS], AX.X))
                elif part == 8:
                    after()
                    step(dve.scalar_tensor_tensor(both, total, TOP_EPS, e2, ALU.mult, ALU.add))
                    step(dve.tensor_tensor(pick[:, 1], pick[:, 1], bc(ex[:, :, EXPERTS:]), ALU.mult))
                elif part == 9:
                    after()
                    step(dve.tensor_scalar(both, both, 1.0, None, ALU.add))
                    step(dve.tensor_scalar(sum2, e2, 1.0, None, ALU.add))
                    step(dve.tensor_tensor(pick[:, 0], pick[:, 0], pick[:, 1], ALU.add))
                elif part == 10:
                    after()
                    step(dve.reciprocal(first, both))
                elif part == 11:
                    after()
                    step(dve.tensor_tensor(csum[par][:], sum2, first, ALU.mult))
                    step(dve.tensor_tensor(comb[par][:], pick[:, 0], bc(first.unsqueeze(2)), ALU.mult))
                    after()

            def accB(t, k, free):
                dve.wait_ge(half_made, (t + 1) * 3)
                if free:
                    dve.wait_ge(accT_in_psum, t - 1)
                dve.tensor_tensor(acc[k][:], gb[:, k, 0], gb[:, k, 1], ALU.add).then_inc(acc_made, 1)

            def residB(i, par, tiles, done):
                dve.wait_ge(moe_made, (i + 1) * CH)
                for c in tiles:
                    ins = dve.scalar_tensor_tensor(RES[:, i, c], bo_rows[:], csum[par][:, c:c + 1], bank(7)[:, cols(c)],
                                                   ALU.mult, ALU.add)
                if done:
                    ins.then_inc(res_made, 1)

            GATE_PLACES = [(2, 4), (2, 5), (2, 6), (2, 7), (3, 0), (3, 1), (3, 2), (3, 3), (3, 4), (3, 5), (3, 6), (3, 7)]

            def stageB(i, par, first=False, last=False):
                for c in range(CH):
                    t = i * CH + c
                    for e in range(EXPERTS):
                        dve.wait_ge(sig_made, t * EXPERTS + e + 1)
                        if e == 0 and not (first and c < 2):
                            dve.wait_ge(acc_made, t - 1)
                        dve.scalar_tensor_tensor(gb[:, c % 2, e], bank(e % 4)[:, 0:HID], comb[par][:, c, e:e + 1],
                                                 sig[:, e % 4], ALU.mult, ALU.mult).then_inc(g_made, 1)
                        if e == 5 and not (first and c == 0):
                            accB(t - 1, (c + 1) % 2, not (first and c < 3))
                        nxt = (2, 0) if last else (1, i + 1)
                        if (c, e) == (0, 0):
                            x_add(*nxt)
                        if (c, e) == (0, 1):
                            bn_stats(*nxt)
                        if (c, e) == (0, 3):
                            bn_aggr(*nxt)
                        if (c, e) == (1, 6):
                            lo(*nxt, 1 - par)
                        if last and (c, e) == (2, 5):
                            x_add(2, 1)
                        if last and (c, e) == (2, 6):
                            bn_stats(2, 1)
                        if last and (c, e) == (3, 0):
                            bn_aggr(2, 1)
                        for part, place in enumerate(GATE_PLACES):
                            if place == (c, e) and not last:
                                gateB(i + 1, 1 - par, part)
                        if first and (c, e) == (1, 4):
                            rstats(1, SEQS - 1)
                        if not first:
                            if (c, e) == (1, 7):
                                residB(i - 1, 1 - par, (0, 1), False)
                            if (c, e) == (2, 1):
                                residB(i - 1, 1 - par, (2, 3), True)
                            if (c, e) == (2, 2):
                                rbn_stats(2, i - 1)
                            if (c, e) == (2, 3):
                                rbn_aggr(2, i - 1)

            dve.wait_ge(z1_made, NT)
            for part in range(len(GATE_PLACES)):
                gateB(0, 0, part)
                if part == 4:
                    residA(NT - 1, SEQS - 1, CH - 1)
            stageB(0, 0, first=True)
            with dve.Fori(1, SEQS - 2, 2) as i:
                stageB(i, 1)
                stageB(i + 1, 0)
            stageB(SEQS - 1, 1, last=True)
            accB(NT - 1, 1, True)

            def variants(i, par):
                dve.wait_ge(cact_made, i * 5 + 1)
                if not isinstance(i, int) or i > 0:
                    dve.wait_ge(o_made, (i - 1) * 2)
                for k in (2, 0, 3, 1):
                    dve.tensor_scalar(qv[par][:, k], qkf[:], qkw[:, k:k + 1], qkb[:, k:k + 1], ALU.mult, ALU.add)\
                       .then_inc(var_made, 1)

            def residC(i):
                dve.wait_ge(czb_made, i + 1)
                dve.wait_ge(cout_made, i + 1)
                dve.tensor_tensor(RES[:, i], z1[:], bank(5).rearrange("p (c d) -> p c d", c=CH), ALU.add)\
                   .then_inc(res_made, 1)

            def gatedD(i, m, par):
                dve.wait_ge(sg_made, i * 3 + m + 1)
                dve.scalar_tensor_tensor(hf[par][:, m], bank(UP_BANKS[m]), 1.0 / (127 * 127), sg[:, m],
                                         ALU.mult, ALU.mult).then_inc(hf_made, 1)

            def stageC(i, par, nxt, first=False, last=False):
                quad = at[:, 0].rearrange("p (c i) -> p c i", c=CH)
                lin = at[:, 1].rearrange("p (c i) -> p c i", c=CH)
                dve.wait_ge(s1_made, i + 1)
                dve.scalar_tensor_tensor(quad, bank(6).rearrange("p (c i) -> p c i", c=CH), 1.0 / GROUP,
                                         near[:].unsqueeze(1).to_broadcast([P, CH, P]), ALU.mult, ALU.add)\
                   .then_inc(att_made, 1)
                dve.wait_ge(s2_made, i + 1)
                dve.tensor_tensor(lin, bank(7).rearrange("p (c i) -> p c i", c=CH),
                                  before[:].unsqueeze(1).to_broadcast([P, CH, P]), ALU.mult).then_inc(att_made, 1)
                dve.wait_ge(att_made, i * 4 + 1)
                dve.scalar_tensor_tensor(at[:, 0], at[:, 0], 0.0, at[:, 0], ALU.max, ALU.mult).then_inc(att_made, 1)
                x_add(*nxt)
                dve.wait_ge(att_made, i * 4 + 3)
                dve.tensor_tensor(at[:, 0], at[:, 0], at[:, 1], ALU.add).then_inc(att_made, 1)
                bn_stats(*nxt)
                if not first:
                    residC(i - 1)
                bn_aggr(*nxt)
                if not last:
                    variants(i + 1, 1 - par)
                if not first:
                    rstats(3, i - 1)
                if last:
                    for m in range(EARLY_D):
                        gatedD(0, m, 0)
                for half in range(2):
                    dve.wait_ge(o_made, i * 2 + half + 1)
                    dve.wait_ge(cact_made, i * 5 + 3 + half)
                    dve.wait_ge(cout_made, i)
                    dve.tensor_tensor(og[:, half], bank(6 + half), gt[par][:, half], ALU.mult).then_inc(og_made, 1)
                lo(*nxt, par)

            variants(0, 0)
            lo(2, 1, 1)
            residB(SEQS - 1, 1, range(CH), True)
            rstats(2, SEQS - 1)
            dve.wait_ge(fillers, 7)
            stageC(0, 0, (2, 2), first=True)
            with dve.Fori(1, SEQS - 4, 2) as i:
                stageC(i, 1, (2, i + 2))
                stageC(i + 1, 0, (2, i + 3))
            stageC(SEQS - 3, 1, (2, SEQS - 1))
            stageC(SEQS - 2, 0, (3, 0))
            stageC(SEQS - 1, 1, (3, 1), last=True)
            x_add(3, 2)
            bn_stats(3, 2)
            residC(SEQS - 1)
            bn_aggr(3, 2)
            rstats(3, SEQS - 1)

            def lastD(i):
                apart(rrstd_made, 3 * SEQS + i + 1 + LCREDIT)
                apart(x_final, i + LCREDIT)
                for c in range(CH):
                    dve.tensor_scalar(last_add[:, c], RES[:, i, c], res_rstd[:, i, c:c + 1], res_shift[:, i, c:c + 1],
                                      ALU.mult, ALU.add).then_inc(ladd_made, 1)

            def stageD(i, par, first=0, last=0):
                for m in range(3):
                    if m == 0 and first < 2 and last < 1:
                        x_add(3, i + 2)
                    if first < 1:
                        dve.wait_ge(dn_made, i - 1)
                    if first < 2 or m >= EARLY_D:
                        gatedD(i, m, par)
                    if m == 0 and first < 2 and last < 1:
                        bn_stats(3, i + 2)
                    if m == 1 and first < 2 and last < 1:
                        bn_aggr(3, i + 2)
                if first < 2 and last < 2:
                    lo(3, i + 1, 1 - par)
                if first < 1:
                    lastD(i - 2)
                if first < 2:
                    rstats(4, i - 1)

            stageD(0, 0, first=2)
            stageD(1, 1, first=1)
            with dve.Fori(2, SEQS - 3, 2) as i:
                stageD(i, 0)
                stageD(i + 1, 1)
            stageD(SEQS - 2, 0, last=1)
            stageD(SEQS - 1, 1, last=2)
            rstats(4, SEQS - 1)
            lastD(SEQS - 2)
            lastD(SEQS - 1)
            dve.wait_ge(ladd_made, SEQS * CH)
            dve.wait_ge(x_final, SEQS - 1 + LCREDIT)
            dve.tensor_tensor(X[:, SEQS - 1], X[:, SEQS - 1], last_add[:], ALU.add).then_inc(x_final, 1)

        @block.tensor
        def _(pe):
            def split3(dst, lhs, rhs, start=True, stop=True):
                (lh, ll), (rh, rl) = lhs, rhs
                pe.matmul(dst, lh, rh, start=start, stop=False)
                pe.matmul(dst, lh, rl, start=False, stop=False)
                return pe.matmul(dst, ll, rh, start=False, stop=stop)

            def zT(stage, i, free, value):
                n = stage * SEQS + i
                pe.wait_ge(z_made, (n + 1) * CH)
                pe.wait_ge(lo_made, n)
                if free is not None:
                    pe.wait_ge(free, value)
                for c in range(CH):
                    ins = pe.transpose(bank(5)[:, cols(c)], Z[:, c], ident[:])
                ins.then_inc(zT_made, 1)

            def zt(par, c=None):
                part = slice(0, TOK) if c is None else cols(c)
                return ZT_hi[par][:, part], ZT_lo[par][:, part]

            pe.wait_ge(consts, 5)

            def stage0(i, par):
                zT(0, i, None, None)
                pe.wait_ge(w1_loaded, (i + 2) * 8 if par == 0 else (i + 1) * 8)
                pe.wait_ge(early_loaded, 16 * NEARLY)
                pe.wait_ge(folded, max(i - 1, 0) if isinstance(i, int) else i - 1)
                pe.matmul(bank(par), negavg[:], w1[:, i, :], start=True, stop=False)
                pe.matmul(bank(par), avgrow[:], b1r[:, i, :], start=False, stop=True).then_inc(fold_made, 1)
                pe.wait_ge(lo_made, i + 1)
                pe.wait_ge(wlo_made, 2)
                for c in range(CH):
                    dst = bank(2)[:, 0:2 * NC].rearrange("p (s c r) -> p s c r", s=SEQS, c=CH)[:, i, c]
                    zh, zl = zt(par, c)
                    pe.matmul(dst[:, 0:2 * HEADS], zh, w_dt[:].rearrange("p k h -> p (k h)"), start=True, stop=False,
                              skip_group_check=True)
                    ins = pe.matmul(dst[:, 0:HEADS], zl, w_dt[:, 0], start=False, stop=True, skip_group_check=True)
                ins.then_inc(dt_made, 1)

            for par in range(2):
                stage0(par, par)
            with pe.Fori(2, SEQS - 1, 2) as i:
                stage0(i, 0)
                stage0(i + 1, 1)
            def bias_products():
                pe.wait_ge(set_v, 6)
                for dst, part in ((bank(7), slice(0, 512)), (bank(6)[:, 0:P], slice(512, 640))):
                    pe.matmul(dst, lnb_avg[:], w4[:, part], start=True, stop=False)
                    pe.matmul(dst, avgrow[:], b4r[:, part], start=False, stop=False)
                    pe.matmul(dst, negavg[:], w4s[:, part], start=False, stop=True)
                pe.matmul(bank(6)[:, P:P + EXPERTS], negavg[:], wg[:], start=True, stop=True).then_inc(set_t, 1)

            PROJ = [256, 384, 512, 640, 0, 128]

            def projA(i, k):
                used = [(gz_made, i * 2 - 1), (gz_made, i * 2), (conv_made, i * 3 + 3), (taps_made, i * 3 + 3),
                        (bc_made, i * 2 + 1), (bc_made, i * 2 + 2)][k]
                if not (k < 2 and isinstance(i, int) and i == 0):
                    pe.wait_ge(*used)
                col = PROJ[k]
                split3(bank(k % 2), (w_in_hi[:, col:col + P], w_in_lo[:, col:col + P]),
                       (XT_hi[:, i, :], XT_lo[:, i, :])).then_inc(proj_made, 1)

            def chunk_in(i, c, par):
                t = i * CH + c
                if c == 0:
                    pe.wait_ge(xc_made, i * 2 + 2)
                    pe.wait_ge(bc_made, i * 2 + 1)
                pe.wait_ge(dtx_made, t)
                pe.wait_ge(btok_made, i * 3 + c)
                for half in range(2):
                    ins = pe.transpose(bank(3)[:, cols(half)], xc[par][:, half, cols(c)], ident[:])
                if c < CH - 1:
                    ins = pe.transpose(bank(3)[:, INNER:INNER + P], Bf[:, cols(c)], ident[:])
                ins.then_inc(T_made, 1)
                pe.wait_ge(E_made, t)
                pe.matmul(bank(4), identb[:], far4[:].rearrange("p h i -> p (h i)"), start=True, stop=False)
                pe.matmul(bank(4), parts[:, t, :], headrows_neg[:].rearrange("p h i -> p (h i)"), start=False, stop=False)
                for h in range(HEADS):
                    ins = pe.matmul(bank(4)[:, cols(h)], headrows[:, h, :], parts[:, t, :], start=False,
                                    stop=h == HEADS - 1)
                ins.then_inc(D_made, 1)

            def pairsA(i, par):
                pe.wait_ge(bc_made, i * 2 + 2)
                pe.wait_ge(M_made, i * CH)
                for c in range(CH):
                    ins = pe.matmul(bank(5)[:, cols(c)], Bf[:, cols(c)], Cf[par][:, cols(c)], start=True, stop=True)
                ins.then_inc(G_made, 1)

            def outA(t, c):
                pe.wait_ge(yg_made, t + 1)
                for half in range(2):
                    ins = pe.matmul(bank(7)[:, 0:P], yf[:, c % 2, half], w_out[:, half], start=half == 0, stop=half == 1)
                ins.then_inc(out_made, 1)

            def yT_A(t, c):
                pe.wait_ge(y_made, t + 1)
                pe.wait_ge(yf_made, 2 * t)
                for half in range(2):
                    ins = pe.transpose(bank(2)[:, cols(half)], ytok[:, c % 2, cols(half)], ident[:])
                ins.then_inc(YT_made, 1)

            def stepA(i, c, par, first=False, last=False):
                t = i * CH + c
                if c < CH - 1:
                    chunk_in(i, c + 1, par)
                pe.wait_ge(M_made, t + 1)
                pe.wait_ge(y_made, t)
                for h in range(HEADS):
                    ins = pe.matmul(bank(6)[:, h * HD:(h + 1) * HD], Mdec[:, c % 2, h],
                                    dtx[:, c % 2, h * HD:(h + 1) * HD], start=True, stop=True)
                if c > 0:
                    pe.wait_ge(st_made, i * 3 + c)
                    ins = pe.matmul(bank(6)[:, INNER:2 * INNER], Cf[par][:, cols(c)], St[:], start=True, stop=True)
                ins.then_inc(Y_made, 1)
                if c < CH - 1:
                    pe.wait_ge(wdtx_made, i * 3 + c + 1)
                    pe.wait_ge(btok_made, i * 3 + c + 1)
                    if not (first and c < 3):
                        pe.wait_ge(resA_made, t - 2)
                    pe.matmul(bank(7)[:, 0:INNER], Btok[:], wdtx[:], start=True, stop=True).then_inc(S_made, 1)
                if c == CH - 1 and not last:
                    pairsA(i + 1, 1 - par)
                    chunk_in(i + 1, 0, 1 - par)
                if not last:
                    for k in ((0,), (1,), (2, 3, 4), (5,))[c]:
                        projA(i + 1, k)
                if not (first and c < 2):
                    if c < CH - 1:
                        pe.wait_ge(st_made, i * 3 + c + 1)
                    else:
                        pe.wait_ge(resA_made, t - 2)
                    outA(t - 2, (c + 2) % CH)
                if not (first and c == 0):
                    yT_A(t - 1, (c + 3) % CH)
                if c == CH - 1 and last:
                    zT(1, 0, M_made, NT)

            def stageA(i, par, first=False, last=False):
                for c in range(CH):
                    stepA(i, c, par, first, last)

            pe.wait_ge(folded, SEQS)
            pe.wait_ge(zT_stashed[0], 32)
            projA(0, 0)
            projA(0, 1)
            bias_products()
            pe.wait_ge(step_v, 17)
            pe.matmul(bank(3)[:, 0:NC], cumneg[:], sm[:, 7], start=True, stop=True).then_inc(cum_in_psum, 1)
            pe.matmul(bank(4)[:, 0:NC], allneg[:], sm[:, 7], start=True, stop=True).then_inc(cum_in_psum, 1)
            pe.wait_ge(parts_made, 5)
            pe.wait_ge(lo_made, SEQS)
            for q in range(3):
                ins = pe.transpose(bank(5).bitcast(BF16)[:, q * P:(q + 1) * P], cparts[:, q], identb[:])
            ins.then_inc(partsT_in_psum, 1)
            for k in range(2, 6):
                projA(0, k)
            for k in range(2):
                pe.wait_ge(zT_stashed[k], 16 * SEQS)
            pe.wait_ge(parts_made, 6)
            pairsA(0, 0)
            pe.wait_ge(rows_moved, 16)
            pe.wait_ge(fillers, 1)
            pe.wait_ge(step_a, 5)
            chunk_in(0, 0, 0)
            pe.wait_ge(set_v, 10)
            stageA(0, 0, first=True)
            with pe.Fori(1, SEQS - 2, 2) as i:
                stageA(i, 1)
                stageA(i + 1, 0)
            stageA(SEQS - 1, 1, last=True)
            pe.wait_ge(resA_made, NT - 2)
            outA(NT - 2, CH - 2)
            yT_A(NT - 1, CH - 1)
            def logitsB(i, par):
                pe.wait_ge(lo_made, SEQS + i + 1)
                pe.wait_ge(gate_v, i * GATE_STEPS)
                for c in range(CH):
                    dst = bank(4)[:, 2 * EXPERTS * c:2 * EXPERTS * (c + 1)]
                    zh, zl = zt(par, c)
                    pe.matmul(dst, zh, wg_parts[:].rearrange("p k e -> p (k e)"), start=True, stop=False,
                              skip_group_check=True)
                    ins = pe.matmul(dst[:, 0:EXPERTS], zl, wg_hi, start=False, stop=True, skip_group_check=True)
                ins.then_inc(logits_made, 1)

            def accT_B(t, k):
                pe.wait_ge(acc_made, t + 1)
                pe.wait_ge(accT_made, t)
                for h in range(2):
                    ins = pe.transpose(bank(6)[:, cols(h)], acc[k][:, cols(h)], ident[:])
                ins.then_inc(accT_in_psum, 1)

            def moe_out(t, i, c):
                pe.wait_ge(accT_made, t + 1)
                if c == 0:
                    pe.wait_ge(res_made, i)
                for h in range(2):
                    ins = pe.matmul(bank(7)[:, cols(c)], accT[:, h], w_o[:, h], start=h == 0, stop=h == 1)
                ins.then_inc(moe_made, 1)

            def stageB(i, par, first=False, last=False):
                for c in range(CH):
                    t = i * CH + c
                    for e in range(EXPERTS):
                        pe.wait_ge(g_made, t * EXPERTS + e + 1)
                        split3(bank(e % 4), zt(par, c), (w1_hi[:, e], w1_lo[:, e])).then_inc(h_made, 1)
                        if not (first and c < 2):
                            if e == 1:
                                accT_B(t - 2, c % 2)
                            if e == 6:
                                moe_out(t - 2, i if c >= 2 else i - 1, (c + 2) % 4)
                        if e == 5 and c == 1:
                            zT(*((2, 0) if last else (1, i + 1)), None, None)
                        if e == 2 and c == 2 and not last:
                            logitsB(i + 1, 1 - par)

            pe.wait_ge(w1lo_made, SEQS)
            pe.wait_ge(wlo_made, 5)
            logitsB(0, 0)
            pe.wait_ge(resA_made, NT - 1)
            outA(NT - 1, CH - 1)
            stageB(0, 0, first=True)
            with pe.Fori(1, SEQS - 2, 2) as i:
                stageB(i, 1)
                stageB(i + 1, 0)
            stageB(SEQS - 1, 1, last=True)
            accT_B(NT - 2, 0)
            moe_out(NT - 2, SEQS - 1, CH - 2)

            def w4p(a, b):
                return w4_hi[:, a:b], w4_lo[:, a:b]

            def projC(i, par, n):
                pe.wait_ge(lo_made, 2 * SEQS + i + 1)
                if n == 0:
                    pe.wait_ge(lkt_made, i)
                    ins = split3(bank(2), w4p(512, 640), zt(par))
                elif n in (1, 4):
                    pe.wait_ge(cact_made, i * 5)
                    if n == 4:
                        pe.wait_ge(kvs_made, i * 3)
                    k = 1 if n == 1 else 0
                    for c in range(2):
                        ins = split3(bank(3 + k)[:, c * HID:(c + 1) * HID], zt(par, 2 * k + c), w4p(0, HID))
                else:
                    pe.wait_ge(cact_made, i * 5)
                    ins = split3(bank(n - 2), w4p(HID + P * (n - 2), HID + P * (n - 1)), zt(par))
                ins.then_inc(cproj_made, 1)

            def kvC(i, par, c):
                if c > 0:
                    pe.wait_ge(kvs_made, i * 3 + c)
                pe.matmul(bank(3)[:, 0:HID], lkt[:, c], vt[par][:, c], start=c == 0, stop=True, skip_group_check=True)\
                  .then_inc(kv_made, 1)

            def outC(i, left):
                pe.wait_ge(og_made, i * 2 + 2)
                pe.wait_ge(lo_made, left)
                for c in range(CH):
                    for half in range(2):
                        ins = pe.matmul(bank(5)[:, cols(c)], og[:, half, cols(c)], w_att[:, half],
                                        start=half == 0, stop=half == 1)
                ins.then_inc(cout_made, 1)

            def gate_up(i, m, par):
                pe.wait_ge(hf_made, i * 3 + m + 1)
                for b, col in ((GATE_BANKS[m], m * P), (UP_BANKS[m], FFN + m * P)):
                    ins = split3(bank(b), (wff_hi[:, col:col + P], wff_lo[:, col:col + P]), zt(par))
                ins.then_inc(gu_made, 1)

            def stageC(i, par, nxt, first=False, last=False):
                q = qv[par]
                pe.wait_ge(var_made, i * 4 + 4)
                pe.wait_ge(og_made, i * 2)
                for c in range(CH):
                    ins = pe.matmul(bank(6)[:, cols(c)], q[:, 2, cols(c)], q[:, 0, cols(c)], start=True, stop=True)
                ins.then_inc(s1_made, 1)
                if first:
                    pe.wait_ge(res_made, SEQS)
                for c in range(CH):
                    ins = pe.matmul(bank(7)[:, cols(c)], q[:, 3, cols(c)], q[:, 1, cols(c)], start=True, stop=True)
                ins.then_inc(s2_made, 1)
                for c in range(CH):
                    ins = pe.transpose(bank(2)[:, cols(c)], q[:, 3, cols(c)], ident[:])
                ins.then_inc(lkT_made, 1)
                if not first:
                    outC(i - 1, 2 * SEQS + i + 2)
                pe.wait_ge(lkt_made, i + 1)
                pe.wait_ge(cact_made, i * 5 + 5)
                for c in range(3):
                    kvC(i, par, c)
                    if c < 2 and not last:
                        projC(i + 1, 1 - par, c)
                    if c < EARLY_D and last:
                        if c == 0:
                            pe.wait_ge(lo_made, 3 * SEQS + 1)
                        gate_up(0, c, 1 - par)
                if not last:
                    projC(i + 1, 1 - par, 2)
                    projC(i + 1, 1 - par, 3)
                pe.wait_ge(att_made, i * 4 + 4)
                pe.wait_ge(kvs_made, i * 3 + 3)
                for half in range(2):
                    for c in range(CH):
                        dst = bank(6 + half)[:, cols(c)]
                        ins = pe.matmul(dst, vt[par][:, c, cols(half)], at[:, 0, cols(c)], start=True, stop=c == 0)
                        if c > 0:
                            ins = pe.matmul(dst, kvs[:, c - 1, cols(half)], q[:, 1, cols(c)], start=False, stop=True)
                    ins.then_inc(o_made, 1)
                if not last:
                    projC(i + 1, 1 - par, 4)
                zT(*nxt, res_made, SEQS + i)

            pe.wait_ge(g_made, NT * EXPERTS + BCREDIT)
            for n in range(5):
                projC(0, 0, n)
            zT(2, 1, None, None)
            accT_B(NT - 1, 1)
            moe_out(NT - 1, SEQS - 1, CH - 1)
            stageC(0, 0, (2, 2), first=True)
            with pe.Fori(1, SEQS - 4, 2) as i:
                stageC(i, 1, (2, i + 2))
                stageC(i + 1, 0, (2, i + 3))
            stageC(SEQS - 3, 1, (2, SEQS - 1))
            stageC(SEQS - 2, 0, (3, 0))
            stageC(SEQS - 1, 1, (3, 1), last=True)
            pe.wait_ge(og_made, SEQS * 2 - 1)
            gate_up(0, EARLY_D, 0)
            outC(SEQS - 1, 3 * SEQS + 2)

            def down(i, par, tiles):
                if tiles[0] == 0:
                    pe.wait_ge(hf_made, (i + 1) * 3 + DCREDIT)
                    pe.wait_ge(resD_made, i)
                for c in tiles:
                    for m in range(3):
                        ins = pe.matmul(bank(7)[:, cols(c)], hf[par][:, m, cols(c)], wdn[:, m], start=m == 0, stop=m == 2)
                if tiles[-1] == CH - 1:
                    ins.then_inc(dn_made, 1)

            def stageD(i, par, first=0, last=0):
                pe.wait_ge(lo_made, 3 * SEQS + i + 1)
                if first < 2:
                    for m in range(3):
                        gate_up(i, m, par)
                if first < 2:
                    down(i - 1, 1 - par, (0, 1))
                if first < 2 and last < 2:
                    zT(3, i + 1, res_made, 2 * SEQS)
                if first < 2:
                    down(i - 1, 1 - par, (2, 3))

            stageD(0, 0, first=2)
            stageD(1, 1, first=1)
            with pe.Fori(2, SEQS - 3, 2) as i:
                stageD(i, 0)
                stageD(i + 1, 1)
            stageD(SEQS - 2, 0, last=1)
            stageD(SEQS - 1, 1, last=2)
            down(SEQS - 1, 1, range(CH))


_INS = ["x", "vectors", "rows", "in_wT", "W1T", "b1", "squares", "W4", "b4", "Wff"]


def kernel(L0_attn_x, L0_attn_norm_w, L0_attn_in_proj_w, L0_attn_conv_w, L0_attn_conv_b, L0_attn_A_log, L0_attn_D,
           L0_attn_dt_bias, L0_attn_out_proj_w, L0_ffn_Wg, L0_ffn_W1, L0_ffn_b1, L0_ffn_Wo, L0_ffn_bo, L1_attn_ln_w,
           L1_attn_ln_b, L1_attn_Wh, L1_attn_bh, L1_attn_Wqk, L1_attn_bqk, L1_attn_qk_w, L1_attn_qk_b,
           L1_attn_rel_table, L1_attn_Wout, L1_attn_bout, L1_ffn_w_gate, L1_ffn_w_up, L1_ffn_w_down):
    import numpy as np
    import concourse.bacc as bacc
    from concourse.bass_utils import run_bass_kernel_spmd

    def row(*arrays):
        return np.concatenate([np.asarray(a).reshape(1, -1) for a in arrays], 1)

    def T(a):
        return np.asarray(a).T

    def halves(a):
        a = np.asarray(a)
        return a.reshape((2, P) + a.shape[1:]).swapaxes(0, 1).reshape(P, -1)

    def columns(a):
        return np.asarray(a).reshape(P, -1)

    arrays = dict(
        x=L0_attn_x,
        vectors=np.concatenate([
            columns(L0_attn_norm_w), halves(np.asarray(L0_attn_conv_w).reshape(INNER, 4)), halves(L0_attn_conv_b),
            halves(np.repeat(np.asarray(L0_attn_D), HD)), columns(L1_attn_ln_w), columns(L1_attn_ln_b),
            T(L1_attn_qk_w), T(L1_attn_qk_b)], 1),
        rows=row(L0_attn_A_log, L0_attn_dt_bias, L1_attn_rel_table, L0_ffn_bo, L1_attn_bout),
        in_wT=T(L0_attn_in_proj_w), W1T=np.asarray(L0_ffn_W1).transpose(0, 2, 1), b1=row(L0_ffn_b1),
        squares=np.concatenate([T(L0_attn_out_proj_w), T(L0_ffn_Wo), np.asarray(L1_attn_Wout)]).reshape(6, P, P),
        W4=np.concatenate([np.asarray(L1_attn_Wh), np.asarray(L1_attn_Wqk), T(L0_ffn_Wg)], 1),
        b4=row(L1_attn_bh, L1_attn_bqk),
        Wff=np.concatenate([T(L1_ffn_w_gate), T(L1_ffn_w_up),
                            T(L1_ffn_w_down).reshape(3, P, P).transpose(1, 0, 2).reshape(P, FFN)], 1))
    nc = bacc.Bacc("TRN2", target_bir_lowering=False, num_devices=1)
    in_map, args = {}, []
    for name in _INS:
        a = np.ascontiguousarray(arrays[name])
        in_map[f"in_{name}"] = a
        args.append(nc.dram_tensor(f"in_{name}", a.shape, mybir.dt.from_np(a.dtype), kind="ExternalInput").ap())
    out = nc.dram_tensor("out", (SEQS, TOK, P), F32, kind="ExternalOutput").ap()
    build(nc, *args, out)
    return run_bass_kernel_spmd(nc, [in_map], core_ids=[0]).results[0]["out"]
```
